# Optimizing a Trainium2 kernel written in Bass

```python
import numpy as np
import jax
import jax.numpy as jnp

def _softmax(x, axis=-1):
    return jax.nn.softmax(x, axis=axis)

def _gelu(x):
    return jax.nn.gelu(x, approximate=True)

def _silu(x):
    return jax.nn.silu(x)

def _sigmoid(x):
    return jax.nn.sigmoid(x)

def _layernorm(x, axis=-1, eps=1e-05):
    m = jnp.mean(x, axis=axis, keepdims=True)
    v = jnp.var(x, axis=axis, keepdims=True)
    return (x - m) / jnp.sqrt(v + eps)

def _scatter_add(tgt, idx, src, axis=0):
    return tgt.at[idx].add(src)

def _segment_sum(src, seg, n):
    return jax.ops.segment_sum(src, seg, n)
kernel_name = 'mk_seq_postln_d1_jaxref_r4_1dbf8a'

def setup_inputs(seed: int=0):
    np.random.seed(seed)
    _w = jnp.asarray

    def _L0_attn_setup():
        import jax, jax.numpy as jnp
        import numpy as np
        B, T, D, H = (8, 1024, 256, 16)
        DK = D // H
        CHUNK = 64
        E, TOPK, MULT, CAPF = (8, 2, 4, 1.25)
        HID = D * MULT
        N = B * T
        CAPACITY = int(CAPF * (N / E))

        def rmsnorm(x, scale):
            return x / jnp.sqrt(jnp.mean(x * x, axis=-1, keepdims=True)) * scale

        def apply_rope(x):
            half = x.shape[-1] // 2
            t = x.shape[2]
            inv = 1.0 / 10000.0 ** (jnp.arange(half, dtype=jnp.float32) / half)
            ang = jnp.arange(t, dtype=jnp.float32)[:, None] * inv[None, :]
            sin, cos = (jnp.sin(ang)[None, None], jnp.cos(ang)[None, None])
            x1, x2 = (x[..., :half], x[..., half:])
            return jnp.concatenate([x1 * cos - x2 * sin, x1 * sin + x2 * cos], axis=-1)

        def phi(x):
            return jax.nn.elu(x) + 1.0

        def attention(x, Wq, bq, Wk, bk, Wv, bv, Wg, bg, Wo, bo):
            b, t, c = x.shape
            heads = lambda y: y.reshape(b, t, H, DK).transpose(0, 2, 1, 3)
            q = phi(apply_rope(heads(x @ Wq + bq)))
            k = phi(apply_rope(heads(x @ Wk + bk)))
            v = heads(x @ Wv + bv)
            g = heads(jax.nn.sigmoid(x @ Wg + bg))
            nc = t // CHUNK
            to_chunks = lambda y: y.reshape(b, H, nc, CHUNK, DK).transpose(2, 0, 1, 3, 4)
            qs, ks_, vs, gs = map(to_chunks, (q, k, v, g))
            S0 = jnp.zeros((b, H, DK, DK), x.dtype)
            Z0 = jnp.zeros((b, H, DK), x.dtype)

            def step(carry, inp):
                S, Z = carry
                qc, kc, vc, gc = inp
                S = S + jnp.einsum('bhtd,bhte->bhde', kc, vc)
                Z = Z + kc.sum(axis=2)
                num = jnp.einsum('bhtd,bhde->bhte', qc, S)
                den = jnp.einsum('bhtd,bhd->bht', qc, Z)[..., None] + 1e-06
                return ((S, Z), gc * (num / den))
            _, outs = jax.lax.scan(step, (S0, Z0), (qs, ks_, vs, gs))
            out = outs.transpose(1, 2, 0, 3, 4).reshape(b, H, t, DK)
            out = out.transpose(0, 2, 1, 3).reshape(b, t, c)
            return out @ Wo + bo

        def moe(x, router_W, router_b, W1, b1, W2, b2):
            b, t, c = x.shape
            n = b * t
            xf = x.reshape(n, c)
            probs = jax.nn.softmax(xf @ router_W + router_b, axis=-1)
            topk_probs, topk_idx = jax.lax.top_k(probs, TOPK)
            topk_probs = topk_probs / topk_probs.sum(axis=-1, keepdims=True)
            out = jnp.zeros_like(xf)
            load = []
            for eid in range(E):
                mask = (topk_idx == eid).reshape(-1)
                idx = jnp.nonzero(mask, size=CAPACITY, fill_value=n * TOPK)[0]
                valid = idx < n * TOPK
                idxc = jnp.minimum(idx, n * TOPK - 1)
                tok, choice = (idxc // TOPK, idxc % TOPK)
                h = jax.nn.gelu(xf[tok] @ W1[eid] + b1[eid], approximate=False) @ W2[eid] + b2[eid]
                gate = jnp.where(valid, topk_probs[tok, choice], 0.0)
                out = out.at[tok].add(gate[:, None] * h)
                load.append(jnp.minimum(mask.sum(), CAPACITY).astype(xf.dtype))
            load = jnp.stack(load)
            importance = probs.sum(axis=0)
            importance = importance / importance.sum()
            load = load / load.sum()
            aux = (importance * load).sum() * E ** 2
            return (out.reshape(b, t, c), aux)

        def _reference_tuple_inner(x, norm1_scale, norm2_scale, Wq, bq, Wk, bk, Wv, bv, Wg, bg, Wo, bo, router_W, router_b, W1, b1, W2, b2):
            x = x + attention(rmsnorm(x, norm1_scale), Wq, bq, Wk, bk, Wv, bv, Wg, bg, Wo, bo)
            moe_out, aux = moe(rmsnorm(x, norm2_scale), router_W, router_b, W1, b1, W2, b2)
            return (x + moe_out, aux)
        key = jax.random.key(seed)
        ks = jax.random.split(key, 16)
        s = 0.02
        r = lambda k, shape: jax.random.normal(k, shape, jnp.float32) * s
        return {'x': jax.random.normal(ks[0], (B, T, D), jnp.float32), 'norm1_scale': jnp.ones((D,), jnp.float32), 'norm2_scale': jnp.ones((D,), jnp.float32), 'Wq': r(ks[1], (D, D)), 'bq': jnp.zeros((D,), jnp.float32), 'Wk': r(ks[2], (D, D)), 'bk': jnp.zeros((D,), jnp.float32), 'Wv': r(ks[3], (D, D)), 'bv': jnp.zeros((D,), jnp.float32), 'Wg': r(ks[4], (D, D)), 'bg': jnp.zeros((D,), jnp.float32), 'Wo': r(ks[5], (D, D)), 'bo': jnp.zeros((D,), jnp.float32), 'router_W': r(ks[6], (D, E)), 'router_b': jnp.zeros((E,), jnp.float32), 'W1': r(ks[7], (E, D, HID)), 'b1': jnp.zeros((E, HID), jnp.float32), 'W2': r(ks[8], (E, HID, D)), 'b2': jnp.zeros((E, D), jnp.float32)}
    _L0_attn_in = _L0_attn_setup()

    def _L0_ffn_setup():
        import math
        import jax, jax.numpy as jnp
        import numpy as np
        D_MODEL = 256
        D_FF = 1024
        E = 8
        K = 2
        CAP_FACTOR = 1.25
        CLAMP = 10000.0
        LN_EPS = 1e-05
        B, S = (2, 512)
        key = jax.random.key(seed)
        ks = jax.random.split(key, 6)
        b12 = math.sqrt(6.0 / (D_MODEL + 2 * D_FF))
        b3 = math.sqrt(6.0 / (D_FF + D_MODEL))
        br = 0.02 * math.sqrt(3.0)
        return {'x': jax.random.normal(ks[0], (B, S, D_MODEL), dtype=jnp.float32), 'ln_gamma': jnp.ones((D_MODEL,), jnp.float32), 'ln_beta': jnp.zeros((D_MODEL,), jnp.float32), 'router_w': jax.random.uniform(ks[1], (E, D_MODEL), jnp.float32, -br, br), 'w12': jax.random.uniform(ks[2], (E, 2 * D_FF, D_MODEL), jnp.float32, -b12, b12), 'w3': jax.random.uniform(ks[3], (E, D_MODEL, D_FF), jnp.float32, -b3, b3)}
    _L0_ffn_in = _L0_ffn_setup()
    _d = {'L0_attn_x': _L0_attn_in['x'], 'L0_attn_norm1_scale': _L0_attn_in['norm1_scale'], 'L0_attn_norm2_scale': _L0_attn_in['norm2_scale'], 'L0_attn_Wq': _L0_attn_in['Wq'], 'L0_attn_bq': _L0_attn_in['bq'], 'L0_attn_Wk': _L0_attn_in['Wk'], 'L0_attn_bk': _L0_attn_in['bk'], 'L0_attn_Wv': _L0_attn_in['Wv'], 'L0_attn_bv': _L0_attn_in['bv'], 'L0_attn_Wg': _L0_attn_in['Wg'], 'L0_attn_bg': _L0_attn_in['bg'], 'L0_attn_Wo': _L0_attn_in['Wo'], 'L0_attn_bo': _L0_attn_in['bo'], 'L0_attn_router_W': _L0_attn_in['router_W'], 'L0_attn_router_b': _L0_attn_in['router_b'], 'L0_attn_W1': _L0_attn_in['W1'], 'L0_attn_b1': _L0_attn_in['b1'], 'L0_attn_W2': _L0_attn_in['W2'], 'L0_attn_b2': _L0_attn_in['b2'], 'L0_ffn_ln_gamma': _L0_ffn_in['ln_gamma'], 'L0_ffn_ln_beta': _L0_ffn_in['ln_beta'], 'L0_ffn_router_w': _L0_ffn_in['router_w'], 'L0_ffn_w12': _L0_ffn_in['w12'], 'L0_ffn_w3': _L0_ffn_in['w3']}
    _x0 = _d['L0_attn_x']
    _d['L0_attn_x'] = jax.random.normal(jax.random.fold_in(jax.random.key(seed), 1), (2, 2048, 256), dtype=_x0.dtype)
    del _x0
    return _d

def reference(L0_attn_x, L0_attn_norm1_scale, L0_attn_norm2_scale, L0_attn_Wq, L0_attn_bq, L0_attn_Wk, L0_attn_bk, L0_attn_Wv, L0_attn_bv, L0_attn_Wg, L0_attn_bg, L0_attn_Wo, L0_attn_bo, L0_attn_router_W, L0_attn_router_b, L0_attn_W1, L0_attn_b1, L0_attn_W2, L0_attn_b2, L0_ffn_ln_gamma, L0_ffn_ln_beta, L0_ffn_router_w, L0_ffn_w12, L0_ffn_w3):

    def _L0_attn_ref(x, norm1_scale, norm2_scale, Wq, bq, Wk, bk, Wv, bv, Wg, bg, Wo, bo, router_W, router_b, W1, b1, W2, b2):
        import jax, jax.numpy as jnp
        import numpy as np
        B, T, D, H = (8, 1024, 256, 16)
        DK = D // H
        CHUNK = 64
        E, TOPK, MULT, CAPF = (8, 2, 4, 1.25)
        HID = D * MULT
        N = B * T
        CAPACITY = int(CAPF * (N / E))

        def rmsnorm(x, scale):
            return x / jnp.sqrt(jnp.mean(x * x, axis=-1, keepdims=True)) * scale

        def apply_rope(x):
            half = x.shape[-1] // 2
            t = x.shape[2]
            inv = 1.0 / 10000.0 ** (jnp.arange(half, dtype=jnp.float32) / half)
            ang = jnp.arange(t, dtype=jnp.float32)[:, None] * inv[None, :]
            sin, cos = (jnp.sin(ang)[None, None], jnp.cos(ang)[None, None])
            x1, x2 = (x[..., :half], x[..., half:])
            return jnp.concatenate([x1 * cos - x2 * sin, x1 * sin + x2 * cos], axis=-1)

        def phi(x):
            return jax.nn.elu(x) + 1.0

        def attention(x, Wq, bq, Wk, bk, Wv, bv, Wg, bg, Wo, bo):
            b, t, c = x.shape
            heads = lambda y: y.reshape(b, t, H, DK).transpose(0, 2, 1, 3)
            q = phi(apply_rope(heads(x @ Wq + bq)))
            k = phi(apply_rope(heads(x @ Wk + bk)))
            v = heads(x @ Wv + bv)
            g = heads(jax.nn.sigmoid(x @ Wg + bg))
            nc = t // CHUNK
            to_chunks = lambda y: y.reshape(b, H, nc, CHUNK, DK).transpose(2, 0, 1, 3, 4)
            qs, ks_, vs, gs = map(to_chunks, (q, k, v, g))
            S0 = jnp.zeros((b, H, DK, DK), x.dtype)
            Z0 = jnp.zeros((b, H, DK), x.dtype)

            def step(carry, inp):
                S, Z = carry
                qc, kc, vc, gc = inp
                S = S + jnp.einsum('bhtd,bhte->bhde', kc, vc)
                Z = Z + kc.sum(axis=2)
                num = jnp.einsum('bhtd,bhde->bhte', qc, S)
                den = jnp.einsum('bhtd,bhd->bht', qc, Z)[..., None] + 1e-06
                return ((S, Z), gc * (num / den))
            _, outs = jax.lax.scan(step, (S0, Z0), (qs, ks_, vs, gs))
            out = outs.transpose(1, 2, 0, 3, 4).reshape(b, H, t, DK)
            out = out.transpose(0, 2, 1, 3).reshape(b, t, c)
            return out @ Wo + bo

        def moe(x, router_W, router_b, W1, b1, W2, b2):
            b, t, c = x.shape
            n = b * t
            xf = x.reshape(n, c)
            probs = jax.nn.softmax(xf @ router_W + router_b, axis=-1)
            topk_probs, topk_idx = jax.lax.top_k(probs, TOPK)
            topk_probs = topk_probs / topk_probs.sum(axis=-1, keepdims=True)
            out = jnp.zeros_like(xf)
            load = []
            for eid in range(E):
                mask = (topk_idx == eid).reshape(-1)
                idx = jnp.nonzero(mask, size=CAPACITY, fill_value=n * TOPK)[0]
                valid = idx < n * TOPK
                idxc = jnp.minimum(idx, n * TOPK - 1)
                tok, choice = (idxc // TOPK, idxc % TOPK)
                h = jax.nn.gelu(xf[tok] @ W1[eid] + b1[eid], approximate=False) @ W2[eid] + b2[eid]
                gate = jnp.where(valid, topk_probs[tok, choice], 0.0)
                out = out.at[tok].add(gate[:, None] * h)
                load.append(jnp.minimum(mask.sum(), CAPACITY).astype(xf.dtype))
            load = jnp.stack(load)
            importance = probs.sum(axis=0)
            importance = importance / importance.sum()
            load = load / load.sum()
            aux = (importance * load).sum() * E ** 2
            return (out.reshape(b, t, c), aux)

        def _reference_tuple_inner(x, norm1_scale, norm2_scale, Wq, bq, Wk, bk, Wv, bv, Wg, bg, Wo, bo, router_W, router_b, W1, b1, W2, b2):
            x = x + attention(rmsnorm(x, norm1_scale), Wq, bq, Wk, bk, Wv, bv, Wg, bg, Wo, bo)
            moe_out, aux = moe(rmsnorm(x, norm2_scale), router_W, router_b, W1, b1, W2, b2)
            return (x + moe_out, aux)
        return _reference_tuple_inner(x, norm1_scale, norm2_scale, Wq, bq, Wk, bk, Wv, bv, Wg, bg, Wo, bo, router_W, router_b, W1, b1, W2, b2)[0]

    def _L0_ffn_ref(x, ln_gamma, ln_beta, router_w, w12, w3):
        import math
        import jax, jax.numpy as jnp
        import numpy as np
        D_MODEL = 256
        D_FF = 1024
        E = 8
        K = 2
        CAP_FACTOR = 1.25
        CLAMP = 10000.0
        LN_EPS = 1e-05
        B, S = (2, 512)
        Bq, Sq, D = x.shape
        T = Bq * Sq
        mu = jnp.mean(x, axis=-1, keepdims=True)
        var = jnp.mean(jnp.square(x - mu), axis=-1, keepdims=True)
        xn = (x - mu) * jax.lax.rsqrt(var + LN_EPS) * ln_gamma + ln_beta
        xf = xn.reshape(T, D)
        logits = jnp.clip(xf @ router_w.T, -CLAMP, CLAMP)
        top_v, top_i = jax.lax.top_k(logits, K)
        m = jnp.max(top_v, axis=-1, keepdims=True)
        ev = jnp.exp(top_v - m)
        top_p = ev / (jnp.sum(ev, axis=-1, keepdims=True) + 1e-12)
        Stot = T * K
        experts = top_i.reshape(-1)
        weights = top_p.reshape(-1)
        tokens = jnp.repeat(jnp.arange(T), K)
        oh = (experts[:, None] == jnp.arange(E)[None, :]).astype(jnp.int32)
        pos = jnp.take_along_axis(jnp.cumsum(oh, axis=0) - 1, experts[:, None], axis=1)[:, 0]
        C = max(1, math.ceil(T * K * CAP_FACTOR / E))
        kept = pos < C
        slot = jnp.where(kept, experts * C + pos, E * C)
        buf = jnp.zeros((E * C + 1, D), x.dtype).at[slot].set(xf[tokens])
        xb = buf[:E * C].reshape(E, C, D)
        gu = jnp.einsum('ecd,efd->ecf', xb, w12)
        g, u = jnp.split(gu, 2, axis=-1)
        h = jax.nn.silu(g) * u
        yb = jnp.einsum('ecf,edf->ecd', h, w3).reshape(E * C, D)
        ys = yb[jnp.minimum(slot, E * C - 1)] * (weights * kept.astype(weights.dtype))[:, None]
        out = jnp.zeros((T, D), x.dtype).at[tokens].add(ys)
        return out.reshape(Bq, Sq, D)
    x = L0_attn_x
    x = _layernorm(x + _L0_attn_ref(x, L0_attn_norm1_scale, L0_attn_norm2_scale, L0_attn_Wq, L0_attn_bq, L0_attn_Wk, L0_attn_bk, L0_attn_Wv, L0_attn_bv, L0_attn_Wg, L0_attn_bg, L0_attn_Wo, L0_attn_bo, L0_attn_router_W, L0_attn_router_b, L0_attn_W1, L0_attn_b1, L0_attn_W2, L0_attn_b2), axis=-1)
    x = _layernorm(x + _L0_ffn_ref(x, L0_ffn_ln_gamma, L0_ffn_ln_beta, L0_ffn_router_w, L0_ffn_w12, L0_ffn_w3), axis=-1)
    return x

_drawn_inputs = setup_inputs


def setup_inputs(seed=0):
    import zlib

    import numpy as np

    out = dict(_drawn_inputs(seed))
    spreads = {'L0_attn_norm1_scale': (1.0, 0.6),
     'L0_attn_norm2_scale': (1.0, 0.535),
     'L0_attn_bq': (0.0, 2.0),
     'L0_attn_bk': (0.0, 2.0),
     'L0_attn_bv': (0.0, 0.489),
     'L0_attn_bg': (0.0, 0.8),
     'L0_attn_bo': (0.0, 0.1),
     'L0_attn_router_b': (0.0, 0.1),
     'L0_attn_b1': (0.0, 0.445),
     'L0_attn_b2': (0.0, 0.1),
     'L0_ffn_ln_gamma': (1.0, 0.2),
     'L0_ffn_ln_beta': (0.0, 0.1)}
    factors = {'L0_attn_Wq': 8.0,
     'L0_attn_Wk': 8.0,
     'L0_attn_Wv': 8.0,
     'L0_attn_Wg': 8.0,
     'L0_attn_Wo': 3.977}
    for name, (base, spread) in spreads.items():
        noise = np.random.default_rng([zlib.crc32(name.encode()), seed]).standard_normal(out[name].shape)
        drawn = base * np.exp(spread * noise) if base else spread * noise
        out[name] = jnp.asarray(drawn.astype(out[name].dtype))
    for name, factor in factors.items():
        out[name] = (out[name] * factor).astype(out[name].dtype)
    return out
```

```python
from contextlib import ExitStack

import numpy as np

import concourse.bass as bass
from concourse import mybir

F32 = mybir.dt.float32
F32R = mybir.dt.float32r
BF16 = mybir.dt.bfloat16
I32 = mybir.dt.int32
ALU = mybir.AluOpType
ACT = mybir.ActivationFunctionType
AX_X = mybir.AxisListType.X

P = 128
BATCH, SEQ, D = 2, 2048, 256
N = BATCH * SEQ
NT = N // P
TPB = NT // BATCH
KD = D // P
H, DK = 16, 16
HALF = DK // 2
CHUNK = 64
E = 8
HPH = P // DK
SW = P + HPH
HID = 1024
NF = HID // P
CAP = 1280
SLOTS = E * CAP
TILES_E = CAP // P
UW = 256
UPE = CAP // UW
UNITS = E * UPE
UT = UW // P
SC = E * TILES_E
EPS = 1e-5
CLAMP = 10000.0

C_ID, C_TRI, C_MASK = 0, P, 2 * P
C_IOTA = C_MASK + SW
C_REV = C_IOTA + P
C_ROW = C_REV + E
C_N = C_ROW + 1


def shape_constants():
    c = np.zeros((P, C_N), np.float32)
    r = np.arange(P)
    c[:, C_ID:C_ID + P] = np.eye(P)
    c[:, C_TRI:C_TRI + P] = r[:, None] < r[None, :]
    c[:, C_MASK:C_MASK + P] = r[:, None] // DK == r[None, :] // DK
    c[:, C_MASK + P:C_MASK + SW] = r[:, None] // DK == np.arange(HPH)[None, :]
    c[:, C_IOTA:C_IOTA + P] = r[None, :]
    c[:, C_REV:C_REV + E] = E - np.arange(E)[None, :]
    c[:, C_ROW] = r
    half = np.arange(HALF, dtype=np.float32) / np.float32(HALF)
    inv = (np.float32(1.0) / np.power(np.float32(10000.0), half)).astype(np.float32)
    ang = (np.arange(SEQ, dtype=np.float32)[:, None] * inv[None, :]).astype(np.float32)
    cos, sin = np.cos(ang).astype(np.float32), np.sin(ang).astype(np.float32)
    rope = np.concatenate([cos, -sin, sin], axis=1).reshape(TPB, P, 3 * HALF).transpose(1, 0, 2)
    return c, np.ascontiguousarray(rope)


def after(eng, sem, count, passed=None):
    if isinstance(count, int) and count <= 0:
        return
    eng.wait_ge(sem, count)
    if passed is not None:
        eng.sem_inc(passed, 1)


LEAD = 2
LOOP_FROM = 4
LOOP_STEPS = (NT - LOOP_FROM - LEAD) // 2


class Tile:

    def __init__(self, n, b, i):
        self.n, self.b, self.i = n, b, i
        self.T = i + b * TPB


def fixed_tile(n):
    return Tile(n, n % 2, n // 2) if 0 <= n < NT else None


def run_tiles(eng, step, before_loop):
    for t in range(-LEAD, LOOP_FROM):
        step(lambda d: fixed_tile(t + d))
    before_loop()
    with eng.Fori(0, LOOP_STEPS) as j:
        for r in range(2):
            step(lambda d: Tile(j * 2 + (LOOP_FROM + r + d), (r + d) % 2, j + (LOOP_FROM + r + d) // 2))
    for t in range(LOOP_FROM + 2 * LOOP_STEPS, NT + LEAD):
        step(lambda d: fixed_tile(t + d))


def attention_phase(nc, bank, io, X, LG, cst, wraw):
    with ExitStack() as ctx:
        def sb(name, shape, dt=F32):
            return ctx.enter_context(nc.sbuf_tensor("A_" + name, shape, dt))

        def sem(name):
            return ctx.enter_context(nc.semaphore("A_" + name))

        wqkvg = sb("wqkvg", [P, KD, 4 * D])
        wo = sb("wo", [P, KD, D])
        wr = sb("wr", [P, KD, E])
        sc1 = sb("sc1", [P, KD])
        sc2 = sb("sc2", [P, KD])
        bqkvg = sb("bqkvg", [P, 4 * D])
        bo = sb("bo", [P, D])
        rope = sb("rope", [P, TPB, 3 * HALF])
        zeros = sb("zeros", [P, KD * SW])
        mhalf = sb("mhalf", [P, 1])
        junk = sb("junk", [P, 2, 2, D])
        ssq1, r1 = sb("ssq1", [P, 2]), sb("r1", [P, 2])
        ssq2, r2 = sb("ssq2", [P, 2]), sb("r2", [P, 2])
        xs = sb("xs", [P, 2, D])
        xT = sb("xT", [P, 2, KD, P])
        qk = sb("qk", [P, 2 * D])
        ra = sb("ra", [P, 2 * D])
        rb = sb("rb", [P, 2 * D])
        rot = sb("rot", [P, 2, 2 * D])
        neg = sb("neg", [P, 2, 2 * D])
        phi = sb("phi", [P, 2, 2 * D])
        va = sb("va", [P, 2, KD, SW])
        gt = sb("gt", [P, 2, D])
        qT = sb("qT", [P, KD, P])
        sm = sb("sm", [P, 2, KD, SW])
        den = sb("den", [P, KD, HPH])
        rden = sb("rden", [P, KD, HPH])
        on = sb("on", [P, 2, D])
        og = sb("og", [P, 2, D])
        oT = sb("oT", [P, KD, P])
        xb = sb("xb", [P, 2, D])
        x1 = sb("x1", [P, 2, D])
        xn = sb("xn", [P, 2, D])
        xnT = sb("xnT", [P, KD, P])

        loads, xg = sem("loads"), [sem(f"xg{g}") for g in range(4)]
        s_w, s_cst = sem("w"), sem("cst")
        s_ssq1, s_r1, s_xs, s_tx, s_xT = map(sem, ("ssq1", "r1", "xs", "tx", "xT"))
        s_pj0, s_pj1, s_qk, s_ra, s_rb, s_rot, s_vg = map(sem, ("pj0", "pj1", "qk", "ra", "rb", "rot", "vg"))
        s_mn, s_ex, s_phi, s_th, s_g = map(sem, ("mn", "ex", "phi", "th", "g"))
        s_tq, s_qT, s_sa, s_mk, s_num = map(sem, ("tq", "qT", "sa", "mk", "num"))
        s_den, s_rden, s_on, s_og = map(sem, ("den", "rden", "on", "og"))
        s_to, s_oT, s_wo, s_xb, s_x1, s_xacc = map(sem, ("to", "oT", "wo", "xb", "x1", "xacc"))
        s_ssq2, s_r2, s_xn, s_tr, s_xnT, s_rt, s_lg = map(sem, ("ssq2", "r2", "xn", "tr", "xnT", "rt", "lg"))
        s_st, s_wst, s_pass, s_pass_dve = [sem(f"st{b}") for b in range(2)], sem("wst"), sem("pass"), sem("pass_dve")

        ident = cst[:, C_ID:C_ID + P]
        hmask = cst[:, C_MASK:C_MASK + SW].unsqueeze(1).to_broadcast([P, KD, SW])
        b_tx, b_tq, b_tor, b_num, b_p0, b_p1 = bank[0:6]
        b_s = bank[6:8]
        tx_ps = b_tx[:, 0:D].rearrange("p (k t) -> p k t", k=KD)
        rt_ps = b_tx[:, 0:E]
        tq_ps = b_tq[:, 0:D].rearrange("p (k t) -> p k t", k=KD)
        wo_ps = b_tq[:, 0:D]
        to_ps = b_tor[:, 0:D].rearrange("p (k t) -> p k t", k=KD)
        tr_ps = b_tor[:, D:2 * D].rearrange("p (k t) -> p k t", k=KD)
        num_ps = b_num[:, 0:KD * SW].rearrange("p (k c) -> p k c", k=KD)
        s_ps = [b[:, 0:KD * SW].rearrange("p (k c) -> p k c", k=KD) for b in b_s]

        def halves(ap):
            return ap.rearrange("p (h a d) -> p h a d", a=2, d=HALF)

        block = ctx.enter_context(nc.Block())

        @block.sync
        def _(sp):
            xv = io["x"].rearrange("b (i p) d -> p b i d", p=P)
            Xv = X[:, :, :].rearrange("p (b i) d -> p b i d", b=BATCH)
            g = TPB // 4
            sp.dma_start(cst[:, :], io["consts"]).then_inc(loads, 16)
            for b in range(BATCH):
                sp.dma_start(Xv[:, b, 0:g, :], xv[:, b, 0:g, :]).then_inc(xg[0], 16)
            sp.dma_start(wqkvg[:, :, :], io["wqkvg"].rearrange("(k p) n -> p k n", p=P)).then_inc(loads, 16)
            sp.dma_start(sc1[:, :], io["sc1"]).then_inc(loads, 16)
            sp.dma_start(sc2[:, :], io["sc2"]).then_inc(loads, 16)
            sp.dma_start(bqkvg[:, :], io["bqkvg"].partition_broadcast(P)).then_inc(loads, 16)
            sp.dma_start(bo[:, :], io["bo"].partition_broadcast(P)).then_inc(loads, 16)
            sp.dma_start(rope[:, :, :], io["rope"]).then_inc(loads, 16)
            sp.dma_start(wo[:, :, :], io["wo"].rearrange("(k p) n -> p k n", p=P)).then_inc(loads, 16)
            sp.dma_start(wr[:, :, :], io["wr1"].rearrange("(k p) n -> p k n", p=P)).then_inc(loads, 16)
            for q in range(1, 4):
                for b in range(BATCH):
                    sp.dma_start(Xv[:, b, q * g:q * g + g, :], xv[:, b, q * g:q * g + g, :]).then_inc(xg[q], 16)
            sp.dma_start(wraw[:, 0:4 * HID], io["w_moe"][0]).then_inc(s_wst, 16)

            def step(at):
                if (t := at(-2)) is not None:
                    after(sp, s_xn, t.n + 1)
                    sp.dma_start(io["xn1"][bass.ts(t.T, P), :], xn[:, t.b, :]).then_inc(s_st[t.b], 16)
            run_tiles(sp, step, lambda: None)
            for b in range(BATCH):
                sp.wait_ge(s_st[b], 16 * TPB)
            sp.wait_ge(s_wst, 16)

        @block.gpsimd
        def _(pool):
            nc.gpsimd.memset(mhalf[:, :], -0.5).then_inc(s_cst, 1)
            nc.gpsimd.memset(zeros[:, :], 0.0).then_inc(s_cst, 1)
            nc.gpsimd.memset(va[:, :, :, :], 1.0).then_inc(s_cst, 1)
            pool.wait_ge(s_cst, 3)
            pool.wait_ge(loads, 16 * 9)
            pool.wait_ge(xg[0], 32)

            def step(at):
                if (t := at(-2)) is not None:
                    after(pool, s_ssq2, t.n + 1, s_pass)
                    after(pool, s_xn, t.n - 1, s_pass)
                    nc.gpsimd.tensor_tensor(r2[:, t.b:t.b + 1], ssq2[:, t.b:t.b + 1], mhalf[:, :], ALU.pow).then_inc(s_r2, 1)
                if (t := at(2)) is not None:
                    after(pool, s_ssq1, t.n + 1, s_pass)
                    after(pool, s_xs, t.n - 1, s_pass)
                    nc.gpsimd.tensor_tensor(r1[:, t.b:t.b + 1], ssq1[:, t.b:t.b + 1], mhalf[:, :], ALU.pow).then_inc(s_r1, 1)
                if (t := at(1)) is not None:
                    after(pool, s_qk, t.n + 1, s_pass)
                    after(pool, s_rot, t.n, s_pass)
                    for a in range(2):
                        sn = rope[:, t.i, HALF + a * HALF:HALF + (a + 1) * HALF]
                        nc.gpsimd.tensor_tensor(halves(rb[:, :])[:, :, a, :], halves(qk[:, :])[:, :, 1 - a, :],
                                                sn.unsqueeze(1).to_broadcast([P, 2 * H, HALF]), ALU.mult).then_inc(s_rb, 1)
                if (t := at(-1)) is not None:
                    after(pool, s_x1, t.n - 1, s_pass)
                    nc.gpsimd.tensor_tensor(xb[:, t.b, :], X[:, t.T, :], bo[:, :], ALU.add).then_inc(s_xb, 1)
                if (t := at(1)) is not None:
                    after(pool, s_th, t.n + 1, s_pass)
                    nc.gpsimd.tensor_scalar(gt[:, t.b, :], gt[:, t.b, :], 0.5, 0.5, ALU.mult, ALU.add).then_inc(s_g, 1)
                if (t := at(0)) is not None:
                    after(pool, s_g, t.n + 1, s_pass)
                    after(pool, s_on, t.n + 1, s_pass)
                    after(pool, s_to, t.n - 1, s_pass)
                    nc.gpsimd.tensor_tensor(og[:, t.b, :], on[:, t.b, :], gt[:, t.b, :], ALU.mult).then_inc(s_og, 1)
                if (t := at(-1)) is not None:
                    after(pool, s_xb, t.n + 1, s_pass)
                    after(pool, s_x1, t.n + 1, s_pass)
                    nc.gpsimd.tensor_tensor(X[:, t.T, :], X[:, t.T, :], x1[:, t.b, :], ALU.add).then_inc(s_xacc, 1)

            def all_x():
                for q in range(1, 4):
                    pool.wait_ge(xg[q], 32)
            run_tiles(pool, step, all_x)

        @block.scalar
        def _(act):
            act.wait_ge(xg[0], 32)

            def step(at):
                if (t := at(-2)) is not None:
                    after(act, s_x1, t.n + 1)
                    after(act, s_r2, t.n - 1)
                    nc.scalar.activation(junk[:, 0, t.b, :], x1[:, t.b, :], ACT.Square, accum_out=ssq2[:, t.b:t.b + 1]).then_inc(s_ssq2, 1)
                if (t := at(2)) is not None:
                    after(act, s_r1, t.n - 1)
                    nc.scalar.activation(junk[:, 1, t.b, :], X[:, t.T, :], ACT.Square, accum_out=ssq1[:, t.b:t.b + 1]).then_inc(s_ssq1, 1)
                if (t := at(0)) is not None:
                    after(act, s_tq, t.n + 1)
                    after(act, s_num, t.n)
                    nc.scalar.activation(qT[:, :, :], tq_ps, ACT.Copy).then_inc(s_qT, 1)
                o, r = at(-1), at(-2)
                if o is not None:
                    after(act, s_to, o.n + 1)
                if r is not None:
                    after(act, s_tr, r.n + 1)
                if o is not None:
                    after(act, s_wo, o.n)
                    nc.scalar.activation(oT[:, :, :], to_ps, ACT.Copy).then_inc(s_oT, 1)
                if r is not None:
                    after(act, s_rt, r.n)
                    nc.scalar.activation(xnT[:, :, :], tr_ps, ACT.Copy).then_inc(s_xnT, 1)
                if (t := at(1)) is not None:
                    after(act, s_vg, 2 * t.n + 2)
                    nc.scalar.activation(gt[:, t.b, :], gt[:, t.b, :], ACT.Tanh, scale=0.5).then_inc(s_th, 1)
                    after(act, s_mn, t.n + 1)
                    nc.scalar.activation(neg[:, t.b, :], neg[:, t.b, :], ACT.Exp).then_inc(s_ex, 1)
                if (t := at(2)) is not None:
                    after(act, s_tx, t.n + 1)
                    after(act, s_pj1, t.n - 1)
                    nc.scalar.activation(xT[:, t.b, :, :], tx_ps, ACT.Copy).then_inc(s_xT, 1)

            def all_x():
                for q in range(1, 4):
                    act.wait_ge(xg[q], 32)
            run_tiles(act, step, all_x)

        @block.vector
        def _(dve):
            dve.wait_ge(loads, 16 * 9)
            for k in range(KD):
                nc.vector.tensor_scalar(wqkvg[:, k, :], wqkvg[:, k, :], sc1[:, k:k + 1], None, ALU.mult).then_inc(s_w, 1)
                nc.vector.tensor_scalar(wr[:, k, :], wr[:, k, :], sc2[:, k:k + 1], None, ALU.mult).then_inc(s_w, 1)
            dve.wait_ge(s_cst, 3)
            dve.wait_ge(xg[0], 32)

            def step(at):
                if (t := at(1)) is not None:
                    after(dve, s_pj0, t.n + 1)
                    after(dve, s_rb, 2 * t.n)
                    nc.vector.tensor_tensor(qk[:, :], b_p0[:, :], bqkvg[:, 0:2 * D], ALU.add).then_inc(s_qk, 1)
                if (t := at(-2)) is not None:
                    after(dve, s_r2, t.n + 1)
                    after(dve, s_st[t.b], t.i * 16)
                    after(dve, s_tr, t.n - 1)
                    nc.vector.tensor_scalar(xn[:, t.b, :], x1[:, t.b, :], r2[:, t.b:t.b + 1], float(D) ** 0.5,
                                            ALU.mult, ALU.mult).then_inc(s_xn, 1)
                if (t := at(1)) is not None:
                    after(dve, s_qk, t.n + 1)
                    cs = rope[:, t.i, 0:HALF].unsqueeze(1).to_broadcast([P, 4 * H, HALF])
                    nc.vector.tensor_tensor(ra[:, :].rearrange("p (h d) -> p h d", d=HALF),
                                            qk[:, :].rearrange("p (h d) -> p h d", d=HALF), cs, ALU.mult).then_inc(s_ra, 1)
                    after(dve, s_pj1, t.n + 1)
                    after(dve, s_sa, 2 * t.n - 2)
                    nc.vector.tensor_tensor(va[:, t.b, :, 0:P], b_p1[:, 0:D].rearrange("p (k c) -> p k c", k=KD),
                                            bqkvg[:, 2 * D:3 * D].rearrange("p (k c) -> p k c", k=KD), ALU.add).then_inc(s_vg, 1)
                    after(dve, s_og, t.n - 1)
                    nc.vector.tensor_tensor(gt[:, t.b, :], b_p1[:, D:2 * D], bqkvg[:, 3 * D:4 * D], ALU.add).then_inc(s_vg, 1)
                    after(dve, s_rb, 2 * t.n + 2)
                    after(dve, s_ra, t.n + 1)
                    nc.vector.tensor_tensor(rot[:, t.b, :], ra[:, :], rb[:, :], ALU.add).then_inc(s_rot, 1)
                    after(dve, s_rot, t.n + 1)
                    nc.vector.tensor_scalar(neg[:, t.b, :], rot[:, t.b, :], 0.0, None, ALU.min).then_inc(s_mn, 1)
                if (t := at(0)) is not None:
                    after(dve, s_num, t.n)
                    for c in range(2):
                        after(dve, s_sa, 2 * t.n + c + 1)
                        nc.vector.tensor_tensor(sm[:, c, :, :], s_ps[t.b], hmask, ALU.mult).then_inc(s_mk, 1)
                if (t := at(2)) is not None:
                    after(dve, s_r1, t.n + 1)
                    after(dve, s_tx, t.n - 1)
                    nc.vector.tensor_scalar(xs[:, t.b, :], X[:, t.T, :], r1[:, t.b:t.b + 1], float(D) ** 0.5,
                                            ALU.mult, ALU.mult).then_inc(s_xs, 1)
                if (t := at(1)) is not None:
                    after(dve, s_ex, t.n + 1)
                    after(dve, s_sa, 2 * t.n - 2)
                    after(dve, s_tq, t.n - 1)
                    nc.vector.scalar_tensor_tensor(out=phi[:, t.b, :], in0=rot[:, t.b, :], scalar=0.0, in1=neg[:, t.b, :],
                                                   op0=ALU.max, op1=ALU.add).then_inc(s_phi, 1)
                if (t := at(0)) is not None:
                    after(dve, s_num, t.n + 1)
                    nc.vector.tensor_scalar(den[:, :, :], num_ps[:, :, P:SW], 1e-6, None, ALU.add).then_inc(s_den, 1)
                    after(dve, s_den, t.n + 1)
                    after(dve, s_on, t.n)
                    nc.vector.reciprocal(rden[:, :, :], den[:, :, :]).then_inc(s_rden, 1)
                    after(dve, s_rden, t.n + 1)
                    after(dve, s_og, t.n - 1)
                    for k in range(KD):
                        ins = nc.vector.tensor_tensor(
                            on[:, t.b, k * P:(k + 1) * P].rearrange("p (h d) -> p h d", d=DK),
                            num_ps[:, k, 0:P].rearrange("p (h d) -> p h d", d=DK),
                            rden[:, k, :].unsqueeze(2).to_broadcast([P, HPH, DK]), ALU.mult)
                        if k == KD - 1:
                            ins.then_inc(s_on, 1)
                if (t := at(-1)) is not None:
                    after(dve, s_wo, t.n + 1)
                    after(dve, s_xb, t.n + 1)
                    after(dve, s_xacc, t.n - 1)
                    after(dve, s_ssq2, t.n - 1)
                    after(dve, s_xn, t.n - 1)
                    nc.vector.tensor_tensor(x1[:, t.b, :], wo_ps, xb[:, t.b, :], ALU.add).then_inc(s_x1, 1)
                if (t := at(-2)) is not None:
                    after(dve, s_rt, t.n + 1, s_pass_dve)
                    nc.vector.tensor_copy(LG[:, t.T, :], rt_ps).then_inc(s_lg, 1)

            def all_x():
                for q in range(1, 4):
                    dve.wait_ge(xg[q], 32)
            run_tiles(dve, step, all_x)

        @block.tensor
        def _(pe):
            pe.wait_ge(loads, 16 * 9)
            pe.wait_ge(s_cst, 3)
            pe.wait_ge(s_w, 2 * KD)
            for b in range(BATCH):
                nc.tensor.matmul(b_s[b][:, 0:KD * SW], zeros[:, 0:P], zeros[:, :], start=True, stop=True)

            def add_chunk(t, c):
                rows = slice(c * CHUNK, (c + 1) * CHUNK)
                for k in range(KD):
                    ins = nc.tensor.matmul(s_ps[t.b][:, k, :], phi[rows, t.b, D + k * P:D + (k + 1) * P],
                                           va[rows, t.b, k, :], start=False, stop=True, skip_group_check=True)
                ins.then_inc(s_sa, 1)

            def step(at):
                if (t := at(1)) is not None:
                    after(pe, s_xT, t.n + 1)
                    for part, b_p, done, free in ((0, b_p0, s_pj0, (s_qk, t.n)), (1, b_p1, s_pj1, (s_vg, 2 * t.n))):
                        after(pe, *free)
                        for k in range(KD):
                            ins = nc.tensor.matmul(b_p[:, :], xT[:, t.b, k, :], wqkvg[:, k, part * 2 * D:(part + 1) * 2 * D],
                                                   start=(k == 0), stop=(k == KD - 1))
                        ins.then_inc(done, 1)
                if (t := at(0)) is not None:
                    after(pe, s_phi, t.n + 1)
                    after(pe, s_x1, t.n - 1)
                    for k in range(KD):
                        ins = nc.tensor.transpose(tq_ps[:, k, :], phi[:, t.b, k * P:(k + 1) * P], ident)
                    ins.then_inc(s_tq, 1)
                    after(pe, s_mk, 2 * t.n - 2)
                    add_chunk(t, 0)
                o, r = at(-1), at(-2)
                if o is not None:
                    after(pe, s_og, o.n + 1)
                    after(pe, s_oT, o.n)
                    after(pe, s_xnT, o.n - 1)
                    for k in range(KD):
                        ins = nc.tensor.transpose(to_ps[:, k, :], og[:, o.b, k * P:(k + 1) * P], ident)
                    ins.then_inc(s_to, 1)
                if r is not None:
                    after(pe, s_xn, r.n + 1)
                    after(pe, s_oT, r.n + 1)
                    after(pe, s_xnT, r.n)
                    for k in range(KD):
                        ins = nc.tensor.transpose(tr_ps[:, k, :], xn[:, r.b, k * P:(k + 1) * P], ident)
                    ins.then_inc(s_tr, 1)
                if (t := at(0)) is not None:
                    after(pe, s_mk, 2 * t.n + 1)
                    add_chunk(t, 1)
                if (t := at(2)) is not None:
                    after(pe, s_xs, t.n + 1)
                    after(pe, s_xT, t.n)
                    after(pe, s_lg, t.n - 4)
                    for k in range(KD):
                        ins = nc.tensor.transpose(tx_ps[:, k, :], xs[:, t.b, k * P:(k + 1) * P], ident)
                    ins.then_inc(s_tx, 1)
                if (t := at(0)) is not None:
                    after(pe, s_qT, t.n + 1)
                    after(pe, s_on, t.n)
                    for c in range(2):
                        after(pe, s_mk, 2 * t.n + c + 1)
                        rows = slice(c * CHUNK, (c + 1) * CHUNK)
                        for k in range(KD):
                            ins = nc.tensor.matmul(num_ps[rows, k, :], qT[:, k, rows], sm[:, c, k, :], start=True, stop=True)
                    ins.then_inc(s_num, 1)
                if (t := at(-1)) is not None:
                    after(pe, s_oT, t.n + 1)
                    after(pe, s_qT, t.n + 2 if isinstance(t.n, int) and t.n + 2 <= NT else (NT if isinstance(t.n, int) else t.n + 2))
                    after(pe, s_x1, t.n)
                    for k in range(KD):
                        ins = nc.tensor.matmul(wo_ps, oT[:, k, :], wo[:, k, :], start=(k == 0), stop=(k == KD - 1))
                    ins.then_inc(s_wo, 1)
                if (t := at(-2)) is not None:
                    after(pe, s_xnT, t.n + 1)
                    after(pe, s_xT, min(t.n + 5, NT) if isinstance(t.n, int) else t.n + 5)
                    after(pe, s_lg, t.n)
                    for k in range(KD):
                        ins = nc.tensor.matmul(rt_ps, xnT[:, k, :], wr[:, k, :], start=(k == 0), stop=(k == KD - 1))
                    ins.then_inc(s_rt, 1)
            run_tiles(pe, step, lambda: None)


def routing_phase(nc, bank, io, tag, first, LG, GATE, GI, IDX, cst, wraw, ws0, qw):
    with ExitStack() as ctx:
        def sb(name, shape, dt=F32):
            return ctx.enter_context(nc.sbuf_tensor(f"{tag}_{name}", shape, dt))

        def sem(name):
            return ctx.enter_context(nc.semaphore(f"{tag}_{name}"))

        rb = sb("rb", [P, E])
        best = sb("best", [P, 2, NT])
        eq = sb("eq", [P, NT, E])
        rev = sb("rev", [P, 2, NT])
        oh = sb("oh", [P, 2, NT, E])
        ohr = sb("ohr", [P, 2, NT, E])
        sel = sb("sel", [P, NT, E], BF16)
        tri = sb("tri", [P, P], BF16)
        ones = sb("ones", [P, P], BF16)
        onef = sb("onef", [P, NT])
        iota = sb("iota", [P, P], BF16)
        zero = sb("zero", [P, 2 * SC], BF16)
        tot = sb("tot", [P, NT, E])
        cum = sb("cum", [P, NT, E])
        rank = sb("rank", [P, NT, E])
        rk = sb("rk", [P, 2, NT])
        kept = sb("kept", [P, 2, NT])
        slot = sb("slot", [P, 2, NT])
        inv = sb("inv", [P, 2, NT])
        invi = sb("invi", [P, 2, NT], I32)
        pci = sb("pci", [P, 2, 2, NT], I32)
        pcf = sb("pcf", [P, 2, 2, NT])
        dl = sb("dl", [P, NT])
        ex = sb("ex", [P, 2, NT])
        den = sb("den", [P, NT])
        rg = sb("rg", [P, NT])
        row1h = sb("row1h", [P, 4, P], BF16)
        col1h = sb("col1h", [P, 4, 2, SC], BF16)
        tok = sb("tok", [P, SC])

        s_ld, s_v, s_ex, s_exin, s_sel, s_rank, s_z = map(sem, ("ld", "v", "ex", "exin", "sel", "rank", "z"))
        s_1h, s_inv, s_set, s_hi, s_lo = map(sem, ("1h", "inv", "set", "hi", "lo"))
        rank_ps = bank[0][:, 0:NT * E].rearrange("p (t e) -> p t e", e=E)
        tot_ps = bank[1][:, 0:NT * E].rearrange("p (t e) -> p t e", e=E)
        tok_ps = bank[2][:, 0:2 * SC].rearrange("p (a c) -> p a c", a=2)
        revc = cst[:, C_REV:C_REV + E].unsqueeze(1).to_broadcast([P, NT, E])

        def over_e(ap):
            return ap.unsqueeze(2).to_broadcast([P, NT, E])

        block = ctx.enter_context(nc.Block())

        @block.sync
        def _(sp):
            if first:
                sp.dma_start(rb[:, :], io["rb"].partition_broadcast(P)).then_inc(s_ld, 16)
                sp.wait_ge(s_ld, 16)

        @block.scalar
        def _(act):
            for q in range(4):
                nc.scalar.activation(ws0[:, 0, q * qw:(q + 1) * qw], wraw[:, q * qw:(q + 1) * qw], ACT.Copy).then_inc(s_hi, 1)
                if q == 1:
                    act.wait_ge(s_exin, 1)
                    nc.scalar.activation(ex[:, 1, :], dl[:, :], ACT.Exp).then_inc(s_ex, 1)

        @block.gpsimd
        def _(pool):
            nc.gpsimd.memset(zero[:, :], 0.0).then_inc(s_set, 1)
            nc.gpsimd.memset(ones[:, :], 1.0).then_inc(s_set, 1)
            nc.gpsimd.memset(onef[:, :], 1.0).then_inc(s_set, 1)
            nc.gpsimd.tensor_copy(tri[:, :], cst[:, C_TRI:C_TRI + P]).then_inc(s_set, 1)
            nc.gpsimd.tensor_copy(iota[:, :], cst[:, C_IOTA:C_IOTA + P]).then_inc(s_set, 1)
            for q in range(4):
                pool.wait_ge(s_hi, q + 1)
                nc.gpsimd.tensor_tensor(ws0[:, 1, q * qw:(q + 1) * qw], wraw[:, q * qw:(q + 1) * qw],
                                        ws0[:, 0, q * qw:(q + 1) * qw].bitcast(F32), ALU.subtract).then_inc(s_lo, 1)

        @block.vector
        def _(dve):
            done = [0]

            def chain(ins):
                done[0] += 1
                ins.then_inc(s_v, 1)
                dve.wait_ge(s_v, done[0])

            V = nc.vector
            if first:
                dve.wait_ge(s_ld, 16)
                chain(V.tensor_tensor(LG[:, :, :], LG[:, :, :], rb[:, :].unsqueeze(1).to_broadcast([P, NT, E]), ALU.add))
            else:
                chain(V.tensor_scalar(LG[:, :, :], LG[:, :, :], CLAMP, -CLAMP, ALU.min, ALU.max))
            for c in range(2):
                chain(V.tensor_reduce(best[:, c, :], LG[:, :, :], AX_X, ALU.max))
                chain(V.tensor_tensor(eq[:, :, :], LG[:, :, :], over_e(best[:, c, :]), ALU.is_equal))
                chain(V.tensor_tensor(eq[:, :, :], eq[:, :, :], revc, ALU.mult))
                chain(V.tensor_reduce(rev[:, c, :], eq[:, :, :], AX_X, ALU.max))
                chain(V.tensor_tensor(oh[:, c, :, :], revc, over_e(rev[:, c, :]), ALU.is_equal))
                if c == 0:
                    chain(V.scalar_tensor_tensor(out=LG[:, :, :], in0=oh[:, 0, :, :], scalar=-3e38, in1=LG[:, :, :],
                                                 op0=ALU.mult, op1=ALU.add))
            V.tensor_tensor(dl[:, :], best[:, 1, :], best[:, 0, :], ALU.subtract).then_inc(s_exin, 1)
            V.tensor_tensor(sel[:, :, :], oh[:, 0, :, :], oh[:, 1, :, :], ALU.add).then_inc(s_sel, 1)
            dve.wait_ge(s_set, 5)
            dve.wait_ge(s_rank, 2)
            chain(V.tensor_copy(tot[:, :, :], tot_ps))
            for e in range(E):
                ins = V.tensor_tensor_scan(cum[:, :, e], onef[:, :], tot[:, :, e], 0.0, ALU.mult, ALU.add)
                if e == E - 1:
                    chain(ins)
            chain(V.tensor_tensor(cum[:, :, :], cum[:, :, :], tot[:, :, :], ALU.subtract))
            chain(V.tensor_tensor(rank[:, :, :], rank_ps, cum[:, :, :], ALU.add))
            for c in range(2):
                ins = V.tensor_tensor(ohr[:, c, :, :], oh[:, c, :, :], rank[:, :, :], ALU.mult)
            chain(ins)
            chain(V.tensor_reduce(rk[:, :, :], ohr[:, :, :, :], AX_X, ALU.add))
            V.tensor_scalar(kept[:, :, :], rk[:, :, :], float(CAP), None, ALU.is_lt)
            chain(V.tensor_scalar(slot[:, :, :], rev[:, :, :], -float(CAP), float(SLOTS), ALU.mult, ALU.add))
            chain(V.tensor_tensor(slot[:, :, :], slot[:, :, :], rk[:, :, :], ALU.add))
            V.tensor_scalar(GI[:, :, :].rearrange("p t c -> p c t"), slot[:, :, :], float(SLOTS - 1), None, ALU.min)
            chain(V.scalar_tensor_tensor(out=inv[:, :, :], in0=kept[:, :, :], scalar=-16384.0, in1=slot[:, :, :],
                                         op0=ALU.mult, op1=ALU.add))
            chain(V.tensor_scalar(invi[:, :, :], inv[:, :, :], 16384.0, None, ALU.add))
            V.tensor_scalar(pci[:, 0, :, :], invi[:, :, :], P - 1, None, ALU.bitwise_and)
            chain(V.tensor_scalar(pci[:, 1, :, :], invi[:, :, :], 7, None, ALU.logical_shift_right))
            chain(V.tensor_copy(pcf[:, :, :, :], pci[:, :, :, :]))
            dve.wait_ge(s_ex, 1)
            chain(V.tensor_scalar(den[:, :], ex[:, 1, :], 1.0, 0.0 if first else 1e-12, ALU.add, ALU.add))
            chain(V.reciprocal(rg[:, :], den[:, :]))
            V.tensor_tensor(GATE[:, :, 0], rg[:, :], kept[:, 0, :], ALU.mult)
            chain(V.tensor_tensor(ex[:, 0, :], ex[:, 1, :], kept[:, 1, :], ALU.mult))
            chain(V.tensor_tensor(GATE[:, :, 1], ex[:, 0, :], rg[:, :], ALU.mult))
            with dve.Fori(0, NT // 2) as j:
                for r in range(2):
                    for c in range(2):
                        g = 2 * r + c
                        T = j * 2 + r
                        if g == 0:
                            dve.wait_ge(s_inv, j * 4 + 4)
                        pf, cf = pcf[:, 0, c, bass.ds(T, 1)], pcf[:, 1, c, bass.ds(T, 1)]
                        V.tensor_scalar(row1h[:, g, :], iota[:, :], pf, None, ALU.is_equal).then_inc(s_1h, 1)
                        V.tensor_scalar(col1h[:, g, 0, :], iota[:, 0:SC], cf, cst[:, bass.ds(T + C_IOTA, 1)], ALU.is_equal,
                                        ALU.mult).then_inc(s_1h, 1)
                        V.tensor_scalar(col1h[:, g, 1, :], iota[:, 0:SC], cf, cst[:, C_ROW:C_ROW + 1], ALU.is_equal,
                                        ALU.mult).then_inc(s_1h, 1)
            dve.wait_ge(s_inv, 2 * NT + 4)
            chain(V.tensor_scalar(tok[:, :], tok_ps[:, 0, :], float(P), None, ALU.mult))
            chain(V.tensor_tensor(IDX[:, :], tok_ps[:, 1, :], tok[:, :], ALU.add))

        @block.tensor
        def _(pe):
            pe.wait_ge(s_set, 5)
            pe.wait_ge(s_sel, 1)
            cols = sel[:, :, :].rearrange("p t e -> p (t e)")
            nc.tensor.matmul(bank[0][:, 0:NT * E], tri[:, :], cols, start=True, stop=True).then_inc(s_rank, 1)
            nc.tensor.matmul(bank[1][:, 0:NT * E], ones[:, :], cols, start=True, stop=True).then_inc(s_rank, 1)
            nc.tensor.matmul(bank[2][:, 0:2 * SC], ones[:, :], zero[:, :], start=True, stop=True)
            pe.sem_inc(s_inv, 4)
            with pe.Fori(0, NT // 2) as j:
                for g in range(4):
                    pe.wait_ge(s_1h, j * 12 + 3 * (g + 1))
                    nc.tensor.matmul(bank[2][:, 0:2 * SC], row1h[:, g, :], col1h[:, g, :, :].rearrange("p a c -> p (a c)"),
                                     start=False, stop=True, skip_group_check=True).then_inc(s_inv, 1)


def expert_phase(nc, bank, io, tag, glu, IDX, xn_dram, y_dram, w_dram, sc_dram, cst, wraw, ws):
    qw = 1536 if glu else 1024
    w2_at = 4096 if glu else 2048
    with ExitStack() as ctx:
        def sb(name, shape, dt=F32):
            return ctx.enter_context(nc.sbuf_tensor(f"{tag}_{name}", shape, dt))

        def sem(name):
            return ctx.enter_context(nc.semaphore(f"{tag}_{name}"))

        xg = sb("xg", [P, UT, D])
        ist = sb("ist", [P, UT], I32)
        xraw = sb("xraw", [P, KD, UW])
        xT = sb("xT", [P, 2, KD, UW], F32R)
        hT = sb("hT", [P, 2, NF, UW], F32R)
        hraw = sb("hraw", [P, 4, UW])
        sg = sb("sg", [P, 4, UW]) if glu else None
        ysb = sb("ysb", [P, UT, D])
        scb = sb("scb", [P, 2 * KD])
        b1 = None if glu else sb("b1", [P, E * NF])
        b2 = None if glu else sb("b2", [P, E, D])

        s_ld, s_gi, s_gx, s_tg, s_xr, s_xh, s_xl = map(sem, ("ld", "gi", "gx", "tg", "xr", "xh", "xl"))
        s_hd, s_sg, s_hm, s_hh, s_hl = map(sem, ("hd", "sg", "hm", "hh", "hl"))
        s_y, s_ye, s_ys, s_wld, s_wh, s_wl = map(sem, ("y", "ye", "ys", "wld", "wh", "wl"))
        s_pass, s_pass_pe = sem("pass"), sem("pass_pe")
        RING = 4
        s_free = s_hm if glu else s_sg
        b_y, b_t = bank[4:6], bank[6]
        t_ps = b_t[:, :].rearrange("p (k n) -> p k n", k=KD)
        ident = cst[:, C_ID:C_ID + P]

        def experts(eng, unit, at_expert=None):
            def one(e, s, last):
                if at_expert:
                    at_expert(e, s, last)
                with eng.Fori(0, UPE - 1) as c:
                    unit(e, c, e * UPE + c, s, not last, True)
                unit(e, UPE - 1, e * UPE + (UPE - 1), s, False, not last)
            with eng.Fori(0, E // 2 - 1) as ee:
                for s in range(2):
                    one(ee * 2 + s, s, False)
            one(E - 2, 0, False)
            one(E - 1, 1, True)

        block = ctx.enter_context(nc.Block())

        @block.sync
        def _(sp):
            sp.dma_start(scb[:, :], sc_dram).then_inc(s_ld, 16)
            if not glu:
                sp.dma_start(b1[:, :], io["b1"]).then_inc(s_ld, 16)
                sp.dma_start(b2[:, :, :].rearrange("p e d -> p (e d)"), io["b2"].partition_broadcast(P)).then_inc(s_ld, 16)

            def next_weights(e, s, last):
                if not last:
                    sp.wait_ge(s_wl, e * 4 + 4)
                    sp.dma_start(wraw[:, 0:4 * qw], w_dram[bass.ds(e + 1, 1)].rearrange("a p n -> p (a n)")).then_inc(s_wld, 16)

            def unit(e, c, u, s, prefetch, more):
                sp.wait_ge(s_ye, u * UT + 2 * UT)
                sp.dma_start(y_dram[bass.ds(u * UW, UW), :].rearrange("(j p) d -> p j d", p=P), ysb[:, :, :]).then_inc(s_ys, 16)
            sp.sem_inc(s_ys, 16)
            experts(sp, unit, next_weights)
            sp.wait_ge(s_ys, 16 * UNITS + 16)

        @block.gpsimd
        def _(pool):
            def gather(u, n):
                nc.gpsimd.tensor_copy(ist[:, :], IDX[:, bass.ds(u * UT, UT)]).then_inc(s_gi, 1)
                after(pool, s_gi, n, s_pass)
                for j in range(UT):
                    nc.gpsimd.indirect_dma_start(
                        out=xg[:, j, :], out_offset=None, in_=xn_dram,
                        in_offset=bass.IndirectOffsetOnAxis(ap=ist[:, j:j + 1], axis=0)).then_inc(s_gx, 16)

            def unit(e, c, u, s, prefetch, more):
                if more:
                    after(pool, s_tg, u + 1, s_pass)
                    gather(u + 1, u + 2)
            gather(0, 1)
            experts(pool, unit)

        @block.scalar
        def _(act):
            def raw_rows():
                for k in range(KD):
                    nc.scalar.activation(xraw[:, k, :], t_ps[:, k, :], ACT.Identity, scale=scb[:, k:k + 1],
                                         bias=scb[:, KD + k:KD + k + 1]).then_inc(s_xr, 1)

            act.sem_inc(s_sg, RING)
            if glu:
                act.sem_inc(s_ye, UT)
            act.wait_ge(s_ld, 16 * (1 if glu else 3))
            act.wait_ge(s_tg, 1)
            raw_rows()

            def unit(e, c, u, s, prefetch, more):
                for f in range(NF):
                    g = u * NF + f
                    act.wait_ge(s_hd, g + 1)
                    ps = bank[f % RING]
                    if glu:
                        act.wait_ge(s_hm, g + 1)
                        nc.scalar.activation(sg[:, f % RING, :], ps[:, 0:UW], ACT.Silu).then_inc(s_sg, 1)
                    else:
                        act.wait_ge(s_hl, g + 1)
                        nc.scalar.activation(hraw[:, f % RING, :], ps[:, 0:UW], ACT.Gelu,
                                             bias=b1[:, bass.ds(e * NF + f, 1)]).then_inc(s_sg, 1)
                if more:
                    act.wait_ge(s_tg, u + 2)
                    act.wait_ge(s_xl, u + 1)
                    raw_rows()
                if prefetch:
                    act.wait_ge(s_wld, e * 16 + 16)
                    act.wait_ge(s_y, e * UPE + 1)
                    nc.scalar.activation(ws[1 - s][:, 0, bass.ds(c * qw, qw)], wraw[:, bass.ds(c * qw, qw)],
                                         ACT.Copy).then_inc(s_wh, 1)
                if glu:
                    act.wait_ge(s_y, u + 2)
                    act.wait_ge(s_ys, u * 16 + 16)
                    for j in range(UT):
                        nc.scalar.activation(ysb[:, j, :], b_y[j][:, 0:D], ACT.Copy).then_inc(s_ye, 1)
            experts(act, unit)

        @block.vector
        def _(dve):
            V = nc.vector

            def split_rows(n):
                dve.wait_ge(s_xr, 2 * n)
                V.tensor_copy(xT[:, 0, :, :], xraw[:, :, :]).then_inc(s_xh, 1)
                dve.wait_ge(s_xh, n)
                V.tensor_tensor(xT[:, 1, :, :], xraw[:, :, :], xT[:, 0, :, :].bitcast(F32), ALU.subtract).then_inc(s_xl, 1)

            dve.sem_inc(s_hl, RING)
            dve.sem_inc(s_hm, RING)
            dve.sem_inc(s_wl, 4)
            if not glu:
                dve.sem_inc(s_ye, UT)
                dve.wait_ge(s_ld, 16 * 3)
            split_rows(1)

            def unit(e, c, u, s, prefetch, more):
                def product(f):
                    dve.wait_ge(s_sg, u * NF + f + 1 + RING)
                    dve.wait_ge(s_hl, u * NF + f + 1)
                    V.tensor_tensor(hraw[:, f % RING, :], sg[:, f % RING, :], bank[f % RING][:, UW:2 * UW],
                                    ALU.mult).then_inc(s_hm, 1)

                def high(f):
                    if f == 0:
                        dve.wait_ge(s_y, u + 1)
                    dve.wait_ge(s_hm if glu else s_sg, u * NF + f + 1 + RING)
                    V.tensor_copy(hT[:, 0, f, :], hraw[:, f % RING, :]).then_inc(s_hh, 1)

                def low(f):
                    dve.wait_ge(s_hh, u * NF + f + 1)
                    V.tensor_tensor(hT[:, 1, f, :], hraw[:, f % RING, :], hT[:, 0, f, :].bitcast(F32),
                                    ALU.subtract).then_inc(s_hl, 1)

                lag = 1 if glu else 0
                for f in range(NF + 1 + lag):
                    if glu and f < NF:
                        product(f)
                    if lag <= f < NF + lag:
                        high(f - lag)
                    if f > lag:
                        low(f - 1 - lag)
                if more:
                    split_rows(u + 2)
                if prefetch:
                    dve.wait_ge(s_wh, e * 4 + c + 1)
                    V.tensor_tensor(ws[1 - s][:, 1, bass.ds(c * qw, qw)], wraw[:, bass.ds(c * qw, qw)],
                                    ws[1 - s][:, 0, bass.ds(c * qw, qw)].bitcast(F32), ALU.subtract).then_inc(s_wl, 1)
                if not glu:
                    dve.wait_ge(s_y, u + 2)
                    dve.wait_ge(s_ys, u * 16 + 16)
                    for j in range(UT):
                        V.tensor_tensor(ysb[:, j, :], b_y[j][:, 0:D], b2[:, bass.ds(e, 1), :].rearrange("p a d -> p (a d)"),
                                        ALU.add).then_inc(s_ye, 1)
            experts(dve, unit)

        @block.tensor
        def _(pe):
            def turn_rows(n):
                pe.wait_ge(s_gx, n * 16 * UT)
                for j in range(UT):
                    for k in range(KD):
                        ins = nc.tensor.transpose(t_ps[:, k, j * P:(j + 1) * P], xg[:, j, k * P:(k + 1) * P], ident)
                ins.then_inc(s_tg, 1)

            def product(out, wts, mov, first, last):
                wh, wl = wts
                mh, ml = mov
                nc.tensor.matmul(out, wh, mh, start=first, stop=False)
                nc.tensor.matmul(out, wh, ml, start=False, stop=False)
                return nc.tensor.matmul(out, wl, mh, start=False, stop=last)

            pe.sem_inc(s_y, 1)
            turn_rows(1)

            def unit(e, c, u, s, prefetch, more):
                w = ws[s]
                pe.wait_ge(s_xl, u + 1)
                for f in range(NF):
                    pe.wait_ge(s_free, u * NF + f + 1)
                    for g in range(2 if glu else 1):
                        for k in range(KD):
                            at = k * (2 * HID if glu else HID) + g * HID + f * P
                            ins = product(bank[f % RING][:, g * UW:(g + 1) * UW],
                                          [w[:, a, at:at + P] for a in range(2)],
                                          [xT[:, a, k, :] for a in range(2)], k == 0, k == KD - 1)
                    ins.then_inc(s_hd, 1)
                if more:
                    turn_rows(u + 2)
                pe.wait_ge(s_ye, u * UT + UT)
                for f in range(NF):
                    pe.wait_ge(s_hl, u * NF + f + 1 + RING)
                    for j in range(UT):
                        ins = product(b_y[j][:, 0:D], [hT[:, a, f, j * P:(j + 1) * P] for a in range(2)],
                                      [w[:, a, w2_at + f * D:w2_at + (f + 1) * D] for a in range(2)], f == 0, f == NF - 1)
                ins.then_inc(s_y, 1)

            def weights(e, s, last):
                after(pe, s_wl, e * 4 + 4, s_pass_pe)
            experts(pe, unit, weights)


def combine_phase(nc, bank, io, tag, first, X, LG, GATE, GI, y_dram, cst, wraw):
    with ExitStack() as ctx:
        def sb(name, shape, dt=F32):
            return ctx.enter_context(nc.sbuf_tensor(f"{tag}_{name}", shape, dt))

        def sem(name):
            return ctx.enter_context(nc.semaphore(f"{tag}_{name}"))

        gi = sb("gi", [P, 2, 2], I32)
        yg = sb("yg", [P, 2, 2, D])
        acc = sb("acc", [P, 2, D])
        st = sb("st", [P, 2, 2, 6])
        mv = sb("mv", [P, 2, 2, 2])
        sd = sb("sd", [P, 2, 2])
        rs = sb("rs", [P, 2, 2])
        x2 = sb("x2", [P, 2, D])
        xr = sb("xr", [P, 2, D])
        xrT = sb("xrT", [P, 2, KD, P])
        scb = sb("scb", [P, 2 * KD])
        wr = sb("wr", [P, KD, E])
        eps = sb("eps", [P, 1])

        s_ld, s_gi, s_set = map(sem, ("ld", "gi", "set"))
        s_gy = [sem(f"gy{r}") for r in range(2)]
        s_a, s_acc, s_bs, s_mv, s_sd, s_rs, s_x2 = map(sem, ("a", "acc", "bs", "mv", "sd", "rs", "x2"))
        s_xc, s_xr, s_tr, s_xT, s_rt, s_lg, s_st = map(sem, ("xc", "xr", "tr", "xT", "rt", "lg", "st"))
        s_pass, s_pass_dve = sem("pass"), sem("pass_dve")
        norms = 2 if first else 1
        ident = cst[:, C_ID:C_ID + P]
        t_ps = [bank[r][:, 0:D].rearrange("p (k t) -> p k t", k=KD) for r in range(2)]
        rows = io["xn2"] if first else io["out"].rearrange("b s d -> (b s) d")
        store = xr if first else x2

        block = ctx.enter_context(nc.Block())

        @block.sync
        def _(sp):
            if first:
                sp.dma_start(scb[:, :], io["sc_ffn"]).then_inc(s_ld, 16)
                sp.dma_start(wr[:, :, :], io["wr2"].rearrange("(k p) n -> p k n", p=P)).then_inc(s_ld, 16)
                sp.dma_start(wraw[:, :], io["w_ffn"][0]).then_inc(s_ld, 16)
            sp.sem_inc(s_st, 32)
            with sp.Fori(0, NT // 2) as j:
                for r in range(2):
                    sp.wait_ge(s_xr if first else s_x2, j * 2 + r + (1 if first else 3))
                    sp.dma_start(rows[bass.ds((j * 2 + r) * P, P), :], store[:, r, :]).then_inc(s_st, 16)
            sp.wait_ge(s_st, 16 * NT + 32)
            if first:
                sp.wait_ge(s_ld, 16 * 3)

        @block.gpsimd
        def _(pool):
            nc.gpsimd.memset(eps[:, :], EPS).then_inc(s_set, 1)
            pool.sem_inc(s_a, 2)
            with pool.Fori(0, NT // 2) as j:
                for r in range(2):
                    T = j * 2 + r
                    after(pool, s_a, T + 1, s_pass)
                    nc.gpsimd.tensor_copy(gi[:, r, :], GI[:, bass.ds(T, 1), :].rearrange("p a c -> p (a c)")).then_inc(s_gi, 1)
                    after(pool, s_gi, T + 1, s_pass)
                    for c in range(2):
                        nc.gpsimd.indirect_dma_start(
                            out=yg[:, r, c, :], out_offset=None, in_=y_dram,
                            in_offset=bass.IndirectOffsetOnAxis(ap=gi[:, r, c:c + 1], axis=0)).then_inc(s_gy[r], 16)

        @block.scalar
        def _(act):
            act.wait_ge(s_set, 1)
            if first:
                act.wait_ge(s_ld, 16 * 3)
            act.sem_inc(s_xT, 4)
            with act.Fori(0, NT // 2) as j:
                for m in range(norms):
                    for r in range(2):
                        act.wait_ge(s_mv, j * 2 * norms + 2 * m + r + 1)
                        nc.scalar.activation(sd[:, m, r:r + 1], mv[:, m, r, 1:2], ACT.Sqrt, bias=eps[:, :]).then_inc(s_sd, 1)
                if first:
                    for r in range(2):
                        act.wait_ge(s_tr, j * 2 + r + 3)
                        act.wait_ge(s_rt, j * 2 + 2)
                        for k in range(KD):
                            nc.scalar.activation(xrT[:, r, k, :], t_ps[r][:, k, :], ACT.Identity, scale=scb[:, k:k + 1],
                                                 bias=scb[:, KD + k:KD + k + 1]).then_inc(s_xT, 1)

        @block.vector
        def _(dve):
            V = nc.vector
            if first:
                dve.wait_ge(s_ld, 16 * 3)
            dve.sem_inc(s_x2, 2)
            dve.sem_inc(s_lg, 2)
            with dve.Fori(0, NT // 2) as j:
                def tile(r):
                    return bass.ds(j * 2 + r, 1)

                def flat(ap):
                    return ap.rearrange("p a d -> p (a d)")

                for r in range(2):
                    dve.wait_ge(s_x2, j * 2 + 2)
                    dve.wait_ge(s_gy[r], (j + 1) * 32)
                    V.scalar_tensor_tensor(out=acc[:, r, :], in0=yg[:, r, 0, :], scalar=flat(GATE[:, tile(r), 0:1]),
                                           in1=flat(X[:, tile(r), :]), op0=ALU.mult, op1=ALU.add).then_inc(s_acc, 1)
                for r in range(2):
                    dve.wait_ge(s_acc, j * 2 + r + 1)
                    V.scalar_tensor_tensor(out=acc[:, r, :], in0=yg[:, r, 1, :], scalar=flat(GATE[:, tile(r), 1:2]),
                                           in1=acc[:, r, :], op0=ALU.mult, op1=ALU.add).then_inc(s_a, 1)
                for m in range(norms):
                    src = acc if m == 0 else x2
                    for r in range(2):
                        if m == 0:
                            dve.wait_ge(s_a, j * 2 + 2 + r + 1)
                        else:
                            dve.wait_ge(s_x2, j * 2 + r + 3)
                        V.bn_stats(st[:, m, r, :], src[:, r, :]).then_inc(s_bs, 1)
                    for r in range(2):
                        after(dve, s_bs, j * 2 * norms + 2 * m + r + 1, s_pass_dve)
                        V.bn_aggr(mv[:, m, r, :], st[:, m, r, :]).then_inc(s_mv, 1)
                    for r in range(2):
                        dve.wait_ge(s_sd, j * 2 * norms + 2 * m + r + 1)
                        V.reciprocal(rs[:, m, r:r + 1], sd[:, m, r:r + 1]).then_inc(s_rs, 1)
                    for r in range(2):
                        dve.wait_ge(s_rs, j * 2 * norms + 2 * m + r + 1)
                        dst = x2 if m == 0 else xr
                        if dst is store:
                            dve.wait_ge(s_st, j * 32 + 32)
                        if m == 1:
                            dve.wait_ge(s_tr, j * 2 + 2)
                        V.tensor_scalar(dst[:, r, :], src[:, r, :], mv[:, m, r, 0:1], rs[:, m, r:r + 1], ALU.subtract,
                                        ALU.mult).then_inc(s_x2 if m == 0 else s_xr, 1)
                if first:
                    for r in range(2):
                        after(dve, s_x2, j * 2 + r + 3, s_pass_dve)
                        V.tensor_copy(flat(X[:, tile(r), :]), x2[:, r, :]).then_inc(s_xc, 1)
                    for r in range(2):
                        after(dve, s_rt, j * 2 + r + 3, s_pass_dve)
                        V.tensor_copy(flat(LG[:, tile(r), :]), bank[2 + r][:, 0:E]).then_inc(s_lg, 1)

        @block.tensor
        def _(pe):
            if not first:
                return
            pe.wait_ge(s_ld, 16 * 3)
            pe.sem_inc(s_tr, 2)
            pe.sem_inc(s_rt, 2)
            with pe.Fori(0, NT // 2) as j:
                for r in range(2):
                    pe.wait_ge(s_xr, j * 2 + r + 1)
                    pe.wait_ge(s_xT, j * 4 + 4)
                    for k in range(KD):
                        ins = nc.tensor.transpose(t_ps[r][:, k, :], xr[:, r, k * P:(k + 1) * P], ident)
                    ins.then_inc(s_tr, 1)
                for r in range(2):
                    pe.wait_ge(s_xT, j * 4 + 2 * r + 6)
                    pe.wait_ge(s_lg, j * 2 + 2)
                    for k in range(KD):
                        ins = nc.tensor.matmul(bank[2 + r][:, 0:E], xrT[:, r, k, :], wr[:, k, :], start=(k == 0), stop=(k == KD - 1))
                    ins.then_inc(s_rt, 1)


def build(nc, io):
    with ExitStack() as ctx:
        def sb(name, shape, dt=F32):
            return ctx.enter_context(nc.sbuf_tensor(name, shape, dt))

        bank = [ctx.enter_context(nc.psum_tensor(f"bank{i}", [P, 512], F32)) for i in range(8)]
        X = sb("X", [P, NT, D])
        LG = sb("LG", [P, NT, E])
        GATE = sb("GATE", [P, NT, 2])
        GI = sb("GI", [P, NT, 2], I32)
        IDX = sb("IDX", [P, SC], I32)
        cst = sb("cst", [P, C_N])
        wraw = sb("wraw", [P, 4 * 1536])
        ws0 = sb("ws0", [P, 2, 6144], F32R)

        attention_phase(nc, bank, io, X, LG, cst, wraw)
        routing_phase(nc, bank, io, "R1", True, LG, GATE, GI, IDX, cst, wraw, ws0, 1024)
        with nc.sbuf_tensor("ws1a", [P, 2, 4096], F32R) as ws1:
            expert_phase(nc, bank, io, "E1", False, IDX, io["xn1"], io["y1"], io["w_moe"], io["sc_moe"], cst, wraw, (ws0, ws1))
        combine_phase(nc, bank, io, "C1", True, X, LG, GATE, GI, io["y1"], cst, wraw)
        routing_phase(nc, bank, io, "R2", False, LG, GATE, GI, IDX, cst, wraw, ws0, 1536)
        with nc.sbuf_tensor("ws1b", [P, 2, 6144], F32R) as ws1:
            expert_phase(nc, bank, io, "E2", True, IDX, io["xn2"], io["y2"], io["w_ffn"], io["sc_ffn"], cst, wraw, (ws0, ws1))
        combine_phase(nc, bank, io, "C2", False, X, LG, GATE, GI, io["y2"], cst, wraw)


def kernel(**inputs):
    import concourse.bacc as bacc
    from concourse.bass_utils import run_bass_kernel_spmd

    g = {k: np.asarray(v) for k, v in inputs.items()}

    def column(v):
        return v.reshape(KD, P).T

    w1 = g["L0_attn_W1"].reshape(E, KD, P, HID).transpose(0, 2, 1, 3).reshape(E, P, -1)
    w2 = g["L0_attn_W2"].reshape(E, NF, P, D).transpose(0, 2, 1, 3).reshape(E, P, -1)
    w12 = g["L0_ffn_w12"].transpose(0, 2, 1).reshape(E, KD, P, 2 * HID).transpose(0, 2, 1, 3).reshape(E, P, -1)
    w3 = g["L0_ffn_w3"].transpose(0, 2, 1).reshape(E, NF, P, D).transpose(0, 2, 1, 3).reshape(E, P, -1)
    consts, rope = shape_constants()
    arrays = {
        "x": g["L0_attn_x"],
        "consts": consts,
        "rope": rope,
        "wqkvg": np.concatenate([g[f"L0_attn_W{c}"] for c in "qkvg"], axis=1),
        "bqkvg": np.concatenate([g[f"L0_attn_b{c}"] for c in "qkvg"]),
        "wo": g["L0_attn_Wo"],
        "bo": g["L0_attn_bo"],
        "sc1": column(g["L0_attn_norm1_scale"]),
        "sc2": column(g["L0_attn_norm2_scale"]),
        "wr1": g["L0_attn_router_W"],
        "rb": g["L0_attn_router_b"],
        "w_moe": np.concatenate([w1, w2], axis=2),
        "b1": g["L0_attn_b1"].reshape(E * NF, P).T,
        "b2": g["L0_attn_b2"].reshape(-1),
        "sc_moe": np.concatenate([column(g["L0_attn_norm2_scale"]), np.zeros((P, KD), np.float32)], axis=1),
        "sc_ffn": np.concatenate([column(g["L0_ffn_ln_gamma"]), column(g["L0_ffn_ln_beta"])], axis=1),
        "wr2": g["L0_ffn_router_w"].T,
        "w_ffn": np.concatenate([w12, w3], axis=2),
    }
    arrays = {f"in_{k}": np.ascontiguousarray(v) for k, v in arrays.items()}
    nc = bacc.Bacc("TRN2", target_bir_lowering=False, num_devices=1)
    io = {k[3:]: nc.dram_tensor(k, v.shape, mybir.dt.from_np(v.dtype), kind="ExternalInput").ap() for k, v in arrays.items()}
    io["out"] = nc.dram_tensor("out_0", (BATCH, SEQ, D), F32, kind="ExternalOutput").ap()
    for name, rows in (("xn1", N), ("xn2", N), ("y1", SLOTS), ("y2", SLOTS)):
        io[name] = nc.dram_tensor(name, (rows, D), F32, kind="Internal").ap()
    build(nc, io)
    r = run_bass_kernel_spmd(nc, [arrays], core_ids=[0])
    return r.results[0]["out_0"]
```

```python
from contextlib import ExitStack

import numpy as np

import concourse.bass as bass
from concourse import mybir

F32 = mybir.dt.float32
F32R = mybir.dt.float32r
BF16 = mybir.dt.bfloat16
I32 = mybir.dt.int32
ALU = mybir.AluOpType
ACT = mybir.ActivationFunctionType
AX_X = mybir.AxisListType.X

P = 128
BATCH, SEQ, D = 2, 2048, 256
N = BATCH * SEQ
NT = N // P
TPB = NT // BATCH
KD = D // P
H, DK = 16, 16
HALF = DK // 2
CHUNK = 64
E = 8
HPH = P // DK
SW = P + HPH
HID = 1024
NF = HID // P
CAP = 1280
SLOTS = E * CAP
TILES_E = CAP // P
UW = 256
UPE = CAP // UW
UNITS = E * UPE
UT = UW // P
SC = E * TILES_E
EPS = 1e-5
CLAMP = 10000.0

C_ID, C_TRI, C_MASK = 0, P, 2 * P
C_IOTA = C_MASK + SW
C_REV = C_IOTA + P
C_ROW = C_REV + E
C_TOK = C_ROW + 1
C_N = C_TOK + 2 * NT


def shape_constants():
    c = np.zeros((P, C_N), np.float32)
    r = np.arange(P)
    c[:, C_ID:C_ID + P] = np.eye(P)
    c[:, C_TRI:C_TRI + P] = r[:, None] < r[None, :]
    c[:, C_MASK:C_MASK + P] = r[:, None] // DK == r[None, :] // DK
    c[:, C_MASK + P:C_MASK + SW] = r[:, None] // DK == np.arange(HPH)[None, :]
    c[:, C_IOTA:C_IOTA + P] = r[None, :]
    c[:, C_REV:C_REV + E] = E - np.arange(E)[None, :]
    c[:, C_ROW] = r
    c[:, C_TOK:C_N:2] = np.arange(NT)[None, :]
    c[:, C_TOK + 1:C_N:2] = r[:, None]
    half = np.arange(HALF, dtype=np.float32) / np.float32(HALF)
    inv = (np.float32(1.0) / np.power(np.float32(10000.0), half)).astype(np.float32)
    ang = (np.arange(SEQ, dtype=np.float32)[:, None] * inv[None, :]).astype(np.float32)
    cos, sin = np.cos(ang).astype(np.float32), np.sin(ang).astype(np.float32)
    rope = np.concatenate([cos, -sin, sin], axis=1).reshape(TPB, P, 3 * HALF).transpose(1, 0, 2)
    return c, np.ascontiguousarray(rope)


def after(eng, sem, count, passed=None):
    if isinstance(count, int) and count <= 0:
        return
    eng.wait_ge(sem, count)
    if passed is not None:
        eng.sem_inc(passed, 1)


LEAD = 2
LOOP_FROM = 4
LOOP_STEPS = (NT - LOOP_FROM - LEAD) // 2


class Tile:

    def __init__(self, n, b, i):
        self.n, self.b, self.i = n, b, i
        self.T = i + b * TPB


def fixed_tile(n):
    return Tile(n, n % 2, n // 2) if 0 <= n < NT else None


def run_tiles(eng, step, before_loop):
    for t in range(-LEAD, LOOP_FROM):
        step(lambda d: fixed_tile(t + d))
    before_loop()
    with eng.Fori(0, LOOP_STEPS) as j:
        for r in range(2):
            step(lambda d: Tile(j * 2 + (LOOP_FROM + r + d), (r + d) % 2, j + (LOOP_FROM + r + d) // 2))
    for t in range(LOOP_FROM + 2 * LOOP_STEPS, NT + LEAD):
        step(lambda d: fixed_tile(t + d))


def attention_phase(nc, bank, passed, io, X, cst, wraw):
    with ExitStack() as ctx:
        def sb(name, shape, dt=F32):
            return ctx.enter_context(nc.sbuf_tensor("A_" + name, shape, dt))

        def sem(name):
            return ctx.enter_context(nc.semaphore("A_" + name))

        wqkvg = sb("wqkvg", [P, KD, 4 * D])
        wsp = sb("wsp", [P, 2, KD, 4 * D], F32R)
        wo = sb("wo", [P, KD, D])
        wr = sb("wr", [P, KD, E])
        sc1 = sb("sc1", [P, KD])
        sc2 = sb("sc2", [P, KD])
        bqkvg = sb("bqkvg", [P, 4 * D])
        bo = sb("bo", [P, D])
        rope = sb("rope", [P, TPB, 3 * HALF])
        zeros = sb("zeros", [P, KD * SW])
        mhalf = sb("mhalf", [P, 1])
        junk = sb("junk", [P, 2, 2, D])
        ssq1, r1 = sb("ssq1", [P, 2]), sb("r1", [P, 2])
        ssq2, r2 = sb("ssq2", [P, 2]), sb("r2", [P, 2])
        xs = sb("xs", [P, 2, D])
        xT = sb("xT", [P, 2, 2, KD, P], F32R)
        qk = sb("qk", [P, 2 * D])
        ra = sb("ra", [P, 2 * D])
        rb = sb("rb", [P, 2 * D])
        rot = sb("rot", [P, 2, 2 * D])
        neg = sb("neg", [P, 2, 2 * D])
        phi = sb("phi", [P, 2, 2 * D])
        va = sb("va", [P, 2, KD, SW])
        gt = sb("gt", [P, 2, D])
        qT = sb("qT", [P, KD, P])
        sm = sb("sm", [P, 2, KD, SW])
        den = sb("den", [P, KD, HPH])
        rden = sb("rden", [P, KD, HPH])
        on = sb("on", [P, 2, D])
        og = sb("og", [P, 2, D])
        oT = sb("oT", [P, KD, P])
        xb = sb("xb", [P, 2, D])
        x1 = sb("x1", [P, 2, D])
        xn = sb("xn", [P, 2, D])
        xnT = sb("xnT", [P, KD, P])

        loads, xg = sem("loads"), [sem(f"xg{g}") for g in range(4)]
        s_w, s_wh, s_wl, s_cst = sem("w"), sem("wh"), sem("wl"), sem("cst")
        s_ssq1, s_r1, s_xs, s_tx, s_xT, s_xl = map(sem, ("ssq1", "r1", "xs", "tx", "xT", "xl"))
        s_pj0, s_pj1, s_qk, s_ra, s_rb, s_rot, s_vg = map(sem, ("pj0", "pj1", "qk", "ra", "rb", "rot", "vg"))
        s_mn, s_ex, s_phi, s_th, s_g = map(sem, ("mn", "ex", "phi", "th", "g"))
        s_tq, s_qT, s_sa, s_mk, s_num = map(sem, ("tq", "qT", "sa", "mk", "num"))
        s_den, s_rden, s_on, s_og = map(sem, ("den", "rden", "on", "og"))
        s_to, s_oT, s_wo, s_xb, s_x1, s_xacc = map(sem, ("to", "oT", "wo", "xb", "x1", "xacc"))
        s_ssq2, s_r2, s_xn, s_tr, s_xnT, s_rt = map(sem, ("ssq2", "r2", "xn", "tr", "xnT", "rt"))
        s_st, s_wst = [sem(f"st{b}") for b in range(2)], sem("wst")
        s_pass, s_pass_act = passed["pool"], passed["act"]

        ident = cst[:, C_ID:C_ID + P]
        hmask = cst[:, C_MASK:C_MASK + SW].unsqueeze(1).to_broadcast([P, KD, SW])
        b_tx, b_tq, b_tor, b_num, b_p0, b_p1 = bank[0:6]
        b_s = bank[6:8]
        tx_ps = b_tx[:, 0:D].rearrange("p (k t) -> p k t", k=KD)
        tq_ps = b_tq[:, 0:D].rearrange("p (k t) -> p k t", k=KD)
        wo_ps = b_tq[:, 0:D]
        to_ps = b_tor[:, 0:D].rearrange("p (k t) -> p k t", k=KD)
        tr_ps = b_tor[:, D:2 * D].rearrange("p (k t) -> p k t", k=KD)
        num_ps = b_num[:, 0:KD * SW].rearrange("p (k c) -> p k c", k=KD)
        s_ps = [b[:, 0:KD * SW].rearrange("p (k c) -> p k c", k=KD) for b in b_s]

        def halves(ap):
            return ap.rearrange("p (h a d) -> p h a d", a=2, d=HALF)

        block = ctx.enter_context(nc.Block())

        @block.sync
        def _(sp):
            xv = io["x"].rearrange("b (i p) d -> p b i d", p=P)
            Xv = X[:, :, :].rearrange("p (b i) d -> p b i d", b=BATCH)
            g = TPB // 4
            sp.dma_start(cst[:, :], io["consts"]).then_inc(loads, 16)
            for b in range(BATCH):
                sp.dma_start(Xv[:, b, 0:g, :], xv[:, b, 0:g, :]).then_inc(xg[0], 16)
            sp.dma_start(wqkvg[:, :, :], io["wqkvg"].rearrange("(k p) n -> p k n", p=P)).then_inc(loads, 16)
            sp.dma_start(sc1[:, :], io["sc1"]).then_inc(loads, 16)
            sp.dma_start(sc2[:, :], io["sc2"]).then_inc(loads, 16)
            sp.dma_start(bqkvg[:, :], io["bqkvg"].partition_broadcast(P)).then_inc(loads, 16)
            sp.dma_start(bo[:, :], io["bo"].partition_broadcast(P)).then_inc(loads, 16)
            sp.dma_start(rope[:, :, :], io["rope"]).then_inc(loads, 16)
            sp.dma_start(wo[:, :, :], io["wo"].rearrange("(k p) n -> p k n", p=P)).then_inc(loads, 16)
            sp.dma_start(wr[:, :, :], io["wr1"].rearrange("(k p) n -> p k n", p=P)).then_inc(loads, 16)
            for q in range(1, 4):
                for b in range(BATCH):
                    sp.dma_start(Xv[:, b, q * g:q * g + g, :], xv[:, b, q * g:q * g + g, :]).then_inc(xg[q], 16)
            sp.dma_start(wraw[:, 0:4 * HID], io["w_moe"][0]).then_inc(s_wst, 16)

            def step(at):
                if (t := at(-2)) is not None:
                    after(sp, s_xn, t.n + 1)
                    sp.dma_start(io["xn1"][bass.ts(t.T, P), :], xn[:, t.b, :]).then_inc(s_st[t.b], 16)
            run_tiles(sp, step, lambda: None)
            for b in range(BATCH):
                sp.wait_ge(s_st[b], 16 * TPB)
            sp.wait_ge(s_wst, 16)

        @block.gpsimd
        def _(pool):
            nc.gpsimd.memset(mhalf[:, :], -0.5).then_inc(s_cst, 1)
            nc.gpsimd.memset(zeros[:, :], 0.0).then_inc(s_cst, 1)
            nc.gpsimd.memset(va[:, :, :, :], 1.0).then_inc(s_cst, 1)
            pool.wait_ge(s_cst, 3)
            pool.wait_ge(loads, 16 * 9)
            pool.wait_ge(xg[0], 32)

            def step(at):
                if (t := at(-2)) is not None:
                    after(pool, s_ssq2, t.n + 1, s_pass)
                    after(pool, s_xn, t.n - 1, s_pass)
                    nc.gpsimd.tensor_tensor(r2[:, t.b:t.b + 1], ssq2[:, t.b:t.b + 1], mhalf[:, :], ALU.pow).then_inc(s_r2, 1)
                if (t := at(2)) is not None:
                    after(pool, s_ssq1, t.n + 1, s_pass)
                    after(pool, s_xs, t.n - 1, s_pass)
                    nc.gpsimd.tensor_tensor(r1[:, t.b:t.b + 1], ssq1[:, t.b:t.b + 1], mhalf[:, :], ALU.pow).then_inc(s_r1, 1)
                if (t := at(1)) is not None:
                    after(pool, s_qk, t.n + 1, s_pass)
                    after(pool, s_rot, t.n, s_pass)
                    for a in range(2):
                        sn = rope[:, t.i, HALF + a * HALF:HALF + (a + 1) * HALF]
                        nc.gpsimd.tensor_tensor(halves(rb[:, :])[:, :, a, :], halves(qk[:, :])[:, :, 1 - a, :],
                                                sn.unsqueeze(1).to_broadcast([P, 2 * H, HALF]), ALU.mult).then_inc(s_rb, 1)
                if (t := at(-1)) is not None:
                    after(pool, s_x1, t.n - 1, s_pass)
                    nc.gpsimd.tensor_tensor(xb[:, t.b, :], X[:, t.T, :], bo[:, :], ALU.add).then_inc(s_xb, 1)
                if (t := at(1)) is not None:
                    after(pool, s_th, t.n + 1, s_pass)
                    nc.gpsimd.tensor_scalar(gt[:, t.b, :], gt[:, t.b, :], 0.5, 0.5, ALU.mult, ALU.add).then_inc(s_g, 1)
                if (t := at(0)) is not None:
                    after(pool, s_g, t.n + 1, s_pass)
                    after(pool, s_on, t.n + 1, s_pass)
                    after(pool, s_to, t.n - 1, s_pass)
                    nc.gpsimd.tensor_tensor(og[:, t.b, :], on[:, t.b, :], gt[:, t.b, :], ALU.mult).then_inc(s_og, 1)
                if (t := at(-1)) is not None:
                    after(pool, s_xb, t.n + 1, s_pass)
                    after(pool, s_x1, t.n + 1, s_pass)
                    nc.gpsimd.tensor_tensor(X[:, t.T, :], X[:, t.T, :], x1[:, t.b, :], ALU.add).then_inc(s_xacc, 1)

            def all_x():
                for q in range(1, 4):
                    pool.wait_ge(xg[q], 32)
            run_tiles(pool, step, all_x)

        @block.scalar
        def _(act):
            for k in range(KD):
                act.wait_ge(s_w, k + 1)
                nc.scalar.activation(wsp[:, 0, k, :], wqkvg[:, k, :], ACT.Copy).then_inc(s_wh, 1)
            act.wait_ge(xg[0], 32)

            def step(at):
                if (t := at(0)) is not None:
                    after(act, s_tq, t.n + 1)
                    after(act, s_num, t.n)
                    nc.scalar.activation(qT[:, :, :], tq_ps, ACT.Copy).then_inc(s_qT, 1)
                if (t := at(-2)) is not None:
                    after(act, s_x1, t.n + 1)
                    after(act, s_r2, t.n - 1)
                    nc.scalar.activation(junk[:, 0, t.b, :], x1[:, t.b, :], ACT.Square, scale=float(D) ** -0.5,
                                         accum_out=ssq2[:, t.b:t.b + 1]).then_inc(s_ssq2, 1)
                if (t := at(2)) is not None:
                    after(act, s_r1, t.n - 1)
                    nc.scalar.activation(junk[:, 1, t.b, :], X[:, t.T, :], ACT.Square, scale=float(D) ** -0.5,
                                         accum_out=ssq1[:, t.b:t.b + 1]).then_inc(s_ssq1, 1)
                if (t := at(-2)) is not None:
                    after(act, s_r2, t.n + 1)
                    after(act, s_st[t.b], t.i * 16)
                    after(act, s_tr, t.n - 1)
                    nc.scalar.activation(xn[:, t.b, :], x1[:, t.b, :], ACT.Copy, scale=r2[:, t.b:t.b + 1]).then_inc(s_xn, 1)
                if (t := at(2)) is not None:
                    after(act, s_r1, t.n + 1)
                    after(act, s_tx, t.n - 1, s_pass_act)
                    nc.scalar.activation(xs[:, t.b, :], X[:, t.T, :], ACT.Copy, scale=r1[:, t.b:t.b + 1]).then_inc(s_xs, 1)
                o, r = at(-1), at(-2)
                if o is not None:
                    after(act, s_to, o.n + 1)
                if r is not None:
                    after(act, s_tr, r.n + 1)
                if o is not None:
                    after(act, s_wo, o.n)
                    nc.scalar.activation(oT[:, :, :], to_ps, ACT.Copy).then_inc(s_oT, 1)
                if r is not None:
                    after(act, s_rt, r.n)
                    nc.scalar.activation(xnT[:, :, :], tr_ps, ACT.Copy).then_inc(s_xnT, 1)
                if (t := at(2)) is not None:
                    after(act, s_tx, t.n + 1)
                    after(act, s_pj1, t.n - 1)
                    after(act, s_xl, t.n - 1)
                    nc.scalar.activation(xT[:, t.b, 0, :, :], tx_ps, ACT.Copy).then_inc(s_xT, 1)
                if (t := at(1)) is not None:
                    after(act, s_vg, 2 * t.n + 2)
                    nc.scalar.activation(gt[:, t.b, :], gt[:, t.b, :], ACT.Tanh, scale=0.5).then_inc(s_th, 1)
                    after(act, s_mn, t.n + 1)
                    nc.scalar.activation(neg[:, t.b, :], neg[:, t.b, :], ACT.Exp).then_inc(s_ex, 1)

            def all_x():
                for q in range(1, 4):
                    act.wait_ge(xg[q], 32)
            run_tiles(act, step, all_x)

        @block.vector
        def _(dve):
            dve.wait_ge(loads, 16 * 9)
            for k in range(KD):
                nc.vector.tensor_scalar(wqkvg[:, k, :], wqkvg[:, k, :], sc1[:, k:k + 1], None, ALU.mult).then_inc(s_w, 1)
            for k in range(KD):
                nc.vector.tensor_scalar(wr[:, k, :], wr[:, k, :], sc2[:, k:k + 1], None, ALU.mult).then_inc(s_w, 1)
            for k in range(KD):
                dve.wait_ge(s_wh, k + 1)
                nc.vector.tensor_tensor(wsp[:, 1, k, :], wqkvg[:, k, :], wsp[:, 0, k, :].bitcast(F32), ALU.subtract).then_inc(s_wl, 1)
            dve.wait_ge(s_cst, 3)

            def mask(t, c):
                after(dve, s_num, t.n)
                after(dve, s_sa, 2 * t.n + c + 1)
                nc.vector.tensor_tensor(sm[:, c, :, :], s_ps[t.b], hmask, ALU.mult).then_inc(s_mk, 1)

            def step(at):
                if (t := at(0)) is not None:
                    mask(t, 0)
                if (t := at(1)) is not None:
                    after(dve, s_pj0, t.n + 1)
                    after(dve, s_rb, 2 * t.n)
                    nc.vector.tensor_tensor(qk[:, :], b_p0[:, :], bqkvg[:, 0:2 * D], ALU.add).then_inc(s_qk, 1)
                    after(dve, s_qk, t.n + 1)
                    cs = rope[:, t.i, 0:HALF].unsqueeze(1).to_broadcast([P, 4 * H, HALF])
                    nc.vector.tensor_tensor(ra[:, :].rearrange("p (h d) -> p h d", d=HALF),
                                            qk[:, :].rearrange("p (h d) -> p h d", d=HALF), cs, ALU.mult).then_inc(s_ra, 1)
                if (t := at(0)) is not None:
                    mask(t, 1)
                if (t := at(1)) is not None:
                    after(dve, s_pj1, t.n + 1)
                    after(dve, s_sa, 2 * t.n - 2)
                    nc.vector.tensor_tensor(va[:, t.b, :, 0:P], b_p1[:, 0:D].rearrange("p (k c) -> p k c", k=KD),
                                            bqkvg[:, 2 * D:3 * D].rearrange("p (k c) -> p k c", k=KD), ALU.add).then_inc(s_vg, 1)
                    after(dve, s_og, t.n - 1)
                    nc.vector.tensor_tensor(gt[:, t.b, :], b_p1[:, D:2 * D], bqkvg[:, 3 * D:4 * D], ALU.add).then_inc(s_vg, 1)
                    after(dve, s_rb, 2 * t.n + 2)
                    after(dve, s_ra, t.n + 1)
                    nc.vector.tensor_tensor(rot[:, t.b, :], ra[:, :], rb[:, :], ALU.add).then_inc(s_rot, 1)
                    after(dve, s_rot, t.n + 1)
                    nc.vector.tensor_scalar(neg[:, t.b, :], rot[:, t.b, :], 0.0, None, ALU.min).then_inc(s_mn, 1)
                if (t := at(0)) is not None:
                    after(dve, s_num, t.n + 1)
                    nc.vector.tensor_scalar(den[:, :, :], num_ps[:, :, P:SW], 1e-6, None, ALU.add).then_inc(s_den, 1)
                    after(dve, s_den, t.n + 1)
                    after(dve, s_on, t.n)
                    nc.vector.reciprocal(rden[:, :, :], den[:, :, :]).then_inc(s_rden, 1)
                if (t := at(2)) is not None:
                    after(dve, s_xT, t.n + 1)
                    after(dve, s_pj1, t.n - 1)
                    nc.vector.tensor_tensor(xT[:, t.b, 1, :, :], tx_ps, xT[:, t.b, 0, :, :].bitcast(F32), ALU.subtract).then_inc(s_xl, 1)
                if (t := at(0)) is not None:
                    after(dve, s_rden, t.n + 1)
                    after(dve, s_og, t.n - 1)
                    for k in range(KD):
                        ins = nc.vector.tensor_tensor(
                            on[:, t.b, k * P:(k + 1) * P].rearrange("p (h d) -> p h d", d=DK),
                            num_ps[:, k, 0:P].rearrange("p (h d) -> p h d", d=DK),
                            rden[:, k, :].unsqueeze(2).to_broadcast([P, HPH, DK]), ALU.mult)
                        if k == KD - 1:
                            ins.then_inc(s_on, 1)
                if (t := at(1)) is not None:
                    after(dve, s_ex, t.n + 1)
                    after(dve, s_sa, 2 * t.n - 2)
                    after(dve, s_tq, t.n - 1)
                    nc.vector.scalar_tensor_tensor(out=phi[:, t.b, :], in0=rot[:, t.b, :], scalar=0.0, in1=neg[:, t.b, :],
                                                   op0=ALU.max, op1=ALU.add).then_inc(s_phi, 1)
                if (t := at(-1)) is not None:
                    after(dve, s_wo, t.n + 1)
                    after(dve, s_xb, t.n + 1)
                    after(dve, s_xacc, t.n - 1)
                    after(dve, s_ssq2, t.n - 1)
                    after(dve, s_xn, t.n - 1)
                    nc.vector.tensor_tensor(x1[:, t.b, :], wo_ps, xb[:, t.b, :], ALU.add).then_inc(s_x1, 1)
            run_tiles(dve, step, lambda: None)

        @block.tensor
        def _(pe):
            pe.wait_ge(loads, 16 * 9)
            pe.wait_ge(s_cst, 3)
            for b in range(BATCH):
                nc.tensor.matmul(b_s[b][:, 0:KD * SW], zeros[:, 0:P], zeros[:, :], start=True, stop=True)

            def add_chunk(t, c):
                rows = slice(c * CHUNK, (c + 1) * CHUNK)
                for k in range(KD):
                    ins = nc.tensor.matmul(s_ps[t.b][:, k, :], phi[rows, t.b, D + k * P:D + (k + 1) * P],
                                           va[rows, t.b, k, :], start=False, stop=True, skip_group_check=True)
                ins.then_inc(s_sa, 1)

            def project(t, part, b_p, done):
                for k in range(KD):
                    for m, (a, b) in enumerate(((0, 0), (0, 1), (1, 0))):
                        ins = nc.tensor.matmul(b_p[:, :], xT[:, t.b, a, k, :], wsp[:, b, k, part * 2 * D:(part + 1) * 2 * D],
                                               start=(k == 0 and m == 0), stop=(k == KD - 1 and m == 2))
                ins.then_inc(done, 1)

            def step(at):
                if (t := at(0)) is not None:
                    after(pe, s_phi, t.n + 1)
                    after(pe, s_x1, t.n - 1)
                    for k in range(KD):
                        ins = nc.tensor.transpose(tq_ps[:, k, :], phi[:, t.b, k * P:(k + 1) * P], ident)
                    ins.then_inc(s_tq, 1)
                    after(pe, s_mk, 2 * t.n - 2)
                    add_chunk(t, 0)
                if (t := at(1)) is not None:
                    if isinstance(t.n, int) and t.n == 0:
                        pe.wait_ge(s_wl, KD)
                    after(pe, s_xl, t.n + 1)
                    after(pe, s_qk, t.n)
                    project(t, 0, b_p0, s_pj0)
                if (t := at(0)) is not None:
                    after(pe, s_mk, 2 * t.n + 1)
                    add_chunk(t, 1)
                if (t := at(1)) is not None:
                    after(pe, s_vg, 2 * t.n)
                    project(t, 1, b_p1, s_pj1)
                o, r = at(-1), at(-2)
                if o is not None:
                    after(pe, s_og, o.n + 1)
                    after(pe, s_oT, o.n)
                    after(pe, s_xnT, o.n - 1)
                    for k in range(KD):
                        ins = nc.tensor.transpose(to_ps[:, k, :], og[:, o.b, k * P:(k + 1) * P], ident)
                    ins.then_inc(s_to, 1)
                if r is not None:
                    after(pe, s_xn, r.n + 1)
                    after(pe, s_oT, r.n + 1)
                    after(pe, s_xnT, r.n)
                    for k in range(KD):
                        ins = nc.tensor.transpose(tr_ps[:, k, :], xn[:, r.b, k * P:(k + 1) * P], ident)
                    ins.then_inc(s_tr, 1)
                if (t := at(2)) is not None:
                    after(pe, s_xs, t.n + 1)
                    after(pe, s_xl, t.n)
                    for k in range(KD):
                        ins = nc.tensor.transpose(tx_ps[:, k, :], xs[:, t.b, k * P:(k + 1) * P], ident)
                    ins.then_inc(s_tx, 1)
                if (t := at(0)) is not None:
                    after(pe, s_qT, t.n + 1)
                    after(pe, s_on, t.n)
                    for c in range(2):
                        after(pe, s_mk, 2 * t.n + c + 1)
                        rows = slice(c * CHUNK, (c + 1) * CHUNK)
                        for k in range(KD):
                            ins = nc.tensor.matmul(num_ps[rows, k, :], qT[:, k, rows], sm[:, c, k, :], start=True, stop=True)
                    ins.then_inc(s_num, 1)
                if (t := at(-1)) is not None:
                    after(pe, s_oT, t.n + 1)
                    after(pe, s_qT, min(t.n + 2, NT) if isinstance(t.n, int) else t.n + 2)
                    after(pe, s_x1, t.n)
                    for k in range(KD):
                        ins = nc.tensor.matmul(wo_ps, oT[:, k, :], wo[:, k, :], start=(k == 0), stop=(k == KD - 1))
                    ins.then_inc(s_wo, 1)
                if (t := at(-2)) is not None:
                    if isinstance(t.n, int) and t.n == 0:
                        pe.wait_ge(s_w, 2 * KD)
                    after(pe, s_xnT, t.n + 1)
                    after(pe, s_xl, min(t.n + 5, NT) if isinstance(t.n, int) else t.n + 5)
                    for k in range(KD):
                        ins = nc.tensor.matmul(b_tx[:, bass.ds(t.T * E + D, E)], xnT[:, k, :], wr[:, k, :],
                                               start=(k == 0), stop=(k == KD - 1))
                    ins.then_inc(s_rt, 1)
            run_tiles(pe, step, lambda: None)


def routing_phase(nc, bank, io, tag, first, LG, GATE, GI, IDX, cst, wraw, ws0, qw):
    with ExitStack() as ctx:
        def sb(name, shape, dt=F32):
            return ctx.enter_context(nc.sbuf_tensor(f"{tag}_{name}", shape, dt))

        def sem(name):
            return ctx.enter_context(nc.semaphore(f"{tag}_{name}"))

        rb = sb("rb", [P, E])
        best = sb("best", [P, 2, NT])
        eq = sb("eq", [P, NT, E])
        rev = sb("rev", [P, 2, NT])
        oh = sb("oh", [P, 2, NT, E])
        ohr = sb("ohr", [P, 2, NT, E])
        sel = sb("sel", [P, NT, E], BF16)
        tri = sb("tri", [P, P], BF16)
        ones = sb("ones", [P, P], BF16)
        onef = sb("onef", [P, NT])
        iota = sb("iota", [P, P], BF16)
        zero = sb("zero", [P, 2 * SC], BF16)
        tot = sb("tot", [P, NT, E])
        cum = sb("cum", [P, NT, E])
        rank = sb("rank", [P, NT, E])
        rk = sb("rk", [P, 2, NT])
        kept = sb("kept", [P, 2, NT])
        slot = sb("slot", [P, 2, NT])
        inv = sb("inv", [P, 2, NT])
        invi = sb("invi", [P, 2, NT], I32)
        pci = sb("pci", [P, 2, 2, NT], I32)
        pcf = sb("pcf", [P, 2, 2, NT])
        dl = sb("dl", [P, NT])
        ex = sb("ex", [P, 2, NT])
        den = sb("den", [P, NT])
        rg = sb("rg", [P, NT])
        row1h = sb("row1h", [P, 4, P], BF16)
        col1h = sb("col1h", [P, 4, 2, SC], BF16)
        tok = sb("tok", [P, SC])

        s_ld, s_v, s_ex, s_exin, s_sel, s_rank, s_z = map(sem, ("ld", "v", "ex", "exin", "sel", "rank", "z"))
        s_1h, s_inv, s_set, s_hi = map(sem, ("1h", "inv", "set", "hi"))
        s_pc = sem("pc")
        lg_ps = bank[0][:, D:D + NT * E].rearrange("p (t e) -> p t e", e=E)
        rank_ps = bank[3][:, 0:NT * E].rearrange("p (t e) -> p t e", e=E)
        tot_ps = bank[1][:, 0:NT * E].rearrange("p (t e) -> p t e", e=E)
        tok_ps = bank[2][:, 0:2 * SC].rearrange("p (a c) -> p a c", a=2)
        iota2 = iota[:, 0:SC].unsqueeze(1).to_broadcast([P, 2, SC])
        revc = cst[:, C_REV:C_REV + E].unsqueeze(1).to_broadcast([P, NT, E])

        def over_e(ap):
            return ap.unsqueeze(2).to_broadcast([P, NT, E])

        block = ctx.enter_context(nc.Block())

        @block.sync
        def _(sp):
            if first:
                sp.dma_start(rb[:, :], io["rb"].partition_broadcast(P)).then_inc(s_ld, 16)
                sp.wait_ge(s_ld, 16)

        @block.scalar
        def _(act):
            for q in range(4):
                nc.scalar.activation(ws0[:, 0, q * qw:(q + 1) * qw], wraw[:, q * qw:(q + 1) * qw], ACT.Copy).then_inc(s_hi, 1)
                if q == 1:
                    act.wait_ge(s_exin, 1)
                    nc.scalar.activation(ex[:, 1, :], dl[:, :], ACT.Exp).then_inc(s_ex, 1)

        @block.gpsimd
        def _(pool):
            nc.gpsimd.memset(zero[:, :], 0.0).then_inc(s_set, 1)
            nc.gpsimd.memset(ones[:, :], 1.0).then_inc(s_set, 1)
            nc.gpsimd.memset(onef[:, :], 1.0).then_inc(s_set, 1)
            nc.gpsimd.tensor_copy(tri[:, :], cst[:, C_TRI:C_TRI + P]).then_inc(s_set, 1)
            nc.gpsimd.tensor_copy(iota[:, :], cst[:, C_IOTA:C_IOTA + P]).then_inc(s_set, 1)
            for q in range(4):
                pool.wait_ge(s_hi, q + 1)
                nc.gpsimd.tensor_tensor(ws0[:, 1, q * qw:(q + 1) * qw], wraw[:, q * qw:(q + 1) * qw],
                                        ws0[:, 0, q * qw:(q + 1) * qw].bitcast(F32), ALU.subtract)

        @block.vector
        def _(dve):
            done = [0]

            def chain(ins):
                done[0] += 1
                ins.then_inc(s_v, 1)
                dve.wait_ge(s_v, done[0])

            V = nc.vector
            if first:
                dve.wait_ge(s_ld, 16)
                chain(V.tensor_tensor(LG[:, :, :], lg_ps, rb[:, :].unsqueeze(1).to_broadcast([P, NT, E]), ALU.add))
            else:
                chain(V.tensor_scalar(LG[:, :, :], lg_ps, CLAMP, -CLAMP, ALU.min, ALU.max))
            for c in range(2):
                chain(V.tensor_reduce(best[:, c, :], LG[:, :, :], AX_X, ALU.max))
                chain(V.tensor_tensor(eq[:, :, :], LG[:, :, :], over_e(best[:, c, :]), ALU.is_equal))
                chain(V.tensor_tensor(eq[:, :, :], eq[:, :, :], revc, ALU.mult))
                chain(V.tensor_reduce(rev[:, c, :], eq[:, :, :], AX_X, ALU.max))
                chain(V.tensor_tensor(oh[:, c, :, :], revc, over_e(rev[:, c, :]), ALU.is_equal))
                if c == 0:
                    chain(V.scalar_tensor_tensor(out=LG[:, :, :], in0=oh[:, 0, :, :], scalar=-3e38, in1=LG[:, :, :],
                                                 op0=ALU.mult, op1=ALU.add))
            V.tensor_tensor(dl[:, :], best[:, 1, :], best[:, 0, :], ALU.subtract).then_inc(s_exin, 1)
            V.tensor_tensor(sel[:, :, :], oh[:, 0, :, :], oh[:, 1, :, :], ALU.add).then_inc(s_sel, 1)
            dve.wait_ge(s_set, 5)
            dve.wait_ge(s_rank, 2)
            chain(V.tensor_copy(tot[:, :, :], tot_ps))
            for e in range(E):
                ins = V.tensor_tensor_scan(cum[:, :, e], onef[:, :], tot[:, :, e], 0.0, ALU.mult, ALU.add)
                if e == E - 1:
                    chain(ins)
            chain(V.tensor_tensor(cum[:, :, :], cum[:, :, :], tot[:, :, :], ALU.subtract))
            chain(V.tensor_tensor(rank[:, :, :], rank_ps, cum[:, :, :], ALU.add))
            for c in range(2):
                ins = V.tensor_tensor(ohr[:, c, :, :], oh[:, c, :, :], rank[:, :, :], ALU.mult)
            chain(ins)
            chain(V.tensor_reduce(rk[:, :, :], ohr[:, :, :, :], AX_X, ALU.add))
            V.tensor_scalar(kept[:, :, :], rk[:, :, :], float(CAP), None, ALU.is_lt)
            chain(V.tensor_scalar(slot[:, :, :], rev[:, :, :], -float(CAP), float(SLOTS), ALU.mult, ALU.add))
            chain(V.tensor_tensor(slot[:, :, :], slot[:, :, :], rk[:, :, :], ALU.add))
            V.tensor_scalar(GI[:, :, :].rearrange("p t c -> p c t"), slot[:, :, :], float(SLOTS - 1), None, ALU.min)
            chain(V.scalar_tensor_tensor(out=inv[:, :, :], in0=kept[:, :, :], scalar=-16384.0, in1=slot[:, :, :],
                                         op0=ALU.mult, op1=ALU.add))
            chain(V.tensor_scalar(invi[:, :, :], inv[:, :, :], 16384.0, None, ALU.add))
            V.tensor_scalar(pci[:, 0, :, :], invi[:, :, :], P - 1, None, ALU.bitwise_and)
            chain(V.tensor_scalar(pci[:, 1, :, :], invi[:, :, :], 7, None, ALU.logical_shift_right))
            V.tensor_copy(pcf[:, :, :, :], pci[:, :, :, :]).then_inc(s_pc, 1)
            dve.wait_ge(s_ex, 1)
            chain(V.tensor_scalar(den[:, :], ex[:, 1, :], 1.0, 0.0 if first else 1e-12, ALU.add, ALU.add))
            chain(V.reciprocal(rg[:, :], den[:, :]))
            V.tensor_tensor(GATE[:, :, 0], rg[:, :], kept[:, 0, :], ALU.mult)
            chain(V.tensor_tensor(ex[:, 0, :], ex[:, 1, :], kept[:, 1, :], ALU.mult))
            chain(V.tensor_tensor(GATE[:, :, 1], ex[:, 0, :], rg[:, :], ALU.mult))
            dve.wait_ge(s_pc, 1)
            with dve.Fori(0, NT // 2) as j:
                for r in range(2):
                    T = j * 2 + r
                    for c in range(2):
                        g = 2 * r + c
                        if g == 0:
                            dve.wait_ge(s_inv, j * 4 + 4)
                        V.scalar_tensor_tensor(out=col1h[:, g, :, :], in0=iota2, scalar=pcf[:, 1, c, bass.ds(T, 1)],
                                               in1=cst[:, bass.ds(T * 2 + C_TOK, 2)].unsqueeze(2).to_broadcast([P, 2, SC]),
                                               op0=ALU.is_equal, op1=ALU.mult).then_inc(s_1h, 1)
                        V.tensor_scalar(row1h[:, g, :], iota[:, :], pcf[:, 0, c, bass.ds(T, 1)], None,
                                        ALU.is_equal).then_inc(s_1h, 1)
            dve.wait_ge(s_inv, 2 * NT + 4)
            chain(V.tensor_scalar(tok[:, :], tok_ps[:, 0, :], float(P), None, ALU.mult))
            chain(V.tensor_tensor(IDX[:, :], tok_ps[:, 1, :], tok[:, :], ALU.add))

        @block.tensor
        def _(pe):
            pe.wait_ge(s_set, 5)
            pe.wait_ge(s_sel, 1)
            cols = sel[:, :, :].rearrange("p t e -> p (t e)")
            nc.tensor.matmul(bank[3][:, 0:NT * E], tri[:, :], cols, start=True, stop=True).then_inc(s_rank, 1)
            nc.tensor.matmul(bank[1][:, 0:NT * E], ones[:, :], cols, start=True, stop=True).then_inc(s_rank, 1)
            nc.tensor.matmul(bank[2][:, 0:2 * SC], ones[:, :], zero[:, :], start=True, stop=True)
            pe.sem_inc(s_inv, 4)
            with pe.Fori(0, NT // 2) as j:
                for g in range(4):
                    pe.wait_ge(s_1h, j * 8 + 2 * g + 2)
                    nc.tensor.matmul(bank[2][:, 0:2 * SC], row1h[:, g, :], col1h[:, g, :, :].rearrange("p a c -> p (a c)"),
                                     start=False, stop=True, skip_group_check=True).then_inc(s_inv, 1)


def expert_phase(nc, bank, passed, io, tag, glu, IDX, xn_dram, y_dram, w_dram, sc_dram, cst, wraw, ws):
    qw = 1536 if glu else 1024
    w2_at = 4096 if glu else 2048
    with ExitStack() as ctx:
        def sb(name, shape, dt=F32):
            return ctx.enter_context(nc.sbuf_tensor(f"{tag}_{name}", shape, dt))

        def sem(name):
            return ctx.enter_context(nc.semaphore(f"{tag}_{name}"))

        xg = sb("xg", [P, UT, D])
        ist = sb("ist", [P, UT], I32)
        xraw = sb("xraw", [P, KD, UW])
        xT = sb("xT", [P, 2, KD, UW], F32R)
        hT = sb("hT", [P, 2, NF, UW], F32R)
        hraw = sb("hraw", [P, 4, UW])
        sg = sb("sg", [P, 4, UW]) if glu else None
        ysb = sb("ysb", [P, UT, D])
        scb = sb("scb", [P, 2 * KD])
        warm = sb("warm", [P, 1])
        b1 = None if glu else sb("b1", [P, E * NF])
        b2 = None if glu else sb("b2", [P, E, D])

        s_ld, s_gi, s_gx, s_tg, s_xr, s_xh, s_xl = map(sem, ("ld", "gi", "gx", "tg", "xr", "xh", "xl"))
        s_hd, s_sg, s_hm, s_hh, s_hl = map(sem, ("hd", "sg", "hm", "hh", "hl"))
        s_y, s_ye, s_ys, s_wld, s_wh, s_wl = map(sem, ("y", "ye", "ys", "wld", "wh", "wl"))
        s_pass, s_pass_pe = passed["pool"], passed["pe"]
        RING = 4
        s_free = s_hm if glu else s_sg
        b_y, b_t = bank[4:6], bank[6]
        t_ps = b_t[:, :].rearrange("p (k n) -> p k n", k=KD)
        ident = cst[:, C_ID:C_ID + P]

        def experts(eng, unit, at_expert=None):
            def one(e, s, last):
                if at_expert:
                    at_expert(e, s, last)
                with eng.Fori(0, UPE - 1) as c:
                    unit(e, c, e * UPE + c, s, not last, True)
                unit(e, UPE - 1, e * UPE + (UPE - 1), s, False, not last)
            with eng.Fori(0, E // 2 - 1) as ee:
                for s in range(2):
                    one(ee * 2 + s, s, False)
            one(E - 2, 0, False)
            one(E - 1, 1, True)

        block = ctx.enter_context(nc.Block())

        @block.sync
        def _(sp):
            sp.dma_start(scb[:, :], sc_dram).then_inc(s_ld, 16)
            if not glu:
                sp.dma_start(b1[:, :], io["b1"]).then_inc(s_ld, 16)
                sp.dma_start(b2[:, :, :].rearrange("p e d -> p (e d)"), io["b2"].partition_broadcast(P)).then_inc(s_ld, 16)

            def next_weights(e, s, last):
                if not last:
                    sp.wait_ge(s_wl, e * 4 + 4)
                    sp.dma_start(wraw[:, 0:4 * qw], w_dram[bass.ds(e + 1, 1)].rearrange("a p n -> p (a n)")).then_inc(s_wld, 16)

            def unit(e, c, u, s, prefetch, more):
                sp.wait_ge(s_ye, u * UT + 2 * UT)
                sp.dma_start(y_dram[bass.ds(u * UW, UW), :].rearrange("(j p) d -> p j d", p=P), ysb[:, :, :]).then_inc(s_ys, 16)
            sp.sem_inc(s_ys, 16)
            experts(sp, unit, next_weights)
            sp.wait_ge(s_ys, 16 * UNITS + 16)

        @block.gpsimd
        def _(pool):
            def gather(u, n):
                nc.gpsimd.tensor_copy(ist[:, :], IDX[:, bass.ds(u * UT, UT)]).then_inc(s_gi, 1)
                after(pool, s_gi, n, s_pass)
                for j in range(UT):
                    nc.gpsimd.indirect_dma_start(
                        out=xg[:, j, :], out_offset=None, in_=xn_dram,
                        in_offset=bass.IndirectOffsetOnAxis(ap=ist[:, j:j + 1], axis=0)).then_inc(s_gx, 16)

            def unit(e, c, u, s, prefetch, more):
                if more:
                    after(pool, s_tg, u + 1, s_pass)
                    gather(u + 1, u + 2)
            gather(0, 1)
            experts(pool, unit)

        @block.scalar
        def _(act):
            def raw_rows():
                for k in range(KD):
                    nc.scalar.activation(xraw[:, k, :], t_ps[:, k, :], ACT.Identity, scale=scb[:, k:k + 1],
                                         bias=scb[:, KD + k:KD + k + 1]).then_inc(s_xr, 1)

            nc.scalar.activation(warm[:, :], cst[:, C_ROW:C_ROW + 1], ACT.Silu if glu else ACT.Gelu)
            act.sem_inc(s_sg, RING)
            if glu:
                act.sem_inc(s_ye, UT)
            act.wait_ge(s_ld, 16 * (1 if glu else 3))
            act.wait_ge(s_tg, 1)
            raw_rows()

            def unit(e, c, u, s, prefetch, more):
                for f in range(NF):
                    g = u * NF + f
                    act.wait_ge(s_hd, g + 1)
                    ps = bank[f % RING]
                    if glu:
                        act.wait_ge(s_hm, g + 1)
                        nc.scalar.activation(sg[:, f % RING, :], ps[:, 0:UW], ACT.Silu).then_inc(s_sg, 1)
                    else:
                        act.wait_ge(s_hl, g + 1)
                        nc.scalar.activation(hraw[:, f % RING, :], ps[:, 0:UW], ACT.Gelu,
                                             bias=b1[:, bass.ds(e * NF + f, 1)]).then_inc(s_sg, 1)
                if more:
                    act.wait_ge(s_tg, u + 2)
                    act.wait_ge(s_xl, u + 1)
                    raw_rows()
                if prefetch:
                    act.wait_ge(s_wld, e * 16 + 16)
                    act.wait_ge(s_y, e * UPE + 1)
                    nc.scalar.activation(ws[1 - s][:, 0, bass.ds(c * qw, qw)], wraw[:, bass.ds(c * qw, qw)],
                                         ACT.Copy).then_inc(s_wh, 1)
                if glu:
                    act.wait_ge(s_y, u + 2)
                    act.wait_ge(s_ys, u * 16 + 16)
                    for j in range(UT):
                        nc.scalar.activation(ysb[:, j, :], b_y[j][:, 0:D], ACT.Copy).then_inc(s_ye, 1)
            experts(act, unit)

        @block.vector
        def _(dve):
            V = nc.vector

            def split_rows(n):
                dve.wait_ge(s_xr, 2 * n)
                V.tensor_copy(xT[:, 0, :, :], xraw[:, :, :]).then_inc(s_xh, 1)
                dve.wait_ge(s_xh, n)
                V.tensor_tensor(xT[:, 1, :, :], xraw[:, :, :], xT[:, 0, :, :].bitcast(F32), ALU.subtract).then_inc(s_xl, 1)

            dve.sem_inc(s_hl, RING)
            dve.sem_inc(s_hm, RING)
            dve.sem_inc(s_wl, 4)
            if not glu:
                dve.sem_inc(s_ye, UT)
                dve.wait_ge(s_ld, 16 * 3)
            split_rows(1)

            def unit(e, c, u, s, prefetch, more):
                def product(f):
                    dve.wait_ge(s_sg, u * NF + f + 1 + RING)
                    dve.wait_ge(s_hl, u * NF + f + 1)
                    V.tensor_tensor(hraw[:, f % RING, :], sg[:, f % RING, :], bank[f % RING][:, UW:2 * UW],
                                    ALU.mult).then_inc(s_hm, 1)

                def high(f):
                    if f == 0:
                        dve.wait_ge(s_y, u + 1)
                    dve.wait_ge(s_hm if glu else s_sg, u * NF + f + 1 + RING)
                    V.tensor_copy(hT[:, 0, f, :], hraw[:, f % RING, :]).then_inc(s_hh, 1)

                def low(f):
                    dve.wait_ge(s_hh, u * NF + f + 1)
                    V.tensor_tensor(hT[:, 1, f, :], hraw[:, f % RING, :], hT[:, 0, f, :].bitcast(F32),
                                    ALU.subtract).then_inc(s_hl, 1)

                lag = 1 if glu else 0
                for f in range(NF + 1 + lag):
                    if glu and f < NF:
                        product(f)
                    if lag <= f < NF + lag:
                        high(f - lag)
                    if f > lag:
                        low(f - 1 - lag)
                if more:
                    split_rows(u + 2)
                if prefetch:
                    dve.wait_ge(s_wh, e * 4 + c + 1)
                    V.tensor_tensor(ws[1 - s][:, 1, bass.ds(c * qw, qw)], wraw[:, bass.ds(c * qw, qw)],
                                    ws[1 - s][:, 0, bass.ds(c * qw, qw)].bitcast(F32), ALU.subtract).then_inc(s_wl, 1)
                if not glu:
                    dve.wait_ge(s_y, u + 2)
                    dve.wait_ge(s_ys, u * 16 + 16)
                    for j in range(UT):
                        V.tensor_tensor(ysb[:, j, :], b_y[j][:, 0:D], b2[:, bass.ds(e, 1), :].rearrange("p a d -> p (a d)"),
                                        ALU.add).then_inc(s_ye, 1)
            experts(dve, unit)

        @block.tensor
        def _(pe):
            def turn_rows(n):
                pe.wait_ge(s_gx, n * 16 * UT)
                for j in range(UT):
                    for k in range(KD):
                        ins = nc.tensor.transpose(t_ps[:, k, j * P:(j + 1) * P], xg[:, j, k * P:(k + 1) * P], ident)
                ins.then_inc(s_tg, 1)

            def product(out, wts, mov, first, last):
                wh, wl = wts
                mh, ml = mov
                nc.tensor.matmul(out, wh, mh, start=first, stop=False)
                nc.tensor.matmul(out, wh, ml, start=False, stop=False)
                return nc.tensor.matmul(out, wl, mh, start=False, stop=last)

            pe.sem_inc(s_y, 1)
            turn_rows(1)

            def unit(e, c, u, s, prefetch, more):
                w = ws[s]
                pe.wait_ge(s_xl, u + 1)
                for f in range(NF):
                    pe.wait_ge(s_free, u * NF + f + 1)
                    for g in range(2 if glu else 1):
                        for k in range(KD):
                            at = k * (2 * HID if glu else HID) + g * HID + f * P
                            ins = product(bank[f % RING][:, g * UW:(g + 1) * UW],
                                          [w[:, a, at:at + P] for a in range(2)],
                                          [xT[:, a, k, :] for a in range(2)], k == 0, k == KD - 1)
                    ins.then_inc(s_hd, 1)
                if more:
                    turn_rows(u + 2)
                pe.wait_ge(s_ye, u * UT + UT)
                for f in range(NF):
                    pe.wait_ge(s_hl, u * NF + f + 1 + RING)
                    for j in range(UT):
                        ins = product(b_y[j][:, 0:D], [hT[:, a, f, j * P:(j + 1) * P] for a in range(2)],
                                      [w[:, a, w2_at + f * D:w2_at + (f + 1) * D] for a in range(2)], f == 0, f == NF - 1)
                ins.then_inc(s_y, 1)

            def weights(e, s, last):
                after(pe, s_wl, e * 4 + 4, s_pass_pe)
            experts(pe, unit, weights)


def combine_phase(nc, bank, passed, io, tag, first, X, GATE, GI, y_dram, cst, wraw):
    G = 4
    with ExitStack() as ctx:
        def sb(name, shape, dt=F32):
            return ctx.enter_context(nc.sbuf_tensor(f"{tag}_{name}", shape, dt))

        def sem(name):
            return ctx.enter_context(nc.semaphore(f"{tag}_{name}"))

        gi = sb("gi", [P, G, 2], I32)
        yg = sb("yg", [P, G, 2, D])
        acc = sb("acc", [P, G, D])
        st = sb("st", [P, 2, G, 6])
        mv = sb("mv", [P, 2, G, 2])
        sd = sb("sd", [P, 2, G])
        rs = sb("rs", [P, 2, G])
        x2 = sb("x2", [P, G, D])
        xr = sb("xr", [P, G, D])
        xrT = sb("xrT", [P, G, KD, P])
        scb = sb("scb", [P, 2 * KD])
        wr = sb("wr", [P, KD, E])
        eps = sb("eps", [P, 1])
        warm = sb("warm", [P, 1])

        s_gi, s_set = map(sem, ("gi", "set"))
        s_gy = [sem(f"gy{r}") for r in range(G)]
        s_a, s_acc, s_bs, s_mv, s_sd, s_rs, s_x2 = map(sem, ("a", "acc", "bs", "mv", "sd", "rs", "x2"))
        s_st, s_pass, s_pass_dve = sem("st"), passed["pool"], passed["dve"]
        s_ld, s_xc, s_xr, s_tr, s_xT, s_rt = map(sem, ("ld", "xc", "xr", "tr", "xT", "rt")) if first else [None] * 6
        norms = 2 if first else 1
        ident = cst[:, C_ID:C_ID + P]
        t_ps = [bank[1 + r][:, 0:D].rearrange("p (k t) -> p k t", k=KD) for r in range(G)]
        rows = io["xn2"] if first else io["out"].rearrange("b s d -> (b s) d")
        store, s_store = (xr, s_xr) if first else (x2, s_x2)

        block = ctx.enter_context(nc.Block())

        @block.sync
        def _(sp):
            if first:
                sp.dma_start(scb[:, :], io["sc_ffn"]).then_inc(s_ld, 16)
                sp.dma_start(wr[:, :, :], io["wr2"].rearrange("(k p) n -> p k n", p=P)).then_inc(s_ld, 16)
                sp.dma_start(wraw[:, :], io["w_ffn"][0]).then_inc(s_ld, 16)
            sp.sem_inc(s_st, 16 * G)
            with sp.Fori(0, NT // G) as j:
                for r in range(G):
                    sp.wait_ge(s_store, j * G + (G + r + 1))
                    sp.dma_start(rows[bass.ds((j * G + r) * P, P), :], store[:, r, :]).then_inc(s_st, 16)
            sp.wait_ge(s_st, 16 * (NT + G))
            if first:
                sp.wait_ge(s_ld, 16 * 3)

        @block.gpsimd
        def _(pool):
            nc.gpsimd.memset(eps[:, :], EPS).then_inc(s_set, 1)
            pool.sem_inc(s_a, G)
            with pool.Fori(0, NT // G) as j:
                for r in range(G):
                    T = j * G + r
                    after(pool, s_a, T + 1, s_pass)
                    nc.gpsimd.tensor_copy(gi[:, r, :], GI[:, bass.ds(T, 1), :].rearrange("p a c -> p (a c)")).then_inc(s_gi, 1)
                    after(pool, s_gi, T + 1, s_pass)
                    for c in range(2):
                        nc.gpsimd.indirect_dma_start(
                            out=yg[:, r, c, :], out_offset=None, in_=y_dram,
                            in_offset=bass.IndirectOffsetOnAxis(ap=gi[:, r, c:c + 1], axis=0)).then_inc(s_gy[r], 16)

        @block.scalar
        def _(act):
            act.wait_ge(s_set, 1)
            nc.scalar.activation(warm[:, :], eps[:, :], ACT.Sqrt)
            if first:
                act.wait_ge(s_ld, 16 * 3)
                act.sem_inc(s_xT, 2 * G)
            with act.Fori(0, NT // G) as j:
                for m in range(norms):
                    act.wait_ge(s_mv, j * (G * norms) + G * (m + 1))
                    nc.scalar.activation(sd[:, m, :], mv[:, m, :, 1], ACT.Sqrt, bias=eps[:, :]).then_inc(s_sd, 1)
                if first:
                    for r in range(G):
                        act.wait_ge(s_x2, j * G + (G + r + 1))
                        nc.scalar.activation(X[:, bass.ds(j * G + r, 1), :].rearrange("p a d -> p (a d)"), x2[:, r, :],
                                             ACT.Copy).then_inc(s_xc, 1)
                    for r in range(G):
                        act.wait_ge(s_tr, j * G + (G + r + 1))
                        act.wait_ge(s_rt, j * G + (r + 1))
                        for k in range(KD):
                            nc.scalar.activation(xrT[:, r, k, :], t_ps[r][:, k, :], ACT.Identity, scale=scb[:, k:k + 1],
                                                 bias=scb[:, KD + k:KD + k + 1]).then_inc(s_xT, 1)

        @block.vector
        def _(dve):
            V = nc.vector
            dve.sem_inc(s_x2, G)
            if first:
                dve.sem_inc(s_xr, G)
                dve.sem_inc(s_xc, G)
            with dve.Fori(0, NT // G) as j:
                def tile(r):
                    return bass.ds(j * G + r, 1)

                def flat(ap):
                    return ap.rearrange("p a d -> p (a d)")

                for r in range(G):
                    dve.wait_ge(s_gy[r], (j + 1) * 32)
                    dve.wait_ge(s_x2, j * G + G)
                    V.scalar_tensor_tensor(out=acc[:, r, :], in0=yg[:, r, 0, :], scalar=flat(GATE[:, tile(r), 0:1]),
                                           in1=flat(X[:, tile(r), :]), op0=ALU.mult, op1=ALU.add).then_inc(s_acc, 1)
                for r in range(G):
                    dve.wait_ge(s_acc, j * G + r + 1)
                    V.scalar_tensor_tensor(out=acc[:, r, :], in0=yg[:, r, 1, :], scalar=flat(GATE[:, tile(r), 1:2]),
                                           in1=acc[:, r, :], op0=ALU.mult, op1=ALU.add).then_inc(s_a, 1)
                for m in range(norms):
                    src, dst, s_dst = (acc, x2, s_x2) if m == 0 else (x2, xr, s_xr)
                    for r in range(G):
                        dve.wait_ge(s_a if m == 0 else s_x2, j * G + (G + r + 1))
                        V.bn_stats(st[:, m, r, :], src[:, r, :]).then_inc(s_bs, 1)
                    for r in range(G):
                        after(dve, s_bs, j * (G * norms) + (G * m + r + 1), s_pass_dve)
                        V.bn_aggr(mv[:, m, r, :], st[:, m, r, :]).then_inc(s_mv, 1)
                    dve.wait_ge(s_sd, j * norms + (m + 1))
                    V.reciprocal(rs[:, m, :], sd[:, m, :]).then_inc(s_rs, 1)
                    dve.wait_ge(s_rs, j * norms + (m + 1))
                    if dst is store:
                        dve.wait_ge(s_st, j * (16 * G) + 16 * G)
                    if m == 1:
                        dve.wait_ge(s_tr, j * G + G)
                    elif first:
                        dve.wait_ge(s_xc, j * G + G)
                        dve.wait_ge(s_xr, j * G + G)
                    for r in range(G):
                        V.tensor_scalar(dst[:, r, :], src[:, r, :], mv[:, m, r, 0:1], rs[:, m, r:r + 1], ALU.subtract,
                                        ALU.mult).then_inc(s_dst, 1)

        @block.tensor
        def _(pe):
            if not first:
                return
            pe.wait_ge(s_ld, 16 * 3)
            pe.sem_inc(s_tr, G)
            pe.sem_inc(s_rt, G)
            with pe.Fori(0, NT // G) as j:
                for r in range(G):
                    pe.wait_ge(s_xr, j * G + (G + r + 1))
                    pe.wait_ge(s_xT, j * (2 * G) + 2 * (r + 1))
                    for k in range(KD):
                        ins = nc.tensor.transpose(t_ps[r][:, k, :], xr[:, r, k * P:(k + 1) * P], ident)
                    ins.then_inc(s_tr, 1)
                for r in range(G):
                    pe.wait_ge(s_xT, j * (2 * G) + 2 * (G + r + 1))
                    for k in range(KD):
                        ins = nc.tensor.matmul(bank[0][:, bass.ds((j * G + r) * E + D, E)], xrT[:, r, k, :], wr[:, k, :],
                                               start=(k == 0), stop=(k == KD - 1))
                    ins.then_inc(s_rt, 1)


def build(nc, io):
    with ExitStack() as ctx:
        def sb(name, shape, dt=F32):
            return ctx.enter_context(nc.sbuf_tensor(name, shape, dt))

        bank = [ctx.enter_context(nc.psum_tensor(f"bank{i}", [P, 512], F32)) for i in range(8)]
        passed = {e: ctx.enter_context(nc.semaphore(f"passed_{e}")) for e in ("pool", "act", "pe", "dve")}
        X = sb("X", [P, NT, D])
        LG = sb("LG", [P, NT, E])
        GATE = sb("GATE", [P, NT, 2])
        GI = sb("GI", [P, NT, 2], I32)
        IDX = sb("IDX", [P, SC], I32)
        cst = sb("cst", [P, C_N])
        wraw = sb("wraw", [P, 4 * 1536])
        ws0 = sb("ws0", [P, 2, 6144], F32R)

        attention_phase(nc, bank, passed, io, X, cst, wraw)
        routing_phase(nc, bank, io, "R1", True, LG, GATE, GI, IDX, cst, wraw, ws0, 1024)
        with nc.sbuf_tensor("ws1a", [P, 2, 4096], F32R) as ws1:
            expert_phase(nc, bank, passed, io, "E1", False, IDX, io["xn1"], io["y1"], io["w_moe"], io["sc_moe"], cst, wraw, (ws0, ws1))
        combine_phase(nc, bank, passed, io, "C1", True, X, GATE, GI, io["y1"], cst, wraw)
        routing_phase(nc, bank, io, "R2", False, LG, GATE, GI, IDX, cst, wraw, ws0, 1536)
        with nc.sbuf_tensor("ws1b", [P, 2, 6144], F32R) as ws1:
            expert_phase(nc, bank, passed, io, "E2", True, IDX, io["xn2"], io["y2"], io["w_ffn"], io["sc_ffn"], cst, wraw, (ws0, ws1))
        combine_phase(nc, bank, passed, io, "C2", False, X, GATE, GI, io["y2"], cst, wraw)


def kernel(**inputs):
    import concourse.bacc as bacc
    from concourse.bass_utils import run_bass_kernel_spmd

    g = {k: np.asarray(v) for k, v in inputs.items()}

    def column(v):
        return v.reshape(KD, P).T

    w1 = g["L0_attn_W1"].reshape(E, KD, P, HID).transpose(0, 2, 1, 3).reshape(E, P, -1)
    w2 = g["L0_attn_W2"].reshape(E, NF, P, D).transpose(0, 2, 1, 3).reshape(E, P, -1)
    w12 = g["L0_ffn_w12"].transpose(0, 2, 1).reshape(E, KD, P, 2 * HID).transpose(0, 2, 1, 3).reshape(E, P, -1)
    w3 = g["L0_ffn_w3"].transpose(0, 2, 1).reshape(E, NF, P, D).transpose(0, 2, 1, 3).reshape(E, P, -1)
    consts, rope = shape_constants()
    arrays = {
        "x": g["L0_attn_x"],
        "consts": consts,
        "rope": rope,
        "wqkvg": np.concatenate([g[f"L0_attn_W{c}"] for c in "qkvg"], axis=1),
        "bqkvg": np.concatenate([g[f"L0_attn_b{c}"] for c in "qkvg"]),
        "wo": g["L0_attn_Wo"],
        "bo": g["L0_attn_bo"],
        "sc1": column(g["L0_attn_norm1_scale"]),
        "sc2": column(g["L0_attn_norm2_scale"]),
        "wr1": g["L0_attn_router_W"],
        "rb": g["L0_attn_router_b"],
        "w_moe": np.concatenate([w1, w2], axis=2),
        "b1": g["L0_attn_b1"].reshape(E * NF, P).T,
        "b2": g["L0_attn_b2"].reshape(-1),
        "sc_moe": np.concatenate([column(g["L0_attn_norm2_scale"]), np.zeros((P, KD), np.float32)], axis=1),
        "sc_ffn": np.concatenate([column(g["L0_ffn_ln_gamma"]), column(g["L0_ffn_ln_beta"])], axis=1),
        "wr2": g["L0_ffn_router_w"].T,
        "w_ffn": np.concatenate([w12, w3], axis=2),
    }
    arrays = {f"in_{k}": np.ascontiguousarray(v) for k, v in arrays.items()}
    nc = bacc.Bacc("TRN2", target_bir_lowering=False, num_devices=1)
    io = {k[3:]: nc.dram_tensor(k, v.shape, mybir.dt.from_np(v.dtype), kind="ExternalInput").ap() for k, v in arrays.items()}
    io["out"] = nc.dram_tensor("out_0", (BATCH, SEQ, D), F32, kind="ExternalOutput").ap()
    for name, rows in (("xn1", N), ("xn2", N), ("y1", SLOTS), ("y2", SLOTS)):
        io[name] = nc.dram_tensor(name, (rows, D), F32, kind="Internal").ap()
    build(nc, io)
    r = run_bass_kernel_spmd(nc, [arrays], core_ids=[0])
    return r.results[0]["out_0"]
```

```python
from contextlib import ExitStack

import numpy as np

import concourse.bass as bass
from concourse import mybir

F32 = mybir.dt.float32
F32R = mybir.dt.float32r
BF16 = mybir.dt.bfloat16
I32 = mybir.dt.int32
ALU = mybir.AluOpType
ACT = mybir.ActivationFunctionType
AX_X = mybir.AxisListType.X

P = 128
BATCH, SEQ, D = 2, 2048, 256
N = BATCH * SEQ
NT = N // P
TPB = NT // BATCH
KD = D // P
H, DK = 16, 16
HALF = DK // 2
CHUNK = 64
E = 8
HPH = P // DK
SW = P + HPH
HID = 1024
NF = HID // P
CAP = 1280
SLOTS = E * CAP
TILES_E = CAP // P
UW = 256
UPE = CAP // UW
UNITS = E * UPE
UT = UW // P
SC = E * TILES_E
EPS = 1e-5
CLAMP = 10000.0

C_ID, C_TRI, C_MASK = 0, P, 2 * P
C_IOTA = C_MASK + SW
C_REV = C_IOTA + P
C_ROW = C_REV + E
C_TOK = C_ROW + 1
C_EPS = C_TOK + NT
C_N = C_EPS + 1


def shape_constants():
    c = np.zeros((P, C_N), np.float32)
    r = np.arange(P)
    c[:, C_ID:C_ID + P] = np.eye(P)
    c[:, C_TRI:C_TRI + P] = (r[:, None] < r[None, :]) - 1.0
    c[:, C_MASK:C_MASK + P] = r[:, None] // DK == r[None, :] // DK
    c[:, C_MASK + P:C_MASK + SW] = r[:, None] // DK == np.arange(HPH)[None, :]
    c[:, C_IOTA:C_IOTA + P] = r[None, :]
    c[:, C_REV:C_REV + E] = E - np.arange(E)[None, :]
    c[:, C_ROW] = r
    c[:, C_TOK:C_EPS] = np.arange(NT)[None, :] * P + r[:, None]
    half = np.arange(HALF, dtype=np.float32) / np.float32(HALF)
    inv = (np.float32(1.0) / np.power(np.float32(10000.0), half)).astype(np.float32)
    ang = (np.arange(SEQ, dtype=np.float32)[:, None] * inv[None, :]).astype(np.float32)
    c[:, C_EPS] = EPS
    cos, sin = np.cos(ang).astype(np.float32), np.sin(ang).astype(np.float32)
    rope = np.concatenate([cos, -sin, sin], axis=1).reshape(TPB, P, 3 * HALF).transpose(1, 0, 2)
    return c, np.ascontiguousarray(rope)


def after(eng, sem, count, passed=None):
    if isinstance(count, int) and count <= 0:
        return
    eng.wait_ge(sem, count)
    if passed is not None:
        eng.sem_inc(passed, 1)


LEAD = 3
LAG = 2
LOOP_FROM = 4
LOOP_STEPS = (NT - LOOP_FROM - LEAD) // 2


class Tile:

    def __init__(self, n, b, i):
        self.n, self.b, self.i = n, b, i
        self.T = i + b * TPB


def fixed_tile(n):
    return Tile(n, n % 2, n // 2) if 0 <= n < NT else None


def run_tiles(eng, step, before_loop):
    for t in range(-LEAD, LOOP_FROM):
        step(lambda d: fixed_tile(t + d))
    before_loop()
    with eng.Fori(0, LOOP_STEPS) as j:
        for r in range(2):
            step(lambda d: Tile(j * 2 + (LOOP_FROM + r + d), (r + d) % 2, j + (LOOP_FROM + r + d) // 2))
    for t in range(LOOP_FROM + 2 * LOOP_STEPS, NT + LAG):
        step(lambda d: fixed_tile(t + d))


def attention_phase(nc, bank, passed, io, X, cst, rbias, wraw):
    with ExitStack() as ctx:
        def sb(name, shape, dt=F32):
            return ctx.enter_context(nc.sbuf_tensor("A_" + name, shape, dt))

        def sem(name):
            return ctx.enter_context(nc.semaphore("A_" + name))

        wqkvg = sb("wqkvg", [P, KD, 4 * D])
        wsp = sb("wsp", [P, 2, KD, 4 * D], F32R)
        wo = sb("wo", [P, KD, D])
        wr = sb("wr", [P, KD, E])
        sc1 = sb("sc1", [P, KD])
        sc2 = sb("sc2", [P, KD])
        bqkvg = sb("bqkvg", [P, 4 * D])
        bo = sb("bo", [P, D])
        rope = sb("rope", [P, TPB, 3 * HALF])
        zeros = sb("zeros", [P, KD * SW])
        mhalf = sb("mhalf", [P, 1])
        junk = sb("junk", [P, 2, 2, D])
        ssq1, r1 = sb("ssq1", [P, 2]), sb("r1", [P, 2])
        ssq2, r2 = sb("ssq2", [P, 2]), sb("r2", [P, 2])
        xs = sb("xs", [P, 2, D])
        xT = sb("xT", [P, 2, 2, KD, P], F32R)
        qk = sb("qk", [P, 2 * D])
        ra = sb("ra", [P, 2 * D])
        rb = sb("rb", [P, 2 * D])
        rot = sb("rot", [P, 2, 2 * D])
        neg = sb("neg", [P, 2, 2 * D])
        phi = sb("phi", [P, 2, 2 * D])
        va = sb("va", [P, 2, KD, SW])
        gt = sb("gt", [P, 2, D])
        qT = sb("qT", [P, KD, P])
        sm = sb("sm", [P, 2, KD, SW])
        den = sb("den", [P, KD, HPH])
        rden = sb("rden", [P, KD, HPH])
        on = sb("on", [P, 2, D])
        og = sb("og", [P, 2, D])
        oT = sb("oT", [P, KD, P])
        xb = sb("xb", [P, 2, D])
        x1 = sb("x1", [P, 2, D])
        xn = sb("xn", [P, 2, D])
        xnT = sb("xnT", [P, KD, P])

        early, loads, xg = sem("early"), sem("loads"), [sem(f"xg{g}") for g in range(4)]
        s_w, s_wh, s_wl, s_cst = sem("w"), sem("wh"), sem("wl"), sem("cst")
        s_ssq1, s_r1, s_xs, s_tx, s_xT, s_xl = map(sem, ("ssq1", "r1", "xs", "tx", "xT", "xl"))
        s_pj0, s_pj1, s_qk, s_ra, s_rb, s_rot, s_vg = map(sem, ("pj0", "pj1", "qk", "ra", "rb", "rot", "vg"))
        s_mn, s_ex, s_phi, s_th, s_g = map(sem, ("mn", "ex", "phi", "th", "g"))
        s_tq, s_qT, s_sa, s_mk, s_num = map(sem, ("tq", "qT", "sa", "mk", "num"))
        s_den, s_rden, s_on, s_og = map(sem, ("den", "rden", "on", "og"))
        s_to, s_oT, s_wo, s_xb, s_x1, s_xacc = map(sem, ("to", "oT", "wo", "xb", "x1", "xacc"))
        s_ssq2, s_r2, s_xn, s_tr, s_xnT, s_rt = map(sem, ("ssq2", "r2", "xn", "tr", "xnT", "rt"))
        s_st, s_wst = [sem(f"st{b}") for b in range(2)], sem("wst")
        s_pass, s_pass_act = passed["pool"], passed["act"]

        LATER = 6
        ident = cst[:, C_ID:C_ID + P]
        hmask = cst[:, C_MASK:C_MASK + SW].unsqueeze(1).to_broadcast([P, KD, SW])
        b_tx, b_tq, b_tor, b_num, b_p0, b_p1 = bank[0:6]
        b_s = bank[6:8]
        tx_ps = b_tx[:, 0:D].rearrange("p (k t) -> p k t", k=KD)
        tq_ps = b_tq[:, 0:D].rearrange("p (k t) -> p k t", k=KD)
        wo_ps = b_tq[:, 0:D]
        to_ps = b_tor[:, 0:D].rearrange("p (k t) -> p k t", k=KD)
        tr_ps = b_tor[:, D:2 * D].rearrange("p (k t) -> p k t", k=KD)
        num_ps = b_num[:, 0:KD * SW].rearrange("p (k c) -> p k c", k=KD)
        s_ps = [b[:, 0:KD * SW].rearrange("p (k c) -> p k c", k=KD) for b in b_s]

        def halves(ap):
            return ap.rearrange("p (h a d) -> p h a d", a=2, d=HALF)

        block = ctx.enter_context(nc.Block())

        @block.sync
        def _(sp):
            xv = io["x"].rearrange("b (i p) d -> p b i d", p=P)
            Xv = X[:, :, :].rearrange("p (b i) d -> p b i d", b=BATCH)
            g = TPB // 4
            sp.dma_start(sc1[:, :], io["sc1"]).then_inc(early, 16)
            sp.dma_start(wqkvg[:, :, :], io["wqkvg"].rearrange("(k p) n -> p k n", p=P)).then_inc(early, 16)
            sp.dma_start(cst[:, :], io["consts"]).then_inc(early, 16)
            for b in range(BATCH):
                sp.dma_start(Xv[:, b, 0:g, :], xv[:, b, 0:g, :]).then_inc(xg[0], 16)
            sp.dma_start(sc2[:, :], io["sc2"]).then_inc(loads, 16)
            sp.dma_start(bqkvg[:, :], io["bqkvg"].partition_broadcast(P)).then_inc(loads, 16)
            sp.dma_start(bo[:, :], io["bo"].partition_broadcast(P)).then_inc(loads, 16)
            sp.dma_start(rope[:, :, :], io["rope"]).then_inc(loads, 16)
            sp.dma_start(wo[:, :, :], io["wo"].rearrange("(k p) n -> p k n", p=P)).then_inc(loads, 16)
            sp.dma_start(wr[:, :, :], io["wr1"].rearrange("(k p) n -> p k n", p=P)).then_inc(loads, 16)
            for q in range(1, 4):
                for b in range(BATCH):
                    sp.dma_start(Xv[:, b, q * g:q * g + g, :], xv[:, b, q * g:q * g + g, :]).then_inc(xg[q], 16)
            sp.dma_start(rbias[:, :], io["rb"].partition_broadcast(P)).then_inc(s_wst, 16)
            sp.dma_start(wraw[:, 0:4 * HID], io["w_moe"][0]).then_inc(s_wst, 16)

            def step(at):
                if (t := at(-2)) is not None:
                    after(sp, s_xn, t.n + 1)
                    sp.dma_start(io["xn1"][bass.ts(t.T, P), :], xn[:, t.b, :]).then_inc(s_st[t.b], 16)
            run_tiles(sp, step, lambda: None)
            for b in range(BATCH):
                sp.wait_ge(s_st[b], 16 * TPB)
            sp.wait_ge(s_wst, 32)

        @block.gpsimd
        def _(pool):
            nc.gpsimd.memset(mhalf[:, :], -0.5).then_inc(s_cst, 1)
            nc.gpsimd.memset(zeros[:, :], 0.0).then_inc(s_cst, 1)
            nc.gpsimd.memset(va[:, :, :, :], 1.0).then_inc(s_cst, 1)
            pool.wait_ge(s_cst, 3)
            pool.wait_ge(xg[0], 32)

            def step(at):
                if (t := at(-2)) is not None:
                    after(pool, s_ssq2, t.n + 1, s_pass)
                    after(pool, s_xn, t.n - 1, s_pass)
                    nc.gpsimd.tensor_tensor(r2[:, t.b:t.b + 1], ssq2[:, t.b:t.b + 1], mhalf[:, :], ALU.pow).then_inc(s_r2, 1)
                if (t := at(-1)) is not None:
                    after(pool, s_g, t.n + 1, s_pass)
                    after(pool, s_on, t.n + 1, s_pass)
                    after(pool, s_to, t.n - 1, s_pass)
                    nc.gpsimd.tensor_tensor(og[:, t.b, :], on[:, t.b, :], gt[:, t.b, :], ALU.mult).then_inc(s_og, 1)
                if (t := at(1)) is not None:
                    if isinstance(t.n, int) and t.n == 0:
                        pool.wait_ge(loads, 16 * LATER)
                    after(pool, s_qk, t.n + 1, s_pass)
                    after(pool, s_rot, t.n, s_pass)
                    for a in range(2):
                        sn = rope[:, t.i, HALF + a * HALF:HALF + (a + 1) * HALF]
                        nc.gpsimd.tensor_tensor(halves(rb[:, :])[:, :, a, :], halves(qk[:, :])[:, :, 1 - a, :],
                                                sn.unsqueeze(1).to_broadcast([P, 2 * H, HALF]), ALU.mult).then_inc(s_rb, 1)
                if (t := at(3)) is not None:
                    after(pool, s_ssq1, t.n + 1, s_pass)
                    after(pool, s_xs, t.n - 1, s_pass)
                    nc.gpsimd.tensor_tensor(r1[:, t.b:t.b + 1], ssq1[:, t.b:t.b + 1], mhalf[:, :], ALU.pow).then_inc(s_r1, 1)
                if (t := at(-1)) is not None:
                    after(pool, s_x1, t.n - 1, s_pass)
                    nc.gpsimd.tensor_tensor(xb[:, t.b, :], X[:, t.T, :], bo[:, :], ALU.add).then_inc(s_xb, 1)
                if (t := at(-2)) is not None:
                    after(pool, s_xb, t.n + 1, s_pass)
                    after(pool, s_x1, t.n + 1, s_pass)
                    nc.gpsimd.tensor_tensor(X[:, t.T, :], X[:, t.T, :], x1[:, t.b, :], ALU.add).then_inc(s_xacc, 1)
                if (t := at(0)) is not None:
                    after(pool, s_th, t.n + 1, s_pass)
                    nc.gpsimd.tensor_scalar(gt[:, t.b, :], gt[:, t.b, :], 0.5, 0.5, ALU.mult, ALU.add).then_inc(s_g, 1)

            def all_x():
                for q in range(1, 4):
                    pool.wait_ge(xg[q], 32)
            run_tiles(pool, step, all_x)

        @block.scalar
        def _(act):
            for k in range(KD):
                act.wait_ge(s_w, k + 1)
                nc.scalar.activation(wsp[:, 0, k, :], wqkvg[:, k, :], ACT.Copy).then_inc(s_wh, 1)
            act.wait_ge(xg[0], 32)

            def step(at):
                if (t := at(-2)) is not None:
                    after(act, s_x1, t.n + 1)
                    after(act, s_r2, t.n - 1)
                    nc.scalar.activation(junk[:, 0, t.b, :], x1[:, t.b, :], ACT.Square, scale=float(D) ** -0.5,
                                         accum_out=ssq2[:, t.b:t.b + 1]).then_inc(s_ssq2, 1)
                if (t := at(3)) is not None:
                    after(act, s_r1, t.n - 1)
                    nc.scalar.activation(junk[:, 1, t.b, :], X[:, t.T, :], ACT.Square, scale=float(D) ** -0.5,
                                         accum_out=ssq1[:, t.b:t.b + 1]).then_inc(s_ssq1, 1)
                if (t := at(-2)) is not None:
                    after(act, s_r2, t.n + 1)
                    after(act, s_st[t.b], t.i * 16)
                    after(act, s_tr, t.n - 1)
                    nc.scalar.activation(xn[:, t.b, :], x1[:, t.b, :], ACT.Copy, scale=r2[:, t.b:t.b + 1]).then_inc(s_xn, 1)
                if (t := at(2)) is not None:
                    after(act, s_tx, t.n + 1)
                    after(act, s_pj1, t.n - 1)
                    after(act, s_xl, t.n - 1)
                    nc.scalar.activation(xT[:, t.b, 0, :, :], tx_ps, ACT.Copy).then_inc(s_xT, 1)
                if (t := at(0)) is not None:
                    after(act, s_tq, t.n + 1)
                    after(act, s_num, t.n)
                    nc.scalar.activation(qT[:, :, :], tq_ps, ACT.Copy).then_inc(s_qT, 1)
                if (t := at(-2)) is not None:
                    after(act, s_tr, t.n + 1)
                    after(act, s_rt, t.n)
                    nc.scalar.activation(xnT[:, :, :], tr_ps, ACT.Copy).then_inc(s_xnT, 1)
                if (t := at(0)) is not None:
                    after(act, s_vg, 2 * t.n + 2)
                    nc.scalar.activation(gt[:, t.b, :], gt[:, t.b, :], ACT.Tanh, scale=0.5).then_inc(s_th, 1)
                if (t := at(-1)) is not None:
                    after(act, s_to, t.n + 1)
                    after(act, s_wo, t.n)
                    nc.scalar.activation(oT[:, :, :], to_ps, ACT.Copy).then_inc(s_oT, 1)
                if (t := at(3)) is not None:
                    after(act, s_r1, t.n + 1)
                    after(act, s_tx, t.n - 1, s_pass_act)
                    nc.scalar.activation(xs[:, t.b, :], X[:, t.T, :], ACT.Copy, scale=r1[:, t.b:t.b + 1]).then_inc(s_xs, 1)
                if (t := at(1)) is not None:
                    after(act, s_mn, t.n + 1)
                    nc.scalar.activation(neg[:, t.b, :], neg[:, t.b, :], ACT.Exp).then_inc(s_ex, 1)

            def all_x():
                for q in range(1, 4):
                    act.wait_ge(xg[q], 32)
            run_tiles(act, step, all_x)

        @block.vector
        def _(dve):
            dve.wait_ge(early, 16 * 3)
            for k in range(KD):
                nc.vector.tensor_scalar(wqkvg[:, k, :], wqkvg[:, k, :], sc1[:, k:k + 1], None, ALU.mult).then_inc(s_w, 1)
            for k in range(KD):
                dve.wait_ge(s_wh, k + 1)
                nc.vector.tensor_tensor(wsp[:, 1, k, :], wqkvg[:, k, :], wsp[:, 0, k, :].bitcast(F32), ALU.subtract).then_inc(s_wl, 1)
            dve.wait_ge(loads, 16 * LATER)
            for k in range(KD):
                nc.vector.tensor_scalar(wr[:, k, :], wr[:, k, :], sc2[:, k:k + 1], None, ALU.mult).then_inc(s_w, 1)
            dve.wait_ge(s_cst, 3)

            def mask(t, c):
                after(dve, s_num, t.n)
                after(dve, s_sa, 2 * t.n + c + 1)
                nc.vector.tensor_tensor(sm[:, c, :, :], s_ps[t.b], hmask, ALU.mult).then_inc(s_mk, 1)

            def step(at):
                if (t := at(-2)) is not None:
                    after(dve, s_wo, t.n + 1)
                    after(dve, s_xb, t.n + 1)
                    after(dve, s_xacc, t.n - 1)
                    after(dve, s_ssq2, t.n - 1)
                    after(dve, s_xn, t.n - 1)
                    nc.vector.tensor_tensor(x1[:, t.b, :], wo_ps, xb[:, t.b, :], ALU.add).then_inc(s_x1, 1)
                if (t := at(0)) is not None:
                    after(dve, s_ex, t.n + 1)
                    after(dve, s_sa, 2 * t.n - 2)
                    after(dve, s_tq, t.n - 1)
                    nc.vector.scalar_tensor_tensor(out=phi[:, t.b, :], in0=rot[:, t.b, :], scalar=0.0, in1=neg[:, t.b, :],
                                                   op0=ALU.max, op1=ALU.add).then_inc(s_phi, 1)
                if (t := at(0)) is not None:
                    after(dve, s_pj1, t.n + 1)
                    after(dve, s_sa, 2 * t.n - 2)
                    nc.vector.tensor_tensor(va[:, t.b, :, 0:P], b_p1[:, 0:D].rearrange("p (k c) -> p k c", k=KD),
                                            bqkvg[:, 2 * D:3 * D].rearrange("p (k c) -> p k c", k=KD), ALU.add).then_inc(s_vg, 1)
                if (t := at(-1)) is not None:
                    after(dve, s_num, t.n + 1)
                    nc.vector.tensor_scalar(den[:, :, :], num_ps[:, :, P:SW], 1e-6, None, ALU.add).then_inc(s_den, 1)
                    after(dve, s_den, t.n + 1)
                    after(dve, s_on, t.n)
                    nc.vector.reciprocal(rden[:, :, :], den[:, :, :]).then_inc(s_rden, 1)
                    after(dve, s_rden, t.n + 1)
                    after(dve, s_og, t.n - 1)
                    for k in range(KD):
                        ins = nc.vector.tensor_tensor(
                            on[:, t.b, k * P:(k + 1) * P].rearrange("p (h d) -> p h d", d=DK),
                            num_ps[:, k, 0:P].rearrange("p (h d) -> p h d", d=DK),
                            rden[:, k, :].unsqueeze(2).to_broadcast([P, HPH, DK]), ALU.mult)
                        if k == KD - 1:
                            ins.then_inc(s_on, 1)
                if (t := at(0)) is not None:
                    after(dve, s_og, t.n - 1)
                    nc.vector.tensor_tensor(gt[:, t.b, :], b_p1[:, D:2 * D], bqkvg[:, 3 * D:4 * D], ALU.add).then_inc(s_vg, 1)
                if (t := at(1)) is not None:
                    after(dve, s_pj0, t.n + 1)
                    after(dve, s_rb, 2 * t.n)
                    nc.vector.tensor_tensor(qk[:, :], b_p0[:, :], bqkvg[:, 0:2 * D], ALU.add).then_inc(s_qk, 1)
                if (t := at(0)) is not None:
                    mask(t, 0)
                if (t := at(2)) is not None:
                    after(dve, s_xT, t.n + 1)
                    after(dve, s_pj1, t.n - 1)
                    nc.vector.tensor_tensor(xT[:, t.b, 1, :, :], tx_ps, xT[:, t.b, 0, :, :].bitcast(F32), ALU.subtract).then_inc(s_xl, 1)
                if (t := at(1)) is not None:
                    after(dve, s_qk, t.n + 1)
                    cs = rope[:, t.i, 0:HALF].unsqueeze(1).to_broadcast([P, 4 * H, HALF])
                    nc.vector.tensor_tensor(ra[:, :].rearrange("p (h d) -> p h d", d=HALF),
                                            qk[:, :].rearrange("p (h d) -> p h d", d=HALF), cs, ALU.mult).then_inc(s_ra, 1)
                if (t := at(0)) is not None:
                    mask(t, 1)
                if (t := at(1)) is not None:
                    after(dve, s_rb, 2 * t.n + 2)
                    after(dve, s_ra, t.n + 1)
                    nc.vector.tensor_tensor(rot[:, t.b, :], ra[:, :], rb[:, :], ALU.add).then_inc(s_rot, 1)
                    after(dve, s_rot, t.n + 1)
                    nc.vector.tensor_scalar(neg[:, t.b, :], rot[:, t.b, :], 0.0, None, ALU.min).then_inc(s_mn, 1)
            run_tiles(dve, step, lambda: None)

        @block.tensor
        def _(pe):
            pe.wait_ge(early, 16 * 3)
            pe.wait_ge(s_cst, 3)
            for b in range(BATCH):
                nc.tensor.matmul(b_s[b][:, 0:KD * SW], zeros[:, 0:P], zeros[:, :], start=True, stop=True)

            def add_chunk(t, c):
                rows = slice(c * CHUNK, (c + 1) * CHUNK)
                for k in range(KD):
                    ins = nc.tensor.matmul(s_ps[t.b][:, k, :], phi[rows, t.b, D + k * P:D + (k + 1) * P],
                                           va[rows, t.b, k, :], start=False, stop=True, skip_group_check=True)
                ins.then_inc(s_sa, 1)

            def project(t, part, b_p, ks):
                for k in ks:
                    for m, (a, b) in enumerate(((0, 0), (0, 1), (1, 0))):
                        ins = nc.tensor.matmul(b_p[:, :], xT[:, t.b, a, k, :], wsp[:, b, k, part * 2 * D:(part + 1) * 2 * D],
                                               start=(k == 0 and m == 0), stop=(k == KD - 1 and m == 2))
                return ins

            def step(at):
                if (t := at(1)) is not None:
                    if isinstance(t.n, int) and t.n == 0:
                        pe.wait_ge(s_wl, KD)
                    after(pe, s_xl, t.n + 1)
                    after(pe, s_qk, t.n)
                    project(t, 0, b_p0, range(KD)).then_inc(s_pj0, 1)
                if (t := at(2)) is not None:
                    after(pe, s_xs, t.n + 1)
                    after(pe, s_xl, t.n)
                    for k in range(KD):
                        ins = nc.tensor.transpose(tx_ps[:, k, :], xs[:, t.b, k * P:(k + 1) * P], ident)
                    ins.then_inc(s_tx, 1)
                if (t := at(0)) is not None:
                    after(pe, s_phi, t.n + 1)
                    after(pe, s_x1, t.n - 1)
                    for k in range(KD):
                        ins = nc.tensor.transpose(tq_ps[:, k, :], phi[:, t.b, k * P:(k + 1) * P], ident)
                    ins.then_inc(s_tq, 1)
                    after(pe, s_mk, 2 * t.n - 2)
                    after(pe, s_vg, 2 * t.n + 1)
                    add_chunk(t, 0)
                if (t := at(-2)) is not None:
                    after(pe, s_xn, t.n + 1)
                    after(pe, s_oT, t.n + 1)
                    after(pe, s_xnT, t.n)
                    for k in range(KD):
                        ins = nc.tensor.transpose(tr_ps[:, k, :], xn[:, t.b, k * P:(k + 1) * P], ident)
                    ins.then_inc(s_tr, 1)
                if (t := at(1)) is not None:
                    after(pe, s_vg, 2 * t.n)
                    project(t, 1, b_p1, [0])
                if (t := at(0)) is not None:
                    after(pe, s_mk, 2 * t.n + 1)
                    add_chunk(t, 1)
                if (t := at(-1)) is not None:
                    after(pe, s_og, t.n + 1)
                    after(pe, s_oT, t.n)
                    after(pe, s_xnT, t.n)
                    for k in range(KD):
                        ins = nc.tensor.transpose(to_ps[:, k, :], og[:, t.b, k * P:(k + 1) * P], ident)
                    ins.then_inc(s_to, 1)
                if (t := at(0)) is not None:
                    after(pe, s_qT, t.n + 1)
                    after(pe, s_on, t.n)
                    for c in range(2):
                        after(pe, s_mk, 2 * t.n + c + 1)
                        rows = slice(c * CHUNK, (c + 1) * CHUNK)
                        for k in range(KD):
                            ins = nc.tensor.matmul(num_ps[rows, k, :], qT[:, k, rows], sm[:, c, k, :], start=True, stop=True)
                    ins.then_inc(s_num, 1)
                if (t := at(-1)) is not None:
                    after(pe, s_oT, t.n + 1)
                    after(pe, s_qT, min(t.n + 2, NT) if isinstance(t.n, int) else t.n + 2)
                    after(pe, s_x1, t.n)
                    for k in range(KD):
                        ins = nc.tensor.matmul(wo_ps, oT[:, k, :], wo[:, k, :], start=(k == 0), stop=(k == KD - 1))
                    ins.then_inc(s_wo, 1)
                if (t := at(1)) is not None:
                    project(t, 1, b_p1, [1]).then_inc(s_pj1, 1)
                if (t := at(-2)) is not None:
                    if isinstance(t.n, int) and t.n == 0:
                        pe.wait_ge(s_w, 2 * KD)
                    after(pe, s_xnT, t.n + 1)
                    after(pe, s_xl, min(t.n + 5, NT) if isinstance(t.n, int) else t.n + 5)
                    for k in range(KD):
                        ins = nc.tensor.matmul(b_tx[:, bass.ds(t.T * E + D, E)], xnT[:, k, :], wr[:, k, :],
                                               start=(k == 0), stop=(k == KD - 1))
                    ins.then_inc(s_rt, 1)
            run_tiles(pe, step, lambda: None)


def routing_phase(nc, bank, io, tag, first, LG, GATE, GI, IDX, cst, rbias, wraw, ws0, qw):
    with ExitStack() as ctx:
        def sb(name, shape, dt=F32):
            return ctx.enter_context(nc.sbuf_tensor(f"{tag}_{name}", shape, dt))

        def sem(name):
            return ctx.enter_context(nc.semaphore(f"{tag}_{name}"))

        best = sb("best", [P, 2, NT])
        eq = sb("eq", [P, NT, E])
        rev = sb("rev", [P, 2, NT])
        oh = sb("oh", [P, 2, NT, E])
        ohr = sb("ohr", [P, 2, NT, E])
        sel = sb("sel", [P, NT, E], BF16)
        tri = sb("tri", [P, P], BF16)
        ones = sb("ones", [P, P], BF16)
        onef = sb("onef", [P, NT])
        zero = sb("zero", [P, SC], BF16)
        cum = sb("cum", [P, NT, E])
        rank = sb("rank", [P, NT, E])
        rk = sb("rk", [P, 2, NT])
        kept = sb("kept", [P, 2, NT])
        slot = sb("slot", [P, 2, NT])
        inv = sb("inv", [P, 2, NT])
        invi = sb("invi", [P, 2, NT], I32)
        pci = sb("pci", [P, 2, 2, NT], I32)
        pcf = sb("pcf", [P, 2, 2, NT])
        dl = sb("dl", [P, NT])
        ex = sb("ex", [P, 2, NT])
        den = sb("den", [P, NT])
        rg = sb("rg", [P, NT])
        row1h = sb("row1h", [P, 2, 4, P])
        col1h = sb("col1h", [P, 2, 4, SC])

        s_v, s_ex, s_exin, s_sel, s_rank = map(sem, ("v", "ex", "exin", "sel", "rank"))
        s_1h, s_inv, s_set, s_hi = map(sem, ("1h", "inv", "set", "hi"))
        s_pc = sem("pc")
        lg_ps = bank[0][:, D:D + NT * E].rearrange("p (t e) -> p t e", e=E)
        rank_ps = bank[3][:, 0:NT * E].rearrange("p (t e) -> p t e", e=E)
        tot_ps = bank[1][:, 0:NT * E].rearrange("p (t e) -> p t e", e=E)
        iota = cst[:, C_IOTA:C_IOTA + P]
        revc = cst[:, C_REV:C_REV + E].unsqueeze(1).to_broadcast([P, NT, E])

        def over_e(ap):
            return ap.unsqueeze(2).to_broadcast([P, NT, E])

        block = ctx.enter_context(nc.Block())

        @block.scalar
        def _(act):
            for q in range(4):
                nc.scalar.activation(ws0[:, 0, q * qw:(q + 1) * qw], wraw[:, q * qw:(q + 1) * qw], ACT.Copy).then_inc(s_hi, 1)
                if q == 0:
                    act.wait_ge(s_exin, 1)
                    nc.scalar.activation(ex[:, 1, :], dl[:, :], ACT.Exp).then_inc(s_ex, 1)

        @block.gpsimd
        def _(pool):
            nc.gpsimd.memset(zero[:, :], 0.0).then_inc(s_set, 1)
            nc.gpsimd.memset(ones[:, :], 1.0).then_inc(s_set, 1)
            nc.gpsimd.memset(onef[:, :], 1.0).then_inc(s_set, 1)
            nc.gpsimd.tensor_copy(tri[:, :], cst[:, C_TRI:C_TRI + P]).then_inc(s_set, 1)
            for q in range(4):
                pool.wait_ge(s_hi, q + 1)
                nc.gpsimd.tensor_tensor(ws0[:, 1, q * qw:(q + 1) * qw], wraw[:, q * qw:(q + 1) * qw],
                                        ws0[:, 0, q * qw:(q + 1) * qw].bitcast(F32), ALU.subtract)

        @block.vector
        def _(dve):
            done = [0]

            def chain(ins):
                done[0] += 1
                ins.then_inc(s_v, 1)
                dve.wait_ge(s_v, done[0])

            V = nc.vector
            if first:
                chain(V.tensor_tensor(LG[:, :, :], lg_ps, rbias[:, :].unsqueeze(1).to_broadcast([P, NT, E]), ALU.add))
            else:
                chain(V.tensor_scalar(LG[:, :, :], lg_ps, CLAMP, -CLAMP, ALU.min, ALU.max))
            for c in range(2):
                chain(V.tensor_reduce(best[:, c, :], LG[:, :, :], AX_X, ALU.max))
                if c == 1:
                    V.tensor_tensor(dl[:, :], best[:, 1, :], best[:, 0, :], ALU.subtract).then_inc(s_exin, 1)
                chain(V.tensor_tensor(eq[:, :, :], LG[:, :, :], over_e(best[:, c, :]), ALU.is_equal))
                chain(V.tensor_tensor(eq[:, :, :], eq[:, :, :], revc, ALU.mult))
                chain(V.tensor_reduce(rev[:, c, :], eq[:, :, :], AX_X, ALU.max))
                chain(V.tensor_tensor(oh[:, c, :, :], revc, over_e(rev[:, c, :]), ALU.is_equal))
                if c == 0:
                    chain(V.scalar_tensor_tensor(out=LG[:, :, :], in0=oh[:, 0, :, :], scalar=-3e38, in1=LG[:, :, :],
                                                 op0=ALU.mult, op1=ALU.add))
            V.tensor_tensor(sel[:, :, :], oh[:, 0, :, :], oh[:, 1, :, :], ALU.add).then_inc(s_sel, 1)
            dve.wait_ge(s_ex, 1)
            chain(V.tensor_scalar(den[:, :], ex[:, 1, :], 1.0, 0.0 if first else 1e-12, ALU.add, ALU.add))
            V.reciprocal(rg[:, :], den[:, :])
            dve.wait_ge(s_set, 4)
            dve.wait_ge(s_rank, 2)
            for e in range(E):
                ins = V.tensor_tensor_scan(cum[:, :, e], onef[:, :], tot_ps[:, :, e], 0.0, ALU.mult, ALU.add)
                if e == E - 1:
                    chain(ins)
            chain(V.tensor_tensor(rank[:, :, :], rank_ps, cum[:, :, :], ALU.add))
            for c in range(2):
                ins = V.tensor_tensor(ohr[:, c, :, :], oh[:, c, :, :], rank[:, :, :], ALU.mult)
            chain(ins)
            chain(V.tensor_reduce(rk[:, :, :], ohr[:, :, :, :], AX_X, ALU.add))
            V.tensor_scalar(kept[:, :, :], rk[:, :, :], float(CAP), None, ALU.is_lt)
            chain(V.tensor_scalar(slot[:, :, :], rev[:, :, :], -float(CAP), float(SLOTS), ALU.mult, ALU.add))
            chain(V.tensor_tensor(slot[:, :, :], slot[:, :, :], rk[:, :, :], ALU.add))
            V.tensor_scalar(GI[:, :, :].rearrange("p t c -> p c t"), slot[:, :, :], float(SLOTS - 1), None, ALU.min)
            chain(V.scalar_tensor_tensor(out=inv[:, :, :], in0=kept[:, :, :], scalar=-16384.0, in1=slot[:, :, :],
                                         op0=ALU.mult, op1=ALU.add))
            chain(V.tensor_scalar(invi[:, :, :], inv[:, :, :], 16384.0, None, ALU.add))
            V.tensor_scalar(pci[:, 0, :, :], invi[:, :, :], P - 1, None, ALU.bitwise_and)
            chain(V.tensor_scalar(pci[:, 1, :, :], invi[:, :, :], 7, None, ALU.logical_shift_right))
            V.tensor_copy(pcf[:, :, :, :], pci[:, :, :, :]).then_inc(s_pc, 1)
            dve.wait_ge(s_pc, 1)
            with dve.Fori(0, NT // 4) as j:
                for h in range(2):
                    dve.wait_ge(s_inv, j * 8 + (4 * h + 4))
                    for g in range(4):
                        T, c = j * 4 + (2 * h + g // 2), g % 2
                        V.tensor_scalar(col1h[:, h, g, :], iota[:, 0:SC], pcf[:, 1, c, bass.ds(T, 1)],
                                        cst[:, bass.ds(T + C_TOK, 1)], ALU.is_equal, ALU.mult).then_inc(s_1h, 1)
                        V.tensor_scalar(row1h[:, h, g, :], iota, pcf[:, 0, c, bass.ds(T, 1)], None,
                                        ALU.is_equal).then_inc(s_1h, 1)
            V.tensor_tensor(GATE[:, :, 0], rg[:, :], kept[:, 0, :], ALU.mult)
            chain(V.tensor_tensor(ex[:, 0, :], ex[:, 1, :], kept[:, 1, :], ALU.mult))
            V.tensor_tensor(GATE[:, :, 1], ex[:, 0, :], rg[:, :], ALU.mult)
            dve.wait_ge(s_inv, 2 * NT + 8)
            V.tensor_copy(IDX[:, :], bank[2][:, 0:SC])

        @block.tensor
        def _(pe):
            pe.wait_ge(s_set, 4)
            pe.wait_ge(s_sel, 1)
            cols = sel[:, :, :].rearrange("p t e -> p (t e)")
            nc.tensor.matmul(bank[3][:, 0:NT * E], tri[:, :], cols, start=True, stop=True).then_inc(s_rank, 1)
            nc.tensor.matmul(bank[1][:, 0:NT * E], ones[:, :], cols, start=True, stop=True).then_inc(s_rank, 1)
            nc.tensor.matmul(bank[2][:, 0:SC], ones[:, :], zero[:, :], start=True, stop=True)
            pe.sem_inc(s_inv, 8)
            with pe.Fori(0, NT // 4) as j:
                for h in range(2):
                    for g in range(4):
                        pe.wait_ge(s_1h, j * 16 + (8 * h + 2 * g + 2))
                        nc.tensor.matmul(bank[2][:, 0:SC], row1h[:, h, g, :], col1h[:, h, g, :],
                                         start=False, stop=True, skip_group_check=True).then_inc(s_inv, 1)


def expert_phase(nc, bank, passed, io, tag, glu, IDX, xn_dram, y_dram, w_dram, sc_dram, cst, wraw, ws):
    qw = 1536 if glu else 1024
    w2_at = 4096 if glu else 2048
    with ExitStack() as ctx:
        def sb(name, shape, dt=F32):
            return ctx.enter_context(nc.sbuf_tensor(f"{tag}_{name}", shape, dt))

        def sem(name):
            return ctx.enter_context(nc.semaphore(f"{tag}_{name}"))

        xg = sb("xg", [P, UT, D])
        ist = sb("ist", [P, UT], I32)
        xraw = sb("xraw", [P, KD, UW])
        xT = sb("xT", [P, 2, KD, UW], F32R)
        hT = sb("hT", [P, 2, NF, UW], F32R)
        hraw = sb("hraw", [P, 4, UW])
        sg = sb("sg", [P, 4, UW]) if glu else None
        ysb = sb("ysb", [P, UT, D])
        scb = sb("scb", [P, 2 * KD])
        warm = sb("warm", [P, 1])
        b1 = None if glu else sb("b1", [P, E * NF])
        b2 = None if glu else sb("b2", [P, E, D])

        s_ld, s_gi, s_gx, s_tg, s_xr, s_xh, s_xl = map(sem, ("ld", "gi", "gx", "tg", "xr", "xh", "xl"))
        s_hd, s_sg, s_hh, s_hl = map(sem, ("hd", "sg", "hh", "hl"))
        s_hm = sem("hm") if glu else None
        s_y, s_ye, s_ys, s_wld, s_wh, s_wl = map(sem, ("y", "ye", "ys", "wld", "wh", "wl"))
        s_pass, s_pass_pe = passed["pool"], passed["pe"]
        RING = 4
        s_free = s_hm if glu else s_sg
        b_y, b_t = bank[4:6], bank[6]
        t_ps = b_t[:, :].rearrange("p (k n) -> p k n", k=KD)
        ident = cst[:, C_ID:C_ID + P]

        def experts(eng, unit, at_expert=None):
            def one(e, s, last):
                if at_expert:
                    at_expert(e, s, last)
                with eng.Fori(0, UPE - 1) as c:
                    unit(e, c, e * UPE + c, s, not last, True)
                unit(e, UPE - 1, e * UPE + (UPE - 1), s, False, not last)
            with eng.Fori(0, E // 2 - 1) as ee:
                for s in range(2):
                    one(ee * 2 + s, s, False)
            one(E - 2, 0, False)
            one(E - 1, 1, True)

        block = ctx.enter_context(nc.Block())

        @block.sync
        def _(sp):
            sp.dma_start(scb[:, :], sc_dram).then_inc(s_ld, 16)
            if not glu:
                sp.dma_start(b1[:, :], io["b1"]).then_inc(s_ld, 16)
                sp.dma_start(b2[:, :, :].rearrange("p e d -> p (e d)"), io["b2"].partition_broadcast(P)).then_inc(s_ld, 16)
            sp.wait_ge(s_tg, 1)

            def next_weights(e, s, last):
                if not last:
                    sp.wait_ge(s_wl, e * 4 + 4)
                    sp.dma_start(wraw[:, 0:4 * qw], w_dram[bass.ds(e + 1, 1)].rearrange("a p n -> p (a n)")).then_inc(s_wld, 16)

            def unit(e, c, u, s, prefetch, more):
                sp.wait_ge(s_ye, u * UT + 2 * UT)
                sp.dma_start(y_dram[bass.ds(u * UW, UW), :].rearrange("(j p) d -> p j d", p=P), ysb[:, :, :]).then_inc(s_ys, 16)
            sp.sem_inc(s_ys, 16)
            experts(sp, unit, next_weights)
            sp.wait_ge(s_ys, 16 * UNITS + 16)

        @block.gpsimd
        def _(pool):
            def gather(u, n):
                nc.gpsimd.tensor_copy(ist[:, :], IDX[:, bass.ds(u * UT, UT)]).then_inc(s_gi, 1)
                after(pool, s_gi, n, s_pass)
                for j in range(UT):
                    nc.gpsimd.indirect_dma_start(
                        out=xg[:, j, :], out_offset=None, in_=xn_dram,
                        in_offset=bass.IndirectOffsetOnAxis(ap=ist[:, j:j + 1], axis=0)).then_inc(s_gx, 16)

            def unit(e, c, u, s, prefetch, more):
                if more:
                    after(pool, s_tg, u + 1, s_pass)
                    gather(u + 1, u + 2)
            gather(0, 1)
            experts(pool, unit)

        @block.scalar
        def _(act):
            def raw_rows():
                for k in range(KD):
                    nc.scalar.activation(xraw[:, k, :], t_ps[:, k, :], ACT.Identity, scale=scb[:, k:k + 1],
                                         bias=scb[:, KD + k:KD + k + 1]).then_inc(s_xr, 1)

            nc.scalar.activation(warm[:, :], cst[:, C_ROW:C_ROW + 1], ACT.Silu if glu else ACT.Gelu)
            act.sem_inc(s_sg, RING)
            if glu:
                act.sem_inc(s_ye, UT)
            act.wait_ge(s_ld, 16 * (1 if glu else 3))
            act.wait_ge(s_tg, 1)
            raw_rows()

            def unit(e, c, u, s, prefetch, more):
                for f in range(NF):
                    g = u * NF + f
                    act.wait_ge(s_hd, g + 1)
                    ps = bank[f % RING]
                    if glu:
                        act.wait_ge(s_hm, g + 1)
                        nc.scalar.activation(sg[:, f % RING, :], ps[:, 0:UW], ACT.Silu).then_inc(s_sg, 1)
                    else:
                        act.wait_ge(s_hl, g + 1)
                        nc.scalar.activation(hraw[:, f % RING, :], ps[:, 0:UW], ACT.Gelu,
                                             bias=b1[:, bass.ds(e * NF + f, 1)]).then_inc(s_sg, 1)
                if more:
                    act.wait_ge(s_tg, u + 2)
                    act.wait_ge(s_xl, u + 1)
                    raw_rows()
                if prefetch:
                    act.wait_ge(s_wld, e * 16 + 16)
                    act.wait_ge(s_y, e * UPE + 1)
                    nc.scalar.activation(ws[1 - s][:, 0, bass.ds(c * qw, qw)], wraw[:, bass.ds(c * qw, qw)],
                                         ACT.Copy).then_inc(s_wh, 1)
                if glu:
                    act.wait_ge(s_y, u + 2)
                    act.wait_ge(s_ys, u * 16 + 16)
                    for j in range(UT):
                        nc.scalar.activation(ysb[:, j, :], b_y[j][:, 0:D], ACT.Copy).then_inc(s_ye, 1)
            experts(act, unit)

        @block.vector
        def _(dve):
            V = nc.vector

            def split_rows(n):
                dve.wait_ge(s_xr, 2 * n)
                V.tensor_copy(xT[:, 0, :, :], xraw[:, :, :]).then_inc(s_xh, 1)
                dve.wait_ge(s_xh, n)
                V.tensor_tensor(xT[:, 1, :, :], xraw[:, :, :], xT[:, 0, :, :].bitcast(F32), ALU.subtract).then_inc(s_xl, 1)

            dve.sem_inc(s_hl, RING)
            if glu:
                dve.sem_inc(s_hm, RING)
            dve.sem_inc(s_wl, 4)
            if not glu:
                dve.sem_inc(s_ye, UT)
                dve.wait_ge(s_ld, 16 * 3)
            split_rows(1)

            def unit(e, c, u, s, prefetch, more):
                def product(f):
                    dve.wait_ge(s_sg, u * NF + f + 1 + RING)
                    dve.wait_ge(s_hl, u * NF + f + 1)
                    V.tensor_tensor(hraw[:, f % RING, :], sg[:, f % RING, :], bank[f % RING][:, UW:2 * UW],
                                    ALU.mult).then_inc(s_hm, 1)

                def high(f):
                    if f == 0:
                        dve.wait_ge(s_y, u + 1)
                    dve.wait_ge(s_hm if glu else s_sg, u * NF + f + 1 + RING)
                    V.tensor_copy(hT[:, 0, f, :], hraw[:, f % RING, :]).then_inc(s_hh, 1)

                def low(f):
                    dve.wait_ge(s_hh, u * NF + f + 1)
                    V.tensor_tensor(hT[:, 1, f, :], hraw[:, f % RING, :], hT[:, 0, f, :].bitcast(F32),
                                    ALU.subtract).then_inc(s_hl, 1)

                lag = 1 if glu else 0
                for f in range(NF + 1 + lag):
                    if glu and f < NF:
                        product(f)
                    if lag <= f < NF + lag:
                        high(f - lag)
                    if f > lag:
                        low(f - 1 - lag)
                if more:
                    split_rows(u + 2)
                if prefetch:
                    dve.wait_ge(s_wh, e * 4 + c + 1)
                    V.tensor_tensor(ws[1 - s][:, 1, bass.ds(c * qw, qw)], wraw[:, bass.ds(c * qw, qw)],
                                    ws[1 - s][:, 0, bass.ds(c * qw, qw)].bitcast(F32), ALU.subtract).then_inc(s_wl, 1)
                if not glu:
                    dve.wait_ge(s_y, u + 2)
                    dve.wait_ge(s_ys, u * 16 + 16)
                    for j in range(UT):
                        V.tensor_tensor(ysb[:, j, :], b_y[j][:, 0:D], b2[:, bass.ds(e, 1), :].rearrange("p a d -> p (a d)"),
                                        ALU.add).then_inc(s_ye, 1)
            experts(dve, unit)

        @block.tensor
        def _(pe):
            def turn_rows(n):
                pe.wait_ge(s_gx, n * 16 * UT)
                for j in range(UT):
                    for k in range(KD):
                        ins = nc.tensor.transpose(t_ps[:, k, j * P:(j + 1) * P], xg[:, j, k * P:(k + 1) * P], ident)
                ins.then_inc(s_tg, 1)

            def product(out, wts, mov, first, last):
                wh, wl = wts
                mh, ml = mov
                nc.tensor.matmul(out, wh, mh, start=first, stop=False)
                nc.tensor.matmul(out, wh, ml, start=False, stop=False)
                return nc.tensor.matmul(out, wl, mh, start=False, stop=last)

            pe.sem_inc(s_y, 1)
            turn_rows(1)

            def unit(e, c, u, s, prefetch, more):
                w = ws[s]
                pe.wait_ge(s_xl, u + 1)
                for f in range(NF):
                    pe.wait_ge(s_free, u * NF + f + 1)
                    for g in range(2 if glu else 1):
                        for k in range(KD):
                            at = k * (2 * HID if glu else HID) + g * HID + f * P
                            ins = product(bank[f % RING][:, g * UW:(g + 1) * UW],
                                          [w[:, a, at:at + P] for a in range(2)],
                                          [xT[:, a, k, :] for a in range(2)], k == 0, k == KD - 1)
                    ins.then_inc(s_hd, 1)
                if more:
                    turn_rows(u + 2)
                pe.wait_ge(s_ye, u * UT + UT)
                for f in range(NF):
                    pe.wait_ge(s_hl, u * NF + f + 1 + RING)
                    for j in range(UT):
                        ins = product(b_y[j][:, 0:D], [hT[:, a, f, j * P:(j + 1) * P] for a in range(2)],
                                      [w[:, a, w2_at + f * D:w2_at + (f + 1) * D] for a in range(2)], f == 0, f == NF - 1)
                ins.then_inc(s_y, 1)

            def weights(e, s, last):
                after(pe, s_wl, e * 4 + 4, s_pass_pe)
            experts(pe, unit, weights)


def combine_phase(nc, bank, passed, io, tag, first, X, GATE, GI, y_dram, cst, wraw):
    G = 4
    PAIRS = NT // (2 * G)
    with ExitStack() as ctx:
        def sb(name, shape, dt=F32):
            return ctx.enter_context(nc.sbuf_tensor(f"{tag}_{name}", shape, dt))

        def sem(name):
            return ctx.enter_context(nc.semaphore(f"{tag}_{name}"))

        gi = sb("gi", [P, 2, G, 2], I32)
        yg = sb("yg", [P, 2, G, 2, D])
        acc = sb("acc", [P, G, D])
        x2 = sb("x2", [P, 2, G, D])
        xr = sb("xr", [P, 2, G, D]) if first else None
        xrT = sb("xrT", [P, G, KD, P]) if first else None
        st = sb("st", [P, 2, G, 6])
        mv = sb("mv", [P, 2, G, 2])
        sd = sb("sd", [P, 2, G])
        rs = sb("rs", [P, 2, G])
        nb = sb("nb", [P, G])
        scb = sb("scb", [P, 2 * KD])
        wr = sb("wr", [P, KD, E])
        warm = sb("warm", [P, 1])

        s_gi = sem("gi")
        s_gy = [[sem(f"gy{h}{r}") for r in range(G // 2)] for h in range(2)]
        s_a, s_acc, s_bs, s_mv, s_sd, s_rs, s_x2 = map(sem, ("a", "acc", "bs", "mv", "sd", "rs", "x2"))
        s_st, s_pass, s_pass_dve = [sem(f"st{h}") for h in range(2)], passed["pool"], passed["dve"]
        s_ld, s_xc, s_nb, s_xr, s_tr, s_xT, s_rt = map(sem, ("ld", "xc", "nb", "xr", "tr", "xT", "rt")) if first else [None] * 7
        norms = 2 if first else 1
        ident = cst[:, C_ID:C_ID + P]
        eps = cst[:, C_EPS:C_EPS + 1]
        t_ps = [bank[1 + r][:, 0:D].rearrange("p (k t) -> p k t", k=KD) for r in range(G)]
        rows = io["xn2"] if first else io["out"].rearrange("b s d -> (b s) d")
        store, s_store = (xr, s_xr) if first else (x2, s_x2)

        def flat(ap):
            return ap.rearrange("p a d -> p (a d)")

        def run_groups(eng, step):
            with eng.Fori(0, PAIRS) as j:
                for h in range(2):
                    step(j * 2 + h, j, h)

        block = ctx.enter_context(nc.Block())

        @block.sync
        def _(sp):
            if first:
                sp.dma_start(scb[:, :], io["sc_ffn"]).then_inc(s_ld, 16)
                sp.dma_start(wr[:, :, :], io["wr2"].rearrange("(k p) n -> p k n", p=P)).then_inc(s_ld, 16)
                sp.dma_start(wraw[:, :], io["w_ffn"][0]).then_inc(s_ld, 16)
            for h in range(2):
                sp.sem_inc(s_st[h], 16 * G)

            def step(q, j, h):
                for r in range(G):
                    sp.wait_ge(s_store, q * G + (2 * G + r + 1))
                    sp.dma_start(rows[bass.ds((q * G + r) * P, P), :], store[:, h, r, :]).then_inc(s_st[h], 16)
            run_groups(sp, step)
            for h in range(2):
                sp.wait_ge(s_st[h], 16 * (NT // 2 + G))
            if first:
                sp.wait_ge(s_ld, 16 * 3)

        @block.gpsimd
        def _(pool):
            pool.sem_inc(s_a, 2 * G)

            def step(q, j, h):
                after(pool, s_a, q * G + G, s_pass)
                nc.gpsimd.tensor_copy(gi[:, h, :, :], GI[:, bass.ds(q * G, G), :]).then_inc(s_gi, 1)
                after(pool, s_gi, q + 1, s_pass)
                for r in range(G):
                    for c in range(2):
                        nc.gpsimd.indirect_dma_start(
                            out=yg[:, h, r, c, :], out_offset=None, in_=y_dram,
                            in_offset=bass.IndirectOffsetOnAxis(ap=gi[:, h, r, c:c + 1], axis=0)).then_inc(s_gy[h][r // 2], 16)
            run_groups(pool, step)

        @block.scalar
        def _(act):
            nc.scalar.activation(warm[:, :], eps, ACT.Sqrt)
            if first:
                act.wait_ge(s_ld, 16 * 3)
                act.sem_inc(s_xT, 2 * G)
                act.sem_inc(s_xc, 2 * G)
                act.sem_inc(s_xr, 2 * G)

            def step(q, j, h):
                act.wait_ge(s_mv, q * (G * norms) + G)
                nc.scalar.activation(sd[:, 0, :], mv[:, 0, :, 1], ACT.Sqrt, bias=eps).then_inc(s_sd, 1)
                if not first:
                    return
                for r in range(G):
                    act.wait_ge(s_x2, q * G + (2 * G + r + 1))
                    nc.scalar.activation(flat(X[:, bass.ds(q * G + r, 1), :]), x2[:, h, r, :], ACT.Copy).then_inc(s_xc, 1)
                act.wait_ge(s_mv, q * (G * norms) + 2 * G)
                nc.scalar.activation(sd[:, 1, :], mv[:, 1, :, 1], ACT.Sqrt, bias=eps).then_inc(s_sd, 1)
                act.wait_ge(s_st[h], j * (16 * G) + 16 * G)
                act.wait_ge(s_tr, q * G + G)
                act.wait_ge(s_nb, q + 1)
                for r in range(G):
                    nc.scalar.activation(xr[:, h, r, :], x2[:, h, r, :], ACT.Identity, scale=rs[:, 1, r:r + 1],
                                         bias=nb[:, r:r + 1]).then_inc(s_xr, 1)
                for r in range(G):
                    act.wait_ge(s_tr, q * G + (2 * G + r + 1))
                    act.wait_ge(s_rt, q * G + (r + 1))
                    for k in range(KD):
                        nc.scalar.activation(xrT[:, r, k, :], t_ps[r][:, k, :], ACT.Identity, scale=scb[:, k:k + 1],
                                             bias=scb[:, KD + k:KD + k + 1]).then_inc(s_xT, 1)
            run_groups(act, step)

        @block.vector
        def _(dve):
            V = nc.vector
            dve.sem_inc(s_x2, 2 * G)

            def stats(q, m, src):
                for r in range(G):
                    if m == 1:
                        dve.wait_ge(s_x2, q * G + (2 * G + r + 1))
                    else:
                        dve.wait_ge(s_a, q * G + (2 * G + r + 1))
                    V.bn_stats(st[:, m, r, :], src[:, r, :]).then_inc(s_bs, 1)
                for r in range(G):
                    after(dve, s_bs, q * (G * norms) + (G * m + r + 1), s_pass_dve)
                    V.bn_aggr(mv[:, m, r, :], st[:, m, r, :]).then_inc(s_mv, 1)
                dve.wait_ge(s_sd, q * norms + (m + 1))
                V.reciprocal(rs[:, m, :], sd[:, m, :]).then_inc(s_rs, 1)
                dve.wait_ge(s_rs, q * norms + (m + 1))

            def step(q, j, h):
                for r in range(G):
                    T = bass.ds(q * G + r, 1)
                    dve.wait_ge(s_gy[h][r // 2], (j + 1) * 64)
                    dve.wait_ge(s_x2, q * G + 2 * G)
                    V.scalar_tensor_tensor(out=acc[:, r, :], in0=yg[:, h, r, 0, :], scalar=flat(GATE[:, T, 0:1]),
                                           in1=flat(X[:, T, :]), op0=ALU.mult, op1=ALU.add).then_inc(s_acc, 1)
                for r in range(G):
                    T = bass.ds(q * G + r, 1)
                    dve.wait_ge(s_acc, q * G + r + 1)
                    V.scalar_tensor_tensor(out=acc[:, r, :], in0=yg[:, h, r, 1, :], scalar=flat(GATE[:, T, 1:2]),
                                           in1=acc[:, r, :], op0=ALU.mult, op1=ALU.add).then_inc(s_a, 1)
                stats(q, 0, acc)
                if first:
                    dve.wait_ge(s_xc, q * G + G)
                    dve.wait_ge(s_xr, q * G + 2 * G)
                else:
                    dve.wait_ge(s_st[h], j * (16 * G) + 16 * G)
                for r in range(G):
                    V.tensor_scalar(x2[:, h, r, :], acc[:, r, :], mv[:, 0, r, 0:1], rs[:, 0, r:r + 1], ALU.subtract,
                                    ALU.mult).then_inc(s_x2, 1)
                if first:
                    stats(q, 1, x2[:, h, :, :])
                    V.scalar_tensor_tensor(out=nb[:, :], in0=mv[:, 1, :, 0], scalar=-1.0, in1=rs[:, 1, :],
                                           op0=ALU.mult, op1=ALU.mult).then_inc(s_nb, 1)
            run_groups(dve, step)

        @block.tensor
        def _(pe):
            if not first:
                return
            pe.wait_ge(s_ld, 16 * 3)
            pe.sem_inc(s_tr, 2 * G)
            pe.sem_inc(s_rt, G)

            def step(q, j, h):
                for r in range(G):
                    pe.wait_ge(s_xr, q * G + (2 * G + r + 1))
                    pe.wait_ge(s_xT, q * (2 * G) + 2 * (r + 1))
                    for k in range(KD):
                        ins = nc.tensor.transpose(t_ps[r][:, k, :], xr[:, h, r, k * P:(k + 1) * P], ident)
                    ins.then_inc(s_tr, 1)
                for r in range(G):
                    pe.wait_ge(s_xT, q * (2 * G) + 2 * (G + r + 1))
                    for k in range(KD):
                        ins = nc.tensor.matmul(bank[0][:, bass.ds((q * G + r) * E + D, E)], xrT[:, r, k, :], wr[:, k, :],
                                               start=(k == 0), stop=(k == KD - 1))
                    ins.then_inc(s_rt, 1)
            run_groups(pe, step)


def build(nc, io):
    with ExitStack() as ctx:
        def sb(name, shape, dt=F32):
            return ctx.enter_context(nc.sbuf_tensor(name, shape, dt))

        bank = [ctx.enter_context(nc.psum_tensor(f"bank{i}", [P, 512], F32)) for i in range(8)]
        passed = {e: ctx.enter_context(nc.semaphore(f"passed_{e}")) for e in ("pool", "act", "pe", "dve")}
        X = sb("X", [P, NT, D])
        LG = sb("LG", [P, NT, E])
        GATE = sb("GATE", [P, NT, 2])
        GI = sb("GI", [P, NT, 2], I32)
        IDX = sb("IDX", [P, SC], I32)
        cst = sb("cst", [P, C_N])
        rbias = sb("rbias", [P, E])
        wraw = sb("wraw", [P, 4 * 1536])
        ws0 = sb("ws0", [P, 2, 6144], F32R)

        attention_phase(nc, bank, passed, io, X, cst, rbias, wraw)
        routing_phase(nc, bank, io, "R1", True, LG, GATE, GI, IDX, cst, rbias, wraw, ws0, 1024)
        with nc.sbuf_tensor("ws1a", [P, 2, 4096], F32R) as ws1:
            expert_phase(nc, bank, passed, io, "E1", False, IDX, io["xn1"], io["y1"], io["w_moe"], io["sc_moe"], cst, wraw, (ws0, ws1))
        combine_phase(nc, bank, passed, io, "C1", True, X, GATE, GI, io["y1"], cst, wraw)
        routing_phase(nc, bank, io, "R2", False, LG, GATE, GI, IDX, cst, rbias, wraw, ws0, 1536)
        with nc.sbuf_tensor("ws1b", [P, 2, 6144], F32R) as ws1:
            expert_phase(nc, bank, passed, io, "E2", True, IDX, io["xn2"], io["y2"], io["w_ffn"], io["sc_ffn"], cst, wraw, (ws0, ws1))
        combine_phase(nc, bank, passed, io, "C2", False, X, GATE, GI, io["y2"], cst, wraw)


def kernel(**inputs):
    import concourse.bacc as bacc
    from concourse.bass_utils import run_bass_kernel_spmd

    g = {k: np.asarray(v) for k, v in inputs.items()}

    def column(v):
        return v.reshape(KD, P).T

    w1 = g["L0_attn_W1"].reshape(E, KD, P, HID).transpose(0, 2, 1, 3).reshape(E, P, -1)
    w2 = g["L0_attn_W2"].reshape(E, NF, P, D).transpose(0, 2, 1, 3).reshape(E, P, -1)
    w12 = g["L0_ffn_w12"].transpose(0, 2, 1).reshape(E, KD, P, 2 * HID).transpose(0, 2, 1, 3).reshape(E, P, -1)
    w3 = g["L0_ffn_w3"].transpose(0, 2, 1).reshape(E, NF, P, D).transpose(0, 2, 1, 3).reshape(E, P, -1)
    consts, rope = shape_constants()
    arrays = {
        "x": g["L0_attn_x"],
        "consts": consts,
        "rope": rope,
        "wqkvg": np.concatenate([g[f"L0_attn_W{c}"] for c in "qkvg"], axis=1),
        "bqkvg": np.concatenate([g[f"L0_attn_b{c}"] for c in "qkvg"]),
        "wo": g["L0_attn_Wo"],
        "bo": g["L0_attn_bo"],
        "sc1": column(g["L0_attn_norm1_scale"]),
        "sc2": column(g["L0_attn_norm2_scale"]),
        "wr1": g["L0_attn_router_W"],
        "rb": g["L0_attn_router_b"],
        "w_moe": np.concatenate([w1, w2], axis=2),
        "b1": g["L0_attn_b1"].reshape(E * NF, P).T,
        "b2": g["L0_attn_b2"].reshape(-1),
        "sc_moe": np.concatenate([column(g["L0_attn_norm2_scale"]), np.zeros((P, KD), np.float32)], axis=1),
        "sc_ffn": np.concatenate([column(g["L0_ffn_ln_gamma"]), column(g["L0_ffn_ln_beta"])], axis=1),
        "wr2": g["L0_ffn_router_w"].T,
        "w_ffn": np.concatenate([w12, w3], axis=2),
    }
    arrays = {f"in_{k}": np.ascontiguousarray(v) for k, v in arrays.items()}
    nc = bacc.Bacc("TRN2", target_bir_lowering=False, num_devices=1)
    io = {k[3:]: nc.dram_tensor(k, v.shape, mybir.dt.from_np(v.dtype), kind="ExternalInput").ap() for k, v in arrays.items()}
    io["out"] = nc.dram_tensor("out_0", (BATCH, SEQ, D), F32, kind="ExternalOutput").ap()
    for name, rows in (("xn1", N), ("xn2", N), ("y1", SLOTS), ("y2", SLOTS)):
        io[name] = nc.dram_tensor(name, (rows, D), F32, kind="Internal").ap()
    build(nc, io)
    r = run_bass_kernel_spmd(nc, [arrays], core_ids=[0])
    return r.results[0]["out_0"]
```
